# Optimizing a Trainium2 kernel written in Bass

```python
import numpy as np
import jax
import jax.numpy as jnp

def _softmax(x, axis=-1):
    return jax.nn.softmax(x, axis=axis)

def _gelu(x):
    return jax.nn.gelu(x, approximate=True)

def _silu(x):
    return jax.nn.silu(x)

def _sigmoid(x):
    return jax.nn.sigmoid(x)

def _layernorm(x, axis=-1, eps=1e-05):
    m = jnp.mean(x, axis=axis, keepdims=True)
    v = jnp.var(x, axis=axis, keepdims=True)
    return (x - m) / jnp.sqrt(v + eps)

def _scatter_add(tgt, idx, src, axis=0):
    return tgt.at[idx].add(src)

def _segment_sum(src, seg, n):
    return jax.ops.segment_sum(src, seg, n)
kernel_name = 'mk_seq_preln_d2_jaxref_r8_393f93'

def setup_inputs(seed: int=0):
    np.random.seed(seed)
    _w = jnp.asarray

    def _L0_attn_setup():
        import jax, jax.numpy as jnp
        import numpy as np
        D_MODEL = 128
        N_HEADS = 16
        HEAD_DIM = D_MODEL // N_HEADS
        N_EXPERTS = 4
        HIDDEN = 4 * D_MODEL
        B, T = (1, 256)

        def _apply_rope(x, sin, cos):
            x1, x2 = (x[..., ::2], x[..., 1::2])
            r1 = x1 * cos - x2 * sin
            r2 = x1 * sin + x2 * cos
            return jnp.stack((r1, r2), axis=-1).reshape(x.shape)
        key = jax.random.key(seed)
        ks = jax.random.split(key, 16)
        s = 0.02
        d, E, Hd = (D_MODEL, N_EXPERTS, HIDDEN)
        return {'x': jax.random.normal(ks[0], (B, T, d), dtype=jnp.float32), 'w_dw': jax.random.normal(ks[1], (d, 3), dtype=jnp.float32) * s, 'w_pw': jax.random.normal(ks[2], (d, d), dtype=jnp.float32) * s, 'w_qkv': jax.random.normal(ks[3], (3 * d, d), dtype=jnp.float32) * s, 'w_o': jax.random.normal(ks[4], (d, d), dtype=jnp.float32) * s, 'w_gate': jax.random.normal(ks[5], (d, d), dtype=jnp.float32) * s, 'b_gate': jnp.zeros((d,), dtype=jnp.float32), 'ln_g': jnp.ones((d,), dtype=jnp.float32), 'ln_b': jnp.zeros((d,), dtype=jnp.float32), 'w_moe_gate': jax.random.normal(ks[6], (E, d), dtype=jnp.float32) * s, 'w1': jax.random.normal(ks[7], (E, Hd, d), dtype=jnp.float32) * s, 'b1': jnp.zeros((E, Hd), dtype=jnp.float32), 'w2': jax.random.normal(ks[8], (E, d, Hd), dtype=jnp.float32) * s, 'b2': jnp.zeros((E, d), dtype=jnp.float32)}
    _L0_attn_in = _L0_attn_setup()

    def _L0_ffn_setup():
        import jax, jax.numpy as jnp
        import numpy as np
        D = 128
        H = 256
        E = 8
        B, T = (4, 256)
        LN_EPS = 1e-05
        key = jax.random.key(seed)
        k = jax.random.split(key, 6)
        std = 0.02
        return {'x': jax.random.normal(k[0], (B, T, D), dtype=jnp.float32), 'gate_w': jax.random.normal(k[1], (E, D), dtype=jnp.float32) * std, 'expert_w1': jax.random.normal(k[2], (E, D, H), dtype=jnp.float32) * std, 'expert_w2': jax.random.normal(k[3], (E, H, D), dtype=jnp.float32) * std, 'ln_gamma': jnp.ones((D,), dtype=jnp.float32), 'ln_beta': jnp.zeros((D,), dtype=jnp.float32)}
    _L0_ffn_in = _L0_ffn_setup()

    def _L1_attn_setup():
        import jax, jax.numpy as jnp
        import numpy as np
        import math
        DIM_EMB = 128
        DIM_QK = 128
        DIM_V = 128
        NORM_FACT = 1.0 / math.sqrt(DIM_EMB)
        key = jax.random.key(seed)
        k0, k1, k2, k3 = jax.random.split(key, 4)
        x = jax.random.normal(k0, (4, 512, DIM_EMB), dtype=jnp.float32)
        s = 1.0 / math.sqrt(DIM_EMB)
        Wq = jax.random.uniform(k1, (DIM_QK, DIM_EMB), jnp.float32, -s, s)
        Wk = jax.random.uniform(k2, (DIM_QK, DIM_EMB), jnp.float32, -s, s)
        Wv = jax.random.uniform(k3, (DIM_V, DIM_EMB), jnp.float32, -s, s)
        return {'x': x, 'Wq': Wq, 'Wk': Wk, 'Wv': Wv}
    _L1_attn_in = _L1_attn_setup()

    def _L1_ffn_setup():
        import jax, jax.numpy as jnp
        import numpy as np
        B, S, H, F, E = (4, 256, 128, 512, 8)
        key = jax.random.key(seed)
        ks = jax.random.split(key, 8)
        s = 1.0 / np.sqrt(H)
        sf = 1.0 / np.sqrt(F)
        return {'x': jax.random.normal(ks[0], (B, S, H), jnp.float32), 'wr': jax.random.uniform(ks[1], (H, E), jnp.float32, -s, s), 'br': jax.random.uniform(ks[2], (E,), jnp.float32, -s, s), 'w1': jax.random.uniform(ks[3], (E, H, F), jnp.float32, -s, s), 'b1': jax.random.uniform(ks[4], (E, F), jnp.float32, -s, s), 'w2': jax.random.uniform(ks[5], (E, F, H), jnp.float32, -sf, sf), 'b2': jax.random.uniform(ks[6], (E, H), jnp.float32, -sf, sf)}
    _L1_ffn_in = _L1_ffn_setup()
    _d = {'L0_attn_x': _L0_attn_in['x'], 'L0_attn_w_dw': _L0_attn_in['w_dw'], 'L0_attn_w_pw': _L0_attn_in['w_pw'], 'L0_attn_w_qkv': _L0_attn_in['w_qkv'], 'L0_attn_w_o': _L0_attn_in['w_o'], 'L0_attn_w_gate': _L0_attn_in['w_gate'], 'L0_attn_b_gate': _L0_attn_in['b_gate'], 'L0_attn_ln_g': _L0_attn_in['ln_g'], 'L0_attn_ln_b': _L0_attn_in['ln_b'], 'L0_attn_w_moe_gate': _L0_attn_in['w_moe_gate'], 'L0_attn_w1': _L0_attn_in['w1'], 'L0_attn_b1': _L0_attn_in['b1'], 'L0_attn_w2': _L0_attn_in['w2'], 'L0_attn_b2': _L0_attn_in['b2'], 'L0_ffn_gate_w': _L0_ffn_in['gate_w'], 'L0_ffn_expert_w1': _L0_ffn_in['expert_w1'], 'L0_ffn_expert_w2': _L0_ffn_in['expert_w2'], 'L0_ffn_ln_gamma': _L0_ffn_in['ln_gamma'], 'L0_ffn_ln_beta': _L0_ffn_in['ln_beta'], 'L1_attn_Wq': _L1_attn_in['Wq'], 'L1_attn_Wk': _L1_attn_in['Wk'], 'L1_attn_Wv': _L1_attn_in['Wv'], 'L1_ffn_wr': _L1_ffn_in['wr'], 'L1_ffn_br': _L1_ffn_in['br'], 'L1_ffn_w1': _L1_ffn_in['w1'], 'L1_ffn_b1': _L1_ffn_in['b1'], 'L1_ffn_w2': _L1_ffn_in['w2'], 'L1_ffn_b2': _L1_ffn_in['b2']}
    _x0 = _d['L0_attn_x']
    _d['L0_attn_x'] = jax.random.normal(jax.random.fold_in(jax.random.key(seed), 1), (16, 512, 128), dtype=_x0.dtype)
    del _x0
    return _d

def reference(L0_attn_x, L0_attn_w_dw, L0_attn_w_pw, L0_attn_w_qkv, L0_attn_w_o, L0_attn_w_gate, L0_attn_b_gate, L0_attn_ln_g, L0_attn_ln_b, L0_attn_w_moe_gate, L0_attn_w1, L0_attn_b1, L0_attn_w2, L0_attn_b2, L0_ffn_gate_w, L0_ffn_expert_w1, L0_ffn_expert_w2, L0_ffn_ln_gamma, L0_ffn_ln_beta, L1_attn_Wq, L1_attn_Wk, L1_attn_Wv, L1_ffn_wr, L1_ffn_br, L1_ffn_w1, L1_ffn_b1, L1_ffn_w2, L1_ffn_b2):

    def _L0_attn_ref(x, w_dw, w_pw, w_qkv, w_o, w_gate, b_gate, ln_g, ln_b, w_moe_gate, w1, b1, w2, b2):
        import jax, jax.numpy as jnp
        import numpy as np
        D_MODEL = 128
        N_HEADS = 16
        HEAD_DIM = D_MODEL // N_HEADS
        N_EXPERTS = 4
        HIDDEN = 4 * D_MODEL
        B, T = (1, 256)

        def _apply_rope(x, sin, cos):
            x1, x2 = (x[..., ::2], x[..., 1::2])
            r1 = x1 * cos - x2 * sin
            r2 = x1 * sin + x2 * cos
            return jnp.stack((r1, r2), axis=-1).reshape(x.shape)
        Bv, Tv, d = x.shape
        H, Dh = (N_HEADS, HEAD_DIM)
        dt = x.dtype
        xp = jnp.pad(x, ((0, 0), (2, 0), (0, 0)))
        y = xp[:, 0:Tv] * w_dw[:, 0] + xp[:, 1:Tv + 1] * w_dw[:, 1] + xp[:, 2:Tv + 2] * w_dw[:, 2]
        y = jnp.einsum('btd,ed->bte', y, w_pw)
        x = x + y
        qkv = jnp.einsum('btd,ed->bte', x, w_qkv).reshape(Bv, Tv, 3, H, Dh)
        q, k, v = (qkv[:, :, 0], qkv[:, :, 1], qkv[:, :, 2])
        inv_freq = 1.0 / 10000.0 ** (jnp.arange(0, Dh, 2, dtype=dt) / Dh)
        pos = jnp.arange(Tv, dtype=dt)
        theta = pos[:, None] * inv_freq[None, :]
        sin = jnp.sin(theta)[None, :, None, :]
        cos = jnp.cos(theta)[None, :, None, :]
        q = _apply_rope(q, sin, cos)
        k = _apply_rope(k, sin, cos)
        q_phi = jax.nn.elu(q) + 1.0
        k_phi = jax.nn.elu(k) + 1.0
        kv = k_phi[..., :, None] * v[..., None, :]
        kv_prefix = jnp.cumsum(kv, axis=1)
        k_prefix = jnp.cumsum(k_phi, axis=1)
        num = jnp.einsum('bthd,bthdm->bthm', q_phi, kv_prefix)
        denom = jnp.sum(q_phi * k_prefix, axis=-1, keepdims=True)
        attn = num / (denom + 1e-06)
        attn = attn.reshape(Bv, Tv, d)
        attn = jnp.einsum('btd,ed->bte', attn, w_o)
        delta = x - jnp.concatenate([x[:, :1], x[:, :-1]], axis=1)
        gate = jax.nn.sigmoid(jnp.einsum('btd,ed->bte', delta, w_gate) + b_gate)
        x = x + gate * attn
        mu = jnp.mean(x, axis=-1, keepdims=True)
        var = jnp.mean((x - mu) ** 2, axis=-1, keepdims=True)
        h = (x - mu) / jnp.sqrt(var + 1e-05) * ln_g + ln_b
        gw = jax.nn.softmax(jnp.einsum('btd,ed->bte', h, w_moe_gate), axis=-1)
        hid = jax.nn.silu(jnp.einsum('btd,efd->btef', h, w1) + b1)
        eo = jnp.einsum('btef,edf->bted', hid, w2) + b2
        ffn = jnp.einsum('bte,bted->btd', gw, eo)
        return x + ffn

    def _L0_ffn_ref(x, gate_w, expert_w1, expert_w2, ln_gamma, ln_beta):
        import jax, jax.numpy as jnp
        import numpy as np
        D = 128
        H = 256
        E = 8
        B, T = (4, 256)
        LN_EPS = 1e-05
        Bb, Tt, Dd = x.shape
        x_flat = x.reshape(Bb * Tt, Dd)
        gate_logits = x_flat @ gate_w.T
        gate_probs = jax.nn.softmax(gate_logits, axis=-1)
        top_val = jnp.max(gate_probs, axis=-1)
        top_idx = jnp.argmax(gate_probs, axis=-1)
        top_val = top_val / (top_val + 1e-08)
        onehot = jax.nn.one_hot(top_idx, expert_w1.shape[0], dtype=x.dtype)
        xe = jnp.einsum('ne,nd->end', onehot, x_flat)
        he = jax.nn.gelu(jnp.einsum('end,edh->enh', xe, expert_w1), approximate=False)
        ye = jnp.einsum('enh,ehd->end', he, expert_w2)
        out_flat = jnp.einsum('end,ne->nd', ye, onehot) * top_val[:, None]
        out = out_flat.reshape(Bb, Tt, Dd)
        mu = jnp.mean(out, axis=-1, keepdims=True)
        var = jnp.mean((out - mu) ** 2, axis=-1, keepdims=True)
        out = (out - mu) * jax.lax.rsqrt(var + LN_EPS) * ln_gamma + ln_beta
        return out

    def _L1_attn_ref(x, Wq, Wk, Wv):
        import jax, jax.numpy as jnp
        import numpy as np
        import math
        DIM_EMB = 128
        DIM_QK = 128
        DIM_V = 128
        NORM_FACT = 1.0 / math.sqrt(DIM_EMB)
        q = jnp.einsum('bne,de->bnd', x, Wq)
        k = jnp.einsum('bne,de->bnd', x, Wk)
        v = jnp.einsum('bne,de->bnd', x, Wv)
        logits = jnp.einsum('bnd,bmd->bnm', q, k)
        score = jax.nn.softmax(logits, axis=-1) * NORM_FACT
        att = jnp.einsum('bnm,bmv->bnv', score, v)
        return att

    def _L1_ffn_ref(x, wr, br, w1, b1, w2, b2):
        import jax, jax.numpy as jnp
        import numpy as np
        B, S, H, F, E = (4, 256, 128, 512, 8)
        scores = jnp.einsum('bsh,he->bse', x, wr) + br
        expert_id = jnp.argmax(scores, axis=-1)
        h = jnp.einsum('bsh,ehf->ebsf', x, w1) + b1[:, None, None, :]
        h = jax.nn.gelu(h, approximate=False)
        y = jnp.einsum('ebsf,efh->ebsh', h, w2) + b2[:, None, None, :]
        one_hot = jax.nn.one_hot(expert_id, E, dtype=x.dtype)
        out = jnp.einsum('ebsh,bse->bsh', y, one_hot)
        return out
    x = L0_attn_x
    x = x + _L0_attn_ref(_layernorm(x, axis=-1), L0_attn_w_dw, L0_attn_w_pw, L0_attn_w_qkv, L0_attn_w_o, L0_attn_w_gate, L0_attn_b_gate, L0_attn_ln_g, L0_attn_ln_b, L0_attn_w_moe_gate, L0_attn_w1, L0_attn_b1, L0_attn_w2, L0_attn_b2)
    x = x + _L0_ffn_ref(_layernorm(x, axis=-1), L0_ffn_gate_w, L0_ffn_expert_w1, L0_ffn_expert_w2, L0_ffn_ln_gamma, L0_ffn_ln_beta)
    x = x + _L1_attn_ref(_layernorm(x, axis=-1), L1_attn_Wq, L1_attn_Wk, L1_attn_Wv)
    x = x + _L1_ffn_ref(_layernorm(x, axis=-1), L1_ffn_wr, L1_ffn_br, L1_ffn_w1, L1_ffn_b1, L1_ffn_w2, L1_ffn_b2)
    return x

_drawn_inputs = setup_inputs


def setup_inputs(seed=0):
    import zlib

    import numpy as np

    out = dict(_drawn_inputs(seed))
    spreads = {'L0_attn_b_gate': (0.0, 0.8),
     'L0_attn_ln_g': (1.0, 0.2),
     'L0_attn_ln_b': (0.0, 0.285),
     'L0_attn_b1': (0.0, 0.1),
     'L0_attn_b2': (0.0, 0.1),
     'L0_ffn_ln_gamma': (1.0, 0.2),
     'L0_ffn_ln_beta': (0.0, 0.1)}
    factors = {'L0_attn_w_qkv': 3.123,
     'L0_attn_w_o': 2.811,
     'L0_attn_w_gate': 7.619,
     'L1_attn_Wq': 3.565,
     'L1_attn_Wk': 3.497,
     'L1_attn_Wv': 3.458,
     'L1_ffn_b1': 6.894,
     'L1_ffn_b2': 4.885}
    for name, (base, spread) in spreads.items():
        noise = np.random.default_rng([zlib.crc32(name.encode()), seed]).standard_normal(out[name].shape)
        drawn = base * np.exp(spread * noise) if base else spread * noise
        out[name] = jnp.asarray(drawn.astype(out[name].dtype))
    for name, factor in factors.items():
        out[name] = (out[name] * factor).astype(out[name].dtype)
    return out
```

```python
from contextlib import ExitStack

import numpy as np

import concourse.bass as bass
from concourse import mybir

F32 = mybir.dt.float32
F32R = mybir.dt.float32r
BF16 = mybir.dt.bfloat16
I32 = mybir.dt.int32
U32 = mybir.dt.uint32
ALU = mybir.AluOpType
ACT = mybir.ActivationFunctionType
AX = mybir.AxisListType

P = 128
BATCHES = 16
SEQ = 512
CT = SEQ // P
TOKENS = BATCHES * SEQ
TILES = TOKENS // P
HEADS, HD = 16, 8
MOE = 4
MOE_CHUNKS = 512 // P
EXPERTS = 8
LN_EPS = 1e-5

ROW = 260
COL_X, COL_TV, COL_ID = 128, 256, 257
SLOT = 256
REGION = TOKENS + SLOT
NSLOT = 40
SPARE = (NSLOT - TOKENS // SLOT) * SLOT
ROWS = EXPERTS * REGION + SPARE
NO_TOKEN = 9000.0

WCOLS = {}


def _columns():
    at = 0
    for name, n in [("pw", P), ("q", P), ("qs", P), ("k", P), ("ks", P), ("v", P), ("o", P), ("gate", P),
                    ("moe_gate", MOE), ("dw", 3), ("b_gate", 1), ("ln_g", 1), ("ln_b", 1),
                    ("b1", MOE * MOE_CHUNKS), ("b2", MOE), ("router0", EXPERTS),
                    ("q1", P), ("k1", P), ("v1", P), ("router1", EXPERTS), ("br1", EXPERTS),
                    ("gamma", P), ("beta", P)]:
        WCOLS[name] = (at, at + n)
        at += n
    return at


NW = _columns()
CCOLS = {}


def _const_columns():
    at = 0
    for name, n in [("ident", P), ("cos", SEQ), ("sin", SEQ), ("tri", P), ("block", P), ("group", 4),
                    ("heads", HEADS), ("sel", MOE * P), ("before", P), ("ids", TILES), ("iota", EXPERTS),
                    ("region", EXPERTS), ("slots", NSLOT)]:
        CCOLS[name] = (at, at + n)
        at += n
    return at


NCONST = _const_columns()


def program(nc, x, wsmall, consts, w1t, w2t, wr0, wr1, br2, out):
    rows_dram = [nc.dram_tensor(f"rows{i}", (ROWS, ROW), F32, kind="Internal").ap() for i in range(2)]
    mid_dram = nc.dram_tensor("mid", (TOKENS, P), F32, kind="Internal").ap()

    with ExitStack() as ctx:
        def sb(name, shape, dt=F32):
            return ctx.enter_context(nc.sbuf_tensor(name, shape, dt))

        X = sb("X", [P, TILES, P])
        W = sb("W", [P, NW])
        C = sb("C", [P, NCONST])
        before = sb("before", [P, P], BF16)
        ones = sb("ones", [P, P], BF16)
        minus_half = sb("minus_half", [P, CT])
        eps = sb("eps", [P, CT])
        scratch = sb("scratch", [P, 2])
        slot_row = sb("slot_row", [P, NSLOT], I32)
        slot_expert = sb("slot_expert", [P, NSLOT], I32)
        PS = ctx.enter_context(nc.psum_tensor("PS", [P, 8, 512], F32))

        def w(name):
            a, b = WCOLS[name]
            return W[:, a:b]

        def c(name):
            a, b = CCOLS[name]
            return C[:, a:b]

        shared = dict(nc=nc, X=X, w=w, c=c, PS=PS, before=before, ones=ones,
                      minus_half=minus_half, eps=eps, scratch=scratch)

        with ExitStack() as front:
            HH = front.enter_context(nc.sbuf_tensor("HH", [P, TOKENS], F32R))
            HL = front.enter_context(nc.sbuf_tensor("HL", [P, TOKENS], F32R))
            LG = front.enter_context(nc.sbuf_tensor("LG", [P, TILES * MOE], F32))
            setup(wsmall=wsmall, consts=consts, W=W, C=C, **shared)
            attention_front(x=x, HH=HH, HL=HL, LG=LG, **shared)
            clear_semaphores(nc)
            mixture(HH=HH, HL=HL, LG=LG, w1t=w1t, w2t=w2t, **shared)
            clear_semaphores(nc)
        slots = dict(slot_row=slot_row, slot_expert=slot_expert)
        route(0, rows=rows_dram[0], **slots, **shared)
        clear_semaphores(nc)
        routed(0, rows=rows_dram[0], weights=wr0, b2=None, dest=mid_dram, **slots, **shared)
        clear_semaphores(nc)
        softmax_attention(mid=mid_dram, **shared)
        clear_semaphores(nc)
        route(1, rows=rows_dram[1], **slots, **shared)
        clear_semaphores(nc)
        routed(1, rows=rows_dram[1], weights=wr1, b2=br2, dest=out, **slots, **shared)


def clear_semaphores(nc):
    nc.all_engine_barrier()
    used = sorted(nc.released_uncleared_semaphores)
    nc.gpsimd.sem_clear(range(used[0], used[-1] + 1))
    nc.all_engine_barrier()


def after_previous(eng, sem, b, per=1):
    if not (isinstance(b, int) and b == 0):
        eng.wait_ge(sem, b * per)


def wait_apart(dve, nc, sem, value, scratch):
    dve.wait_ge(sem, value)
    nc.vector.memset(scratch[:, 0:1], 0.0)


def setup(nc, wsmall, consts, W, C, X, w, c, PS, before, ones, minus_half, eps, scratch):
    with ExitStack() as ctx:
        sem = lambda n: ctx.enter_context(nc.semaphore(n))
        weights_in, consts_in, made = sem("weights_in"), sem("consts_in"), sem("made")
        block = ctx.enter_context(nc.Block())

        @block.sync
        def _(sp):
            sp.dma_start(W[:, :], wsmall).then_inc(weights_in, 16)
            sp.dma_start(C[:, :], consts).then_inc(consts_in, 16)
            sp.wait_ge(weights_in, 16)
            sp.wait_ge(consts_in, 16)

        @block.vector
        def _(dve):
            nc.vector.memset(ones[:, :], 1.0)
            nc.vector.memset(minus_half[:, :], -0.5)
            nc.vector.memset(eps[:, :], LN_EPS)
            nc.vector.memset(scratch[:, 1:2], 0.0)
            dve.wait_ge(consts_in, 16)
            nc.vector.tensor_copy(before[:, :], c("before"))
            dve.wait_ge(weights_in, 16)
            nc.vector.tensor_scalar(w("b_gate"), w("b_gate"), 0.5, None, ALU.mult)
            nc.vector.tensor_scalar(w("o"), w("o"), 0.5, None, ALU.mult).then_inc(made, 1)


def attention_front(nc, X, w, c, PS, before, ones, minus_half, eps, scratch, HH, HL, LG, x):
    with ExitStack() as ctx:
        def sb(name, shape, dt=F32):
            return ctx.enter_context(nc.sbuf_tensor(name, shape, dt))

        def sem(name):
            return ctx.enter_context(nc.semaphore("a_" + name))

        st = sb("st", [P, CT, 6])
        mv = sb("mv", [P, CT, 2])
        ve = sb("ve", [P, CT])
        rstd = sb("rstd", [P, CT])
        xn = sb("xn", [P, CT, P])
        xnT = sb("xnT", [P, SEQ + 2])
        y = sb("y", [P, 3, SEQ])
        x1T = sb("x1T", [P, 2, SEQ])
        delta = sb("delta", [P, 2, SEQ])
        rot = sb("rot", [P, 3, SEQ])
        ex = sb("ex", [P, SEQ])
        qphi = sb("qphi", [P, 2, SEQ])
        kphi = sb("kphi", [P, 2, SEQ])
        vt = sb("vt", [P, 2, CT, P])
        vm = sb("vm", [P, 2, CT, 4, P])
        ktok = sb("ktok", [P, CT - 1, P])
        km = sb("km", [P, 4, SEQ])
        kp = sb("kp", [P, SEQ])
        prod = sb("prod", [P, SEQ])
        am = sb("am", [P, 3, 4 * P])
        state = sb("state", [P, CT - 1, P])
        den = sb("den", [P, 2, CT * HEADS])
        spread = sb("spread", [P, SEQ])
        rdT = sb("rdT", [P, SEQ])
        attn = sb("attn", [P, SEQ])
        th = sb("th", [P, SEQ])
        gated = sb("gated", [P, SEQ])
        x2T = sb("x2T", [P, SEQ])
        st2 = sb("st2", [P, CT, 6])
        mv2 = sb("mv2", [P, CT, 2])
        ve2 = sb("ve2", [P, CT])
        rstd2 = sb("rstd2", [P, CT])
        z = sb("z", [P, CT, P])
        h = sb("h", [P, SEQ])
        minus_one = sb("minus_one", [P, 1])

        x_in = sem("x_in"); zeroed = sem("zeroed"); act_const = sem("act_const")
        ln1 = sem("ln1"); ln1_stats = sem("ln1_stats"); ve1_done = sem("ve1_done"); rstd1_ready = sem("rstd1_ready")
        xn_ready = sem("xn_ready"); xnT_psum = sem("xnT_psum"); xnT_ready = sem("xnT_ready")
        conv = sem("conv"); pw_psum = sem("pw_psum"); x1_ready = sem("x1_ready")
        delta_ready = sem("delta_ready")
        qk_psum = sem("qk_psum"); qk_read = sem("qk_read"); rot_step = sem("rot_step"); exp_ready = sem("exp_ready")
        phi_ready = sem("phi_ready"); v_psum = sem("v_psum"); v_ready = sem("v_ready")
        kT_psum = sem("kT_psum"); ktok_ready = sem("ktok_ready"); km_ready = sem("km_ready")
        kp_ready = sem("kp_ready"); prod_ready = sem("prod_ready")
        scores_psum = sem("scores_psum"); am_ready = sem("am_ready"); am_used = sem("am_used")
        state_psum = sem("state_psum"); state_ready = sem("state_ready")
        den_psum = sem("den_psum"); den_step = sem("den_step"); spread_ready = sem("spread_ready"); rdT_psum = sem("rdT_psum"); rdT_ready = sem("rdT_ready")
        num_psum = sem("num_psum"); attn_ready = sem("attn_ready"); gate_psum = sem("gate_psum")
        wo_psum = sem("wo_psum"); th_ready = sem("th_ready"); x2_step = sem("x2_step")
        x2_psum = sem("x2_psum"); ln2 = sem("ln2"); ln2_stats = sem("ln2_stats"); ve2_done = sem("ve2_done")
        rstd2_ready = sem("rstd2_ready"); z_ready = sem("z_ready"); zT_psum = sem("zT_psum"); h_ready = sem("h_ready")
        hh_ready = sem("hh_ready"); lg_psum = sem("lg_psum"); lg_ready = sem("lg_ready")

        block = ctx.enter_context(nc.Block())
        ident = c("ident")

        def diagonal(t, u, tile):
            base = t[:, u, tile, 0, 0:1]
            ap = [list(base.ap[0]), [P + HD, 4], [4 * HD, 4], [1, HD]]
            return bass.AP(tensor=base.tensor, offset=base.offset, ap=ap)

        def tokens(t, b):
            return t[:, bass.ds(b * CT, CT), :]

        def both_stages(f, a):
            for step in f(0, 0):
                step()
            a(0, 0, f(1, 1))
            eng = a.engine
            with eng.Fori(0, (BATCHES - 2) // 2) as i:
                for u in range(2):
                    b = i * 2 + (1 + u)
                    a(b, 1 - u, f(b + 1, u))
            a(BATCHES - 1, (BATCHES - 1) % 2, [])

        @block.sync
        def _(sp):
            for b in range(BATCHES):
                if b:
                    sp.wait_ge(x_in, 16 * b)
                sp.dma_start(X[:, b * CT:(b + 1) * CT, :], x[b].rearrange("(c p) d -> p c d", p=P)).then_inc(x_in, 16)
            sp.wait_ge(x_in, 16 * BATCHES)

        @block.gpsimd
        def _(pool):
            nc.gpsimd.memset(minus_one[:, :], -1.0).then_inc(act_const, 1)
            nc.gpsimd.memset(xnT[:, 0:2], 0.0)
            nc.gpsimd.memset(delta[:, :, 0:1], 0.0)
            nc.gpsimd.memset(vm[:, :, :, :, :], 0.0).then_inc(zeroed, 1)

            def f(b, u):
                def rstd_step():
                    pool.wait_ge(ln1_stats, b + 1)
                    nc.gpsimd.tensor_tensor(ve[:, :], mv[:, :, 1], eps[:, 0:CT], ALU.add).then_inc(ve1_done, 1)
                    pool.wait_ge(ve1_done, b + 1)
                    nc.gpsimd.tensor_tensor(rstd[:, :], ve[:, :], minus_half[:, :], ALU.pow).then_inc(rstd1_ready, 1)

                def delta_step():
                    pool.wait_ge(x1_ready, b + 1)
                    nc.gpsimd.tensor_tensor(delta[:, u, 1:], x1T[:, u, 1:], x1T[:, u, 0:SEQ - 1],
                                            ALU.subtract).then_inc(delta_ready, 1)
                return [rstd_step, delta_step]

            def a(b, u, nxt):
                pool.wait_ge(kp_ready, b + 1)
                nc.gpsimd.tensor_tensor(prod[:, :], qphi[:, u, :], kp[:, :], ALU.mult).then_inc(prod_ready, 1)
                for step in nxt:
                    step()
                pool.wait_ge(ln2_stats, b + 1)
                nc.gpsimd.tensor_tensor(ve2[:, :], mv2[:, :, 1], eps[:, 0:CT], ALU.add).then_inc(ve2_done, 1)
                pool.wait_ge(ve2_done, b + 1)
                nc.gpsimd.tensor_tensor(rstd2[:, :], ve2[:, :], minus_half[:, :], ALU.pow).then_inc(rstd2_ready, 1)
            a.engine = pool
            both_stages(f, a)

        @block.tensor
        def _(pe):
            def f(b, u):
                def transpose_xn():
                    pe.wait_ge(xn_ready, b + 1)
                    after_previous(pe, v_ready, b)
                    for t in range(CT):
                        mm = nc.tensor.transpose(PS[:, 0, t * P:(t + 1) * P], xn[:, t, :], ident)
                    mm.then_inc(xnT_psum, 1)

                def pointwise():
                    pe.wait_ge(conv, 3 * b + 3)
                    nc.tensor.matmul(PS[:, 0, :], w("pw"), y[:, 2, :], start=True, stop=True).then_inc(pw_psum, 1)

                def project(name, n):
                    pe.wait_ge(x1_ready, b + 1)
                    if n:
                        pe.wait_ge(qk_read, 2 * b + 1)
                    else:
                        after_previous(pe, qk_read, b, 2)
                    nc.tensor.matmul(PS[:, 1, :], w(name), x1T[:, u, :], start=True, stop=True)
                    nc.tensor.matmul(PS[:, 2, :], w(name + "s"), x1T[:, u, :],
                                     start=True, stop=True).then_inc(qk_psum, 1)

                def values():
                    for t in range(CT):
                        mm = nc.tensor.matmul(PS[:, 0, t * P:(t + 1) * P], x1T[:, u, t * P:(t + 1) * P],
                                              w("v"), start=True, stop=True)
                    mm.then_inc(v_psum, 1)
                return [transpose_xn, pointwise, lambda: project("q", 0), values, lambda: project("k", 1)]

            def a(b, u, nxt):
                nxt = list(nxt)

                def turn():
                    if nxt:
                        nxt.pop(0)()

                pe.wait_ge(phi_ready, 2 * b + 2)
                for t in range(CT - 1):
                    mm = nc.tensor.transpose(PS[:, 7, t * P:(t + 1) * P], kphi[:, u, t * P:(t + 1) * P], ident)
                mm.then_inc(kT_psum, 1)
                pe.wait_ge(v_ready, b + 1)
                pe.wait_ge(km_ready, b + 1)

                def scores(n):
                    t, g = divmod(n, 4)
                    if n >= 2:
                        pe.wait_ge(am_ready, 16 * b + n - 1)
                    else:
                        after_previous(pe, am_ready, b, 16)
                    for j in range(4):
                        mm = nc.tensor.matmul(PS[:, 3 + n % 2, j * P:(j + 1) * P],
                                              km[32 * g:32 * g + 32, j, t * P:(t + 1) * P],
                                              qphi[32 * g:32 * g + 32, u, t * P:(t + 1) * P], start=True, stop=True)
                    mm.then_inc(scores_psum, 1)

                def weigh(n):
                    t, g = divmod(n, 4)
                    if g == 0 and t:
                        pe.wait_ge(state_ready, 3 * b + t)
                        nc.tensor.matmul(PS[:, 5, t * P:(t + 1) * P], state[:, t - 1, :],
                                         qphi[:, u, t * P:(t + 1) * P], start=True, stop=False, skip_group_check=True)
                    pe.wait_ge(am_ready, 16 * b + n + 1)
                    for j in range(4):
                        mm = nc.tensor.matmul(PS[32 * g:32 * g + 32, 5, t * P:(t + 1) * P],
                                              vm[:, u, t, j, 32 * g:32 * g + 32],
                                              am[:, n % 3, j * P:(j + 1) * P],
                                              start=(t == 0 and j == 0), stop=(j == 3), skip_group_check=True)
                    mm.then_inc(am_used, 1)

                for n in range(16):
                    scores(n)
                    if n == 1:
                        pe.wait_ge(ktok_ready, b + 1)
                        after_previous(pe, lg_ready, b)
                    if n in (1, 5, 9):
                        t = n // 4
                        if t:
                            pe.wait_ge(state_ready, 3 * b + t)
                        nc.tensor.matmul(PS[:, 6, 0:P], ktok[:, t, :], vt[:, u, t, :], start=(t == 0), stop=True,
                                         skip_group_check=True).then_inc(state_psum, 1)
                    if n >= 1:
                        weigh(n - 1)
                    if n == 10:
                        pe.wait_ge(prod_ready, b + 1)
                        for t in range(CT):
                            mm = nc.tensor.matmul(PS[:, 7, t * HEADS:(t + 1) * HEADS], prod[:, t * P:(t + 1) * P],
                                                  c("heads"), start=True, stop=True)
                        mm.then_inc(den_psum, 1)
                    if n == 13:
                        pe.wait_ge(spread_ready, b + 1)
                        for t in range(CT):
                            mm = nc.tensor.transpose(PS[:, 7, t * P:(t + 1) * P], spread[:, t * P:(t + 1) * P], ident)
                        mm.then_inc(rdT_psum, 1)
                    if n == 14:
                        pe.wait_ge(state_ready, 3 * b + 3)
                        pe.wait_ge(delta_ready, b + 1)
                        nc.tensor.matmul(PS[:, 6, :], w("gate"), delta[:, u, :], start=True, stop=True).then_inc(gate_psum, 1)
                    if n in (4, 6, 8, 11, 12):
                        turn()
                weigh(15)
                pe.wait_ge(attn_ready, b + 1)
                pe.wait_ge(rdT_ready, b + 1)
                nc.tensor.matmul(PS[:, 7, :], w("o"), attn[:, :], start=True, stop=True).then_inc(wo_psum, 1)
                pe.wait_ge(x2_step, 2 * b + 2)
                for t in range(CT):
                    mm = nc.tensor.transpose(PS[:, 7, t * P:(t + 1) * P], x2T[:, t * P:(t + 1) * P], ident)
                mm.then_inc(x2_psum, 1)
                pe.wait_ge(z_ready, b + 1)
                pe.wait_ge(th_ready, b + 1)
                for t in range(CT):
                    mm = nc.tensor.transpose(PS[:, 6, t * P:(t + 1) * P], z[:, t, :], ident)
                mm.then_inc(zT_psum, 1)
                pe.wait_ge(h_ready, b + 1)
                for t in range(CT):
                    mm = nc.tensor.matmul(PS[:, 6, t * MOE:(t + 1) * MOE], h[:, t * P:(t + 1) * P], w("moe_gate"),
                                          start=True, stop=True)
                mm.then_inc(lg_psum, 1)
            a.engine = pe
            both_stages(f, a)

        @block.scalar
        def _(act):
            nc.scalar.preload_act_table(ACT.Exp)
            act.wait_ge(act_const, 1)
            act.wait_ge(zeroed, 1)

            def f(b, u):
                def copy_xnT():
                    act.wait_ge(xnT_psum, b + 1)
                    after_previous(act, x1_ready, b)
                    nc.scalar.activation(xnT[:, 2:], PS[:, 0, :], ACT.Copy).then_inc(xnT_ready, 1)
                    act.wait_ge(xnT_ready, b + 1)
                    nc.scalar.activation(y[:, 0, :], xnT[:, 0:SEQ], ACT.Copy, scale=w("dw")[:, 0:1]).then_inc(conv, 1)

                def copy_v():
                    act.wait_ge(v_psum, b + 1)
                    if not isinstance(b, int) or b >= 2:
                        act.wait_ge(am_used, 16 * (b - 1))
                    nc.scalar.activation(vt[:, u, :, :].rearrange("p c d -> p (c d)"), PS[:, 0, :], ACT.Copy)
                    for t in range(CT):
                        src = PS[:, 0, t * P:(t + 1) * P].rearrange("p (g j m) -> p j g m", j=4, m=HD)
                        ins = nc.scalar.activation(diagonal(vm, u, t), src, ACT.Copy)
                    ins.then_inc(v_ready, 1)

                def exps(n):
                    act.wait_ge(rot_step, 6 * b + 3 * n + 3)
                    nc.scalar.activation(ex[:, :], rot[:, 2, :], ACT.Exp, bias=minus_one[:, 0:1]).then_inc(exp_ready, 1)
                return [copy_xnT, lambda: exps(0), copy_v, lambda: exps(1)]

            def a(b, u, nxt):
                nxt = list(nxt)

                def turn():
                    if nxt:
                        nxt.pop(0)()
                act.wait_ge(kT_psum, b + 1)
                nc.scalar.activation(ktok[:, :, :].rearrange("p c d -> p (c d)"), PS[:, 7, 0:(CT - 1) * P],
                                     ACT.Copy).then_inc(ktok_ready, 1)
                turn()
                turn()
                turn()
                turn()
                act.wait_ge(den_step, 2 * b + 2)
                nc.scalar.activation(spread[:, :].rearrange("p (h m) -> p h m", m=HD),
                                     den[:, 1, :].unsqueeze(2).to_broadcast([P, CT * HEADS, HD]),
                                     ACT.Copy).then_inc(spread_ready, 1)
                act.wait_ge(rdT_psum, b + 1)
                nc.scalar.activation(rdT[:, :], PS[:, 7, :], ACT.Copy).then_inc(rdT_ready, 1)
                act.wait_ge(gate_psum, b + 1)
                nc.scalar.activation(th[:, :], PS[:, 6, :], ACT.Tanh, bias=w("b_gate"), scale=0.5).then_inc(th_ready, 1)
                act.wait_ge(zT_psum, b + 1)
                after_previous(act, hh_ready, b, 2)
                nc.scalar.activation(h[:, :], PS[:, 6, :], ACT.Identity, bias=w("ln_b"), scale=w("ln_g")).then_inc(h_ready, 1)
                act.wait_ge(lg_psum, b + 1)
                nc.scalar.activation(LG[:, bass.ds(b * (CT * MOE), CT * MOE)], PS[:, 6, 0:CT * MOE],
                                     ACT.Copy).then_inc(lg_ready, 1)
            a.engine = act
            both_stages(f, a)

        @block.vector
        def _(dve):
            def f(b, u):
                def stats():
                    dve.wait_ge(x_in, 16 * b + 16)
                    for t in range(CT):
                        xt = X[:, bass.ds(b * CT + t, 1), :].rearrange("p o d -> p (o d)")
                        nc.vector.bn_stats(st[:, t, :], xt).then_inc(ln1, 1)
                    wait_apart(dve, nc, ln1, CT * b + CT, scratch)
                    for t in range(CT):
                        ins = nc.vector.bn_aggr(mv[:, t, :], st[:, t, :])
                    ins.then_inc(ln1_stats, 1)

                def normalise():
                    dve.wait_ge(rstd1_ready, b + 1)
                    for t in range(CT):
                        xt = X[:, bass.ds(b * CT + t, 1), :].rearrange("p o d -> p (o d)")
                        ins = nc.vector.tensor_scalar(xn[:, t, :], xt, mv[:, t, 0:1], rstd[:, t:t + 1],
                                                      ALU.subtract, ALU.mult)
                    ins.then_inc(xn_ready, 1)

                def convolve():
                    for k in (1, 2):
                        dve.wait_ge(conv, 3 * b + k)
                        nc.vector.scalar_tensor_tensor(y[:, k, :], xnT[:, k:k + SEQ], w("dw")[:, k:k + 1],
                                                       y[:, k - 1, :], ALU.mult, ALU.add).then_inc(conv, 1)

                def residual():
                    dve.wait_ge(pw_psum, b + 1)
                    nc.vector.tensor_tensor(x1T[:, u, :], PS[:, 0, :], xnT[:, 2:], ALU.add).then_inc(x1_ready, 1)

                def rotate(n, dst):
                    dve.wait_ge(qk_psum, 2 * b + n + 1)
                    nc.vector.tensor_tensor(rot[:, 0, :], PS[:, 1, :], c("cos"), ALU.mult).then_inc(rot_step, 1)
                    nc.vector.tensor_tensor(rot[:, 1, :], PS[:, 2, :], c("sin"), ALU.mult).then_inc(qk_read, 1)
                    dve.wait_ge(rot_step, 6 * b + 3 * n + 1)
                    dve.wait_ge(qk_read, 2 * b + n + 1)
                    nc.vector.scalar_tensor_tensor(rot[:, 2, :], rot[:, 0, :], 1.0, rot[:, 1, :],
                                                   ALU.add, ALU.add).then_inc(rot_step, 2)

                def phi(n, dst):
                    dve.wait_ge(exp_ready, 2 * b + n + 1)
                    nc.vector.scalar_tensor_tensor(dst[:, u, :], ex[:, :], 1.0, rot[:, 2, :], ALU.min,
                                                   ALU.max).then_inc(phi_ready, 1)
                return [stats, normalise, convolve, residual, lambda: rotate(0, qphi), lambda: phi(0, qphi),
                        lambda: rotate(1, kphi), lambda: phi(1, kphi)]

            def a(b, u, nxt):
                nxt = list(nxt)

                def turn():
                    if nxt:
                        nxt.pop(0)()
                dve.wait_ge(phi_ready, 2 * b + 2)
                after_previous(dve, am_used, b, 16)
                for j in range(4):
                    ins = nc.vector.tensor_scalar(km[:, j, :], kphi[:, u, :], c("group")[:, j:j + 1], None, ALU.mult)
                ins.then_inc(km_ready, 1)
                nc.vector.tensor_tensor_scan(kp[:, :], kphi[:, u, :], kphi[:, u, :], 0.0,
                                             ALU.add, ALU.max).then_inc(kp_ready, 1)
                for n in range(16):
                    if n in (2, 6, 10):
                        t = n // 4
                        dve.wait_ge(state_psum, 3 * b + t + 1)
                        nc.vector.tensor_tensor(state[:, t, :], PS[:, 6, 0:P], c("block"), ALU.mult).then_inc(state_ready, 1)
                    if n == 12:
                        dve.wait_ge(den_psum, b + 1)
                        nc.vector.tensor_scalar(den[:, 0, :], PS[:, 7, 0:CT * HEADS], 1e-6, None, ALU.add).then_inc(den_step, 1)
                        dve.wait_ge(den_step, 2 * b + 1)
                        nc.vector.reciprocal(den[:, 1, :], den[:, 0, :]).then_inc(den_step, 1)
                    dve.wait_ge(scores_psum, 16 * b + n + 1)
                    if n >= 3:
                        dve.wait_ge(am_used, 16 * b + n - 2)
                    nc.vector.tensor_tensor(am[:, n % 3, :].rearrange("p (j q) -> p j q", j=4),
                                            PS[:, 3 + n % 2, :].rearrange("p (j q) -> p j q", j=4),
                                            c("tri").unsqueeze(1).to_broadcast([P, 4, P]), ALU.mult).then_inc(am_ready, 1)
                    if n in (1, 3, 5, 7, 9, 11, 13, 14):
                        turn()
                dve.wait_ge(am_used, 16 * b + 16)
                dve.wait_ge(rdT_ready, b + 1)
                nc.vector.tensor_tensor(attn[:, :], PS[:, 5, :], rdT[:, :], ALU.mult).then_inc(attn_ready, 1)
                dve.wait_ge(wo_psum, b + 1)
                dve.wait_ge(th_ready, b + 1)
                nc.vector.scalar_tensor_tensor(gated[:, :], th[:, :], 1.0, PS[:, 7, :], ALU.add, ALU.mult).then_inc(x2_step, 1)
                dve.wait_ge(x2_step, 2 * b + 1)
                nc.vector.tensor_tensor(x2T[:, :], gated[:, :], x1T[:, u, :], ALU.add).then_inc(x2_step, 1)
                dve.wait_ge(x2_psum, b + 1)
                for t in range(CT):
                    nc.vector.bn_stats(st2[:, t, :], PS[:, 7, t * P:(t + 1) * P]).then_inc(ln2, 1)
                wait_apart(dve, nc, ln2, CT * b + CT, scratch)
                for t in range(CT):
                    ins = nc.vector.bn_aggr(mv2[:, t, :], st2[:, t, :])
                ins.then_inc(ln2_stats, 1)
                nc.vector.tensor_tensor(tokens(X, b), tokens(X, b), PS[:, 7, :].rearrange("p (c d) -> p c d", c=CT),
                                        ALU.add)
                dve.wait_ge(rstd2_ready, b + 1)
                for t in range(CT):
                    ins = nc.vector.tensor_scalar(z[:, t, :], PS[:, 7, t * P:(t + 1) * P], mv2[:, t, 0:1],
                                                  rstd2[:, t:t + 1], ALU.subtract, ALU.mult)
                ins.then_inc(z_ready, 1)
                dve.wait_ge(h_ready, b + 1)
                nc.vector.tensor_copy(HH[:, bass.ds(b * SEQ, SEQ)], h[:, :]).then_inc(hh_ready, 1)
                dve.wait_ge(hh_ready, 2 * b + 1)
                nc.vector.tensor_tensor(HL[:, bass.ds(b * SEQ, SEQ)], h[:, :],
                                        HH[:, bass.ds(b * SEQ, SEQ)].bitcast(F32), ALU.subtract).then_inc(hh_ready, 1)
            a.engine = dve
            both_stages(f, a)


def mixture(nc, X, w, c, PS, before, ones, minus_half, eps, scratch, HH, HL, LG, w1t, w2t):
    with ExitStack() as ctx:
        def sb(name, shape, dt=F32):
            return ctx.enter_context(nc.sbuf_tensor("m_" + name, shape, dt))

        def sem(name):
            return ctx.enter_context(nc.semaphore("m_" + name))

        FF = MOE * 512
        raw = sb("raw", [P, FF])
        w1h, w1l, w2h, w2l = (sb(n, [P, FF], F32R) for n in ("w1h", "w1l", "w2h", "w2l"))
        gate = sb("gate", [P, TILES, MOE])
        top = sb("top", [P, TILES])
        total = sb("total", [P, TILES])
        gparts = sb("gparts", [P, TILES, 2 * MOE])
        gp = sb("gp", [P, CT * 2 * MOE])
        gT = sb("gT", [2 * MOE, SEQ], F32R)
        selr = sb("selr", [2 * MOE, MOE * P], F32R)
        gb = sb("gb", [P, 2, SEQ])
        S = sb("S", [P, 3, SEQ])
        Sh = sb("Sh", [P, 3, SEQ], F32R)
        Sl = sb("Sl", [P, 3, SEQ], F32R)
        oe = sb("oe", [P, 2, SEQ])

        w_in = sem("w_in"); w_split = sem("w_split"); raw_read = sem("raw_read")
        gate_step = sem("gate_step"); exp_done = sem("exp_done"); gates_ready = sem("gates_ready")
        gp_ready = sem("gp_ready"); gT_psum = sem("gT_psum"); gT_ready = sem("gT_ready")
        gb_psum = sem("gb_psum"); gb_ready = sem("gb_ready")
        h_psum = sem("h_psum"); s_ready = sem("s_ready"); sh_ready = sem("sh_ready"); sl_ready = sem("sl_ready")
        s_used = sem("s_used"); out_psum = sem("out_psum"); oe_ready = sem("oe_ready"); back_psum = sem("back_psum")
        oe_used = sem("oe_used"); x_ready = sem("x_ready")

        block = ctx.enter_context(nc.Block())
        ident = c("ident")
        N = MOE * MOE_CHUNKS

        def over_batches(eng, one):
            one(0)
            with eng.Fori(1, BATCHES) as b:
                one(b)

        @block.sync
        def _(sp):
            sp.dma_start(raw[:, :], w1t).then_inc(w_in, 16)
            sp.wait_ge(raw_read, 1)
            sp.dma_start(raw[:, :], w2t).then_inc(w_in, 16)
            sp.wait_ge(w_in, 32)

        @block.tensor
        def _(pe):
            pe.wait_ge(w_split, 5)

            def up(b, n):
                if n >= 3:
                    pe.wait_ge(s_ready, N * b + n - 2)
                else:
                    after_previous(pe, s_ready, b, N)
                tok = bass.ds(b * SEQ, SEQ)
                bank = PS[:, n % 3, :]
                f = slice(n * P, (n + 1) * P)
                nc.tensor.matmul(bank, w1h[:, f], HH[:, tok], start=True, stop=False)
                nc.tensor.matmul(bank, w1h[:, f], HL[:, tok], start=False, stop=False)
                nc.tensor.matmul(bank, w1l[:, f], HH[:, tok], start=False, stop=True).then_inc(h_psum, 1)

            def down(b, n):
                e, k = divmod(n, MOE_CHUNKS)
                bank = PS[:, 3 + e % 2, :]
                if k == 0:
                    if e >= 2:
                        pe.wait_ge(oe_ready, MOE * b + e - 1)
                    else:
                        after_previous(pe, oe_ready, b, MOE)
                f = slice(n * P, (n + 1) * P)
                pe.wait_ge(sh_ready, N * b + n + 1)
                nc.tensor.matmul(bank, w2h[:, f], Sh[:, n % 3, :], start=(k == 0), stop=False)
                nc.tensor.matmul(bank, w2l[:, f], Sh[:, n % 3, :], start=False, stop=False)
                pe.wait_ge(sl_ready, N * b + n + 1)
                last = nc.tensor.matmul(bank, w2h[:, f], Sl[:, n % 3, :], start=False, stop=(k == MOE_CHUNKS - 1))
                if k == MOE_CHUNKS - 1:
                    last.then_inc(out_psum, 1)
                else:
                    last.then_inc(s_used, 1)

            def back(b, e):
                pe.wait_ge(oe_ready, MOE * b + e + 1)
                if e == 0:
                    after_previous(pe, x_ready, b)
                for t in range(CT):
                    mm = nc.tensor.matmul(PS[:, 7, t * P:(t + 1) * P], oe[:, e % 2, t * P:(t + 1) * P], ident,
                                          is_transpose=True, start=(e == 0 and t == 0), stop=(e == MOE - 1),
                                          skip_group_check=True)
                mm.then_inc(back_psum, 1)

            def gates(b):
                pe.wait_ge(gp_ready, b + 1)
                after_previous(pe, gb_ready, b, MOE)
                for t in range(CT):
                    mm = nc.tensor.transpose(PS[0:2 * MOE, 5, t * P:(t + 1) * P],
                                             gp[:, t * 2 * MOE:(t + 1) * 2 * MOE], ident)
                mm.then_inc(gT_psum, 1)

            def spread(b, e):
                pe.wait_ge(gT_ready, b + 1)
                if e:
                    pe.wait_ge(gb_ready, MOE * b + e)
                nc.tensor.matmul(PS[:, 6, :], selr[:, e * P:(e + 1) * P], gT[:, :], start=True,
                                 stop=True).then_inc(gb_psum, 1)

            def one(b):
                gates(b)
                for n in range(N + 2):
                    if n < N:
                        up(b, n)
                    if n in (2, 5, 9, 13):
                        spread(b, (2, 5, 9, 13).index(n))
                    if n >= 2:
                        down(b, n - 2)
                    if n in (8, 12, 16):
                        back(b, n // 4 - 2)
                back(b, 3)
            over_batches(pe, one)

        @block.scalar
        def _(act):
            nc.scalar.preload_act_table(ACT.Exp)
            act.wait_ge(gate_step, 2)
            nc.scalar.activation(gate[:, :, :], gate[:, :, :], ACT.Exp).then_inc(exp_done, 1)
            nc.scalar.preload_act_table(ACT.Silu)

            def one(b):
                act.wait_ge(gT_psum, b + 1)
                nc.scalar.activation(gT[:, :], PS[0:2 * MOE, 5, :], ACT.Copy).then_inc(gT_ready, 1)
                for n in range(N):
                    act.wait_ge(h_psum, N * b + n + 1)
                    if n >= 3:
                        act.wait_ge(sl_ready, N * b + n - 2)
                    else:
                        after_previous(act, sl_ready, b, N)
                    nc.scalar.activation(S[:, n % 3, :], PS[:, n % 3, :], ACT.Silu, bias=w("b1")[:, n:n + 1]).then_inc(s_ready, 1)
                    if n in (2, 5, 9, 13):
                        e = (2, 5, 9, 13).index(n)
                        act.wait_ge(gb_psum, MOE * b + e + 1)
                        if e >= 2:
                            act.wait_ge(oe_ready, MOE * b + e - 1)
                        else:
                            after_previous(act, oe_ready, b, MOE)
                        nc.scalar.activation(gb[:, e % 2, :], PS[:, 6, :], ACT.Copy).then_inc(gb_ready, 1)
            over_batches(act, one)

        @block.vector
        def _(dve):
            nc.vector.tensor_copy(selr[:, :], c("sel")[0:2 * MOE, :]).then_inc(w_split, 1)
            lg = LG[:, :].rearrange("p (t e) -> p t e", e=MOE)
            wide = lambda a: a.unsqueeze(2).to_broadcast([P, TILES, MOE])
            nc.vector.tensor_reduce(top[:, :], lg, AX.X, ALU.max).then_inc(gate_step, 1)
            dve.wait_ge(gate_step, 1)
            nc.vector.tensor_tensor(gate[:, :, :], lg, wide(top[:, :]), ALU.subtract).then_inc(gate_step, 1)
            dve.wait_ge(exp_done, 1)
            nc.vector.tensor_reduce(total[:, :], gate[:, :, :], AX.X, ALU.add).then_inc(gate_step, 1)
            dve.wait_ge(gate_step, 3)
            nc.vector.reciprocal(top[:, :], total[:, :]).then_inc(gate_step, 1)
            dve.wait_ge(gate_step, 4)
            nc.vector.tensor_tensor(gate[:, :, :], gate[:, :, :], wide(top[:, :]), ALU.mult).then_inc(gate_step, 1)
            dve.wait_ge(gate_step, 5)
            nc.vector.tensor_copy(gparts[:, :, 0:MOE].bitcast(F32R), gate[:, :, :]).then_inc(gate_step, 1)
            dve.wait_ge(gate_step, 6)
            nc.vector.tensor_tensor(gparts[:, :, MOE:], gate[:, :, :], gparts[:, :, 0:MOE], ALU.subtract).then_inc(gates_ready, 1)
            for k, (hi, lo) in enumerate([(w1h, w1l), (w2h, w2l)]):
                dve.wait_ge(w_in, 16 * k + 16)
                nc.vector.tensor_copy(hi[:, :], raw[:, :]).then_inc(w_split, 1)
                dve.wait_ge(w_split, 2 * k + 2)
                nc.vector.tensor_tensor(lo[:, :], raw[:, :], hi[:, :].bitcast(F32), ALU.subtract).then_inc(w_split, 1)
                dve.wait_ge(w_split, 2 * k + 3)
                if k == 0:
                    nc.vector.engine_nop().then_inc(raw_read, 1)
            dve.wait_ge(gates_ready, 1)

            def one(b):
                after_previous(dve, gT_psum, b)
                nc.vector.tensor_copy(gp[:, :].rearrange("p (t e) -> p t e", t=CT),
                                      gparts[:, bass.ds(b * CT, CT), :]).then_inc(gp_ready, 1)
                for n in range(N + 4):
                    if n < N:
                        dve.wait_ge(s_ready, N * b + n + 1)
                        if n >= 3:
                            wait_used(dve, b, n - 3)
                        nc.vector.tensor_copy(Sh[:, n % 3, :], S[:, n % 3, :]).then_inc(sh_ready, 1)
                        dve.wait_ge(sh_ready, N * b + n + 1)
                        nc.vector.tensor_tensor(Sl[:, n % 3, :], S[:, n % 3, :], Sh[:, n % 3, :].bitcast(F32),
                                                ALU.subtract).then_inc(sl_ready, 1)
                    if n >= 7 and n % 4 == 3 or n == N + 3:
                        e = n // 4 - 1
                        dve.wait_ge(out_psum, MOE * b + e + 1)
                        dve.wait_ge(gb_ready, MOE * b + e + 1)
                        if e >= 2:
                            dve.wait_ge(back_psum, MOE * b + e - 1)
                        else:
                            after_previous(dve, back_psum, b, MOE)
                        nc.vector.scalar_tensor_tensor(oe[:, e % 2, :], PS[:, 3 + e % 2, :], w("b2")[:, e:e + 1],
                                                       gb[:, e % 2, :], ALU.add, ALU.mult).then_inc(oe_ready, 1)
                dve.wait_ge(back_psum, MOE * b + MOE)
                xb = X[:, bass.ds(b * CT, CT), :]
                nc.vector.tensor_tensor(xb, xb, PS[:, 7, :].rearrange("p (c d) -> p c d", c=CT), ALU.add).then_inc(x_ready, 1)

            def wait_used(eng, b, n):
                e, k = divmod(n, MOE_CHUNKS)
                if k == MOE_CHUNKS - 1:
                    eng.wait_ge(out_psum, MOE * b + e + 1)
                else:
                    eng.wait_ge(s_used, (N - MOE) * b + e * (MOE_CHUNKS - 1) + k + 1)
            over_batches(dve, one)


def route(layer, nc, X, w, c, PS, before, ones, minus_half, eps, scratch, rows, slot_row, slot_expert):
    with ExitStack() as ctx:
        def sb(name, shape, dt=F32):
            return ctx.enter_context(nc.sbuf_tensor(f"r{layer}_" + name, shape, dt))

        def sem(name):
            return ctx.enter_context(nc.semaphore(f"r{layer}_" + name))

        st = sb("st", [P, CT, 6])
        mv = sb("mv", [P, CT, 2])
        ve = sb("ve", [P, CT])
        rstd = sb("rstd", [P, CT])
        row = sb("row", [P, 2, CT, ROW])
        xT = sb("xT", [P, SEQ])
        lg = sb("lg", [P, CT, EXPERTS])
        top = sb("top", [P, CT, 8])
        at = sb("at", [P, CT, 8], U32)
        first = sb("first", [P, CT])
        hot = sb("hot", [P, CT, EXPERTS], BF16)
        hot32 = sb("hot32", [P, CT, EXPERTS])
        soft = sb("soft", [P, CT, EXPERTS])
        small = sb("small", [P, 4, CT])
        base = sb("base", [P, EXPERTS])
        place = sb("place", [P, 2, CT, EXPERTS])
        pos = sb("pos", [P, CT])
        posi = sb("posi", [P, 2, CT], I32)
        padding = sb("padding", [P, 2, ROW])
        told = sb("told", [P, CT])
        got = sb("got", [P, EXPERTS])
        tiles = sb("tiles", [P, EXPERTS])
        ends = sb("ends", [P, EXPERTS])
        jump = sb("jump", [P, EXPERTS])
        slot_at = sb("slot_at", [P, NSLOT])
        number = sb("number", [P, NSLOT])
        skipped = sb("skipped", [P, NSLOT])
        over = sb("over", [P, EXPERTS, NSLOT])
        passed = sb("passed", [P, NSLOT, EXPERTS])
        jumped = sb("jumped", [P, NSLOT, EXPERTS])
        padi = sb("padi", [P, EXPERTS], I32)

        cleared = sem("cleared"); ln = sem("ln"); ln_stats = sem("ln_stats"); ve_done = sem("ve_done")
        rstd_ready = sem("rstd_ready"); xn_ready = sem("xn_ready"); x_copied = sem("x_copied")
        xT_psum = sem("xT_psum"); xT_ready = sem("xT_ready"); lg_psum = sem("lg_psum"); lg_ready = sem("lg_ready")
        pick = sem("pick"); hot_ready = sem("hot_ready"); count_psum = sem("count_psum"); place_step = sem("place_step")
        pos_ready = sem("pos_ready"); soft_ready = sem("soft_ready"); exp_ready = sem("exp_ready")
        gate_step = sem("gate_step"); tv_ready = sem("tv_ready"); scattered = [sem("scattered_even"), sem("scattered_odd")]
        told_done = sem("told_done"); ends_ready = sem("ends_ready"); padded = sem("padded"); table = sem("table")

        block = ctx.enter_context(nc.Block())
        ident = c("ident")
        router = w(f"router{layer}")

        def over_batches(eng, one):
            one(0, 0, None)
            one(1, 1, None)
            with eng.Fori(1, BATCHES // 2) as i:
                for u in range(2):
                    one(i * 2 + u, u, i)

        @block.sync
        def _(sp):
            sp.wait_ge(cleared, 1)
            spare = rows[EXPERTS * REGION:, :].rearrange("(n p) r -> p n r", p=P)
            for s in range(SPARE // SLOT):
                sp.dma_start(spare[:, 2 * s:2 * s + 2, :], padding[:, :, :]).then_inc(padded, 16)
            sp.wait_ge(ends_ready, 1)
            for e in range(EXPERTS):
                end = sp.value_load(padi[0:1, e:e + 1], min_val=e * REGION, max_val=e * REGION + TOKENS)
                sp.dma_start(rows[bass.ds(end, SLOT), :].rearrange("(n p) r -> p n r", p=P),
                             padding[:, :, :]).then_inc(padded, 16)
            sp.wait_ge(padded, 16 * (SPARE // SLOT + EXPERTS))

        @block.gpsimd
        def _(pool):
            nc.gpsimd.memset(padding[:, :, :], 0.0).then_inc(ve_done, 1)
            pool.wait_ge(ve_done, 1)
            nc.gpsimd.memset(padding[:, :, COL_ID:COL_ID + 1], NO_TOKEN).then_inc(cleared, 1)

            def one(b, u, turn):
                pool.wait_ge(ln_stats, b + 1)
                nc.gpsimd.tensor_tensor(ve[:, :], mv[:, :, 1], eps[:, 0:CT], ALU.add).then_inc(ve_done, 1)
                pool.wait_ge(ve_done, b + 2)
                nc.gpsimd.tensor_tensor(rstd[:, :], ve[:, :], minus_half[:, :], ALU.pow).then_inc(rstd_ready, 1)
                pool.wait_ge(pos_ready, b + 1)
                pool.wait_ge(tv_ready, b + 1)
                pool.wait_ge(x_copied, b + 1)
                nc.gpsimd.tensor_tensor(told[:, :], minus_half[:, :], minus_half[:, :], ALU.mult)
                for t in range(CT):
                    nc.gpsimd.indirect_dma_start(
                        out=rows, out_offset=bass.IndirectOffsetOnAxis(ap=posi[:, u, t:t + 1], axis=0),
                        in_=row[:, u, t, :], in_offset=None).then_inc(scattered[u], 16)
            over_batches(pool, one)
            pool.wait_ge(scattered[0], 16 * TILES // 2)
            pool.wait_ge(scattered[1], 16 * TILES // 2)

        @block.tensor
        def _(pe):
            def one(b, u, turn):
                pe.wait_ge(xn_ready, b + 1)
                for t in range(CT):
                    mm = nc.tensor.transpose(PS[:, 0, t * P:(t + 1) * P], row[:, u, t, 0:P], ident)
                mm.then_inc(xT_psum, 1)
                pe.wait_ge(xT_ready, b + 1)
                after_previous(pe, lg_ready, b)
                for t in range(CT):
                    mm = nc.tensor.matmul(PS[:, 1, t * EXPERTS:(t + 1) * EXPERTS], xT[:, t * P:(t + 1) * P], router,
                                          start=True, stop=True)
                mm.then_inc(lg_psum, 1)
                pe.wait_ge(hot_ready, b + 1)
                flat = hot[:, :, :].rearrange("p t e -> p (t e)")
                counts = PS[:, 2, 0:CT * EXPERTS]
                nc.tensor.matmul(counts, before[:, :], flat, start=True, stop=True, skip_group_check=True)
                for d in range(1, CT):
                    mm = nc.tensor.matmul(PS[:, 2, d * EXPERTS:CT * EXPERTS], ones[:, :], flat[:, 0:(CT - d) * EXPERTS],
                                          start=False, stop=True, skip_group_check=True)
                for t in range(CT):
                    mm = nc.tensor.matmul(PS[:, 3, 0:EXPERTS], ones[:, :], hot[:, t, :], start=(t == 0), stop=(t == CT - 1))
                mm.then_inc(count_psum, 1)
            over_batches(pe, one)

        @block.scalar
        def _(act):
            nc.scalar.preload_act_table(ACT.Exp)

            def one(b, u, turn):
                act.wait_ge(xT_psum, b + 1)
                nc.scalar.activation(xT[:, :], PS[:, 0, :], ACT.Copy).then_inc(xT_ready, 1)
                nc.scalar.activation(row[:, u, :, COL_X:COL_X + P], X[:, bass.ds(b * CT, CT), :], ACT.Copy).then_inc(x_copied, 1)
                act.wait_ge(soft_ready, b + 1)
                nc.scalar.activation(soft[:, :, :], soft[:, :, :], ACT.Exp).then_inc(exp_ready, 1)
            over_batches(act, one)

        @block.vector
        def _(dve):
            nc.vector.tensor_copy(base[:, :], c("region")).then_inc(place_step, 1)
            nc.vector.memset(row[:, :, :, COL_TV:ROW], 0.0).then_inc(place_step, 1)
            dve.wait_ge(place_step, 2)

            def one(b, u, turn):
                for t in range(CT):
                    nc.vector.bn_stats(st[:, t, :], X[:, bass.ds(b * CT + t, 1), :].rearrange("p o d -> p (o d)")).then_inc(ln, 1)
                wait_apart(dve, nc, ln, CT * b + CT, scratch)
                for t in range(CT):
                    ins = nc.vector.bn_aggr(mv[:, t, :], st[:, t, :])
                ins.then_inc(ln_stats, 1)
                dve.wait_ge(rstd_ready, b + 1)
                if turn is not None:
                    dve.wait_ge(scattered[u], 16 * CT * turn)
                for t in range(CT):
                    xt = X[:, bass.ds(b * CT + t, 1), :].rearrange("p o d -> p (o d)")
                    ins = nc.vector.tensor_scalar(row[:, u, t, 0:P], xt, mv[:, t, 0:1], rstd[:, t:t + 1],
                                                  ALU.subtract, ALU.mult)
                ins.then_inc(xn_ready, 1)
                nc.vector.tensor_copy(row[:, u, :, COL_ID:COL_ID + 1], c("ids")[:, bass.ds(b * CT, CT)].unsqueeze(2))
                dve.wait_ge(lg_psum, b + 1)
                scores = PS[:, 1, 0:CT * EXPERTS].rearrange("p (t e) -> p t e", t=CT)
                if layer:
                    nc.vector.tensor_tensor(lg[:, :, :], scores, w("br1").unsqueeze(1).to_broadcast([P, CT, EXPERTS]),
                                            ALU.add).then_inc(lg_ready, 1)
                else:
                    nc.vector.tensor_copy(lg[:, :, :], scores).then_inc(lg_ready, 1)
                wait_apart(dve, nc, lg_ready, b + 1, scratch)
                for t in range(CT):
                    ins = nc.vector.max(top[:, t, :], lg[:, t, :])
                ins.then_inc(pick, 1)
                wait_apart(dve, nc, pick, 3 * b + 1, scratch)
                for t in range(CT):
                    ins = nc.vector.max_index(at[:, t, :], top[:, t, :], lg[:, t, :])
                ins.then_inc(pick, 1)
                nc.vector.tensor_tensor(soft[:, :, :], lg[:, :, :], top[:, :, 0:1].to_broadcast([P, CT, EXPERTS]),
                                        ALU.subtract).then_inc(soft_ready, 1)
                dve.wait_ge(pick, 3 * b + 2)
                nc.vector.tensor_copy(first[:, :], at[:, :, 0]).then_inc(pick, 1)
                dve.wait_ge(pick, 3 * b + 3)
                nc.vector.tensor_tensor(hot32[:, :, :], c("iota").unsqueeze(1).to_broadcast([P, CT, EXPERTS]),
                                        first[:, :].unsqueeze(2).to_broadcast([P, CT, EXPERTS]), ALU.is_equal)
                nc.vector.tensor_tensor(hot[:, :, :], c("iota").unsqueeze(1).to_broadcast([P, CT, EXPERTS]),
                                        first[:, :].unsqueeze(2).to_broadcast([P, CT, EXPERTS]), ALU.is_equal).then_inc(hot_ready, 1)
                dve.wait_ge(exp_ready, b + 1)
                nc.vector.tensor_reduce(small[:, 0, :], soft[:, :, :], AX.X, ALU.add).then_inc(gate_step, 1)
                dve.wait_ge(gate_step, 4 * b + 1)
                nc.vector.reciprocal(small[:, 1, :], small[:, 0, :]).then_inc(gate_step, 1)
                dve.wait_ge(gate_step, 4 * b + 2)
                nc.vector.tensor_scalar(small[:, 2, :], small[:, 1, :], 1e-8, None, ALU.add).then_inc(gate_step, 1)
                dve.wait_ge(gate_step, 4 * b + 3)
                nc.vector.reciprocal(small[:, 3, :], small[:, 2, :]).then_inc(gate_step, 1)
                dve.wait_ge(gate_step, 4 * b + 4)
                nc.vector.tensor_tensor(row[:, u, :, COL_TV:COL_TV + 1], small[:, 1, :].unsqueeze(2),
                                        small[:, 3, :].unsqueeze(2), ALU.mult).then_inc(tv_ready, 1)
                dve.wait_ge(count_psum, b + 1)
                nc.vector.tensor_tensor(place[:, 0, :, :], PS[:, 2, 0:CT * EXPERTS].rearrange("p (t e) -> p t e", t=CT),
                                        base[:, :].unsqueeze(1).to_broadcast([P, CT, EXPERTS]), ALU.add).then_inc(place_step, 1)
                dve.wait_ge(place_step, 4 * b + 3)
                nc.vector.tensor_tensor(place[:, 1, :, :], place[:, 0, :, :], hot32[:, :, :], ALU.mult).then_inc(place_step, 1)
                nc.vector.tensor_tensor(base[:, :], base[:, :], PS[:, 3, 0:EXPERTS], ALU.add).then_inc(place_step, 1)
                dve.wait_ge(place_step, 4 * b + 4)
                nc.vector.tensor_reduce(pos[:, :], place[:, 1, :, :], AX.X, ALU.add).then_inc(place_step, 1)
                dve.wait_ge(place_step, 4 * b + 6)
                nc.vector.tensor_copy(posi[:, u, :], pos[:, :]).then_inc(pos_ready, 1)
            over_batches(dve, one)
            nc.vector.tensor_copy(padi[:, :], base[:, :]).then_inc(ends_ready, 1)
            nc.vector.tensor_tensor(got[:, :], base[:, :], c("region"), ALU.subtract).then_inc(table, 1)
            nc.vector.tensor_scalar(slot_at[:, :], c("slots"), float(SLOT), None, ALU.mult).then_inc(table, 1)
            dve.wait_ge(table, 2)
            by_expert = [P, EXPERTS, NSLOT]
            nc.vector.tensor_tensor(over[:, :, :], got[:, :].unsqueeze(2).to_broadcast(by_expert),
                                    slot_at[:, :].unsqueeze(1).to_broadcast(by_expert), ALU.is_gt).then_inc(table, 1)
            dve.wait_ge(table, 3)
            nc.vector.tensor_reduce(tiles[:, :], over[:, :, :], AX.X, ALU.add).then_inc(table, 1)
            dve.wait_ge(table, 4)
            nc.vector.tensor_tensor_scan(ends[:, :], tiles[:, :], tiles[:, :], 0.0, ALU.add, ALU.max).then_inc(table, 1)
            nc.vector.tensor_scalar(jump[:, :], tiles[:, :], -float(SLOT), float(REGION), ALU.mult, ALU.add).then_inc(table, 1)
            dve.wait_ge(table, 6)
            by_slot = [P, NSLOT, EXPERTS]
            nc.vector.tensor_tensor(passed[:, :, :], c("slots").unsqueeze(2).to_broadcast(by_slot),
                                    ends[:, :].unsqueeze(1).to_broadcast(by_slot), ALU.is_ge).then_inc(table, 1)
            dve.wait_ge(table, 7)
            nc.vector.tensor_reduce(number[:, :], passed[:, :, :], AX.X, ALU.add).then_inc(table, 1)
            nc.vector.tensor_tensor(jumped[:, :, :], passed[:, :, :], jump[:, :].unsqueeze(1).to_broadcast(by_slot),
                                    ALU.mult).then_inc(table, 1)
            dve.wait_ge(table, 9)
            nc.vector.tensor_scalar(slot_expert[:, :], number[:, :], float(EXPERTS - 1), None, ALU.min).then_inc(table, 1)
            nc.vector.tensor_reduce(skipped[:, :], jumped[:, :, :], AX.X, ALU.add).then_inc(table, 1)
            dve.wait_ge(table, 11)
            nc.vector.tensor_tensor(slot_row[:, :], skipped[:, :], slot_at[:, :], ALU.add).then_inc(table, 1)
            dve.wait_ge(table, 12)



def routed(layer, nc, X, w, c, PS, before, ones, minus_half, eps, scratch, rows, weights, b2, dest, slot_row, slot_expert):
    chunks = (2, 4)[layer]
    B1 = 2 * chunks * P
    with ExitStack() as ctx:
        def sb(name, shape, dt=F32):
            return ctx.enter_context(nc.sbuf_tensor(f"f{layer}_" + name, shape, dt))

        def sem(name):
            return ctx.enter_context(nc.semaphore(f"f{layer}_" + name))

        row = sb("row", [P, 2, 2, ROW])
        wt = sb("wt", [P, 2, weights.shape[2]])
        b2r = sb("b2r", [1, 2, P])
        one_row = sb("one_row", [1, P])
        xT = sb("xT", [P, 2, SLOT])
        hid = sb("hid", [P, 2, chunks, SLOT])
        y = sb("y", [P, 2, P])
        st = sb("st", [P, 2, 6])
        mv = sb("mv", [P, 2, 2])
        ve = sb("ve", [P, 2])
        rstd = sb("rstd", [P, 2])
        zed = sb("zed", [P, 3, 2, P])
        res = sb("res", [P, 2, 2, P])
        token = sb("token", [P, 2, 2], I32)
        told = sb("told", [P, CT])

        rows_in = [sem(f"rows_in{u}") for u in range(2)]
        weights_in = [sem(f"weights_in{u}") for u in range(2)]
        one_made = sem("one_made"); xT_psum = sem("xT_psum"); xT_ready = sem("xT_ready"); h_psum = sem("h_psum")
        hid_ready = sem("hid_ready"); out_psum = sem("out_psum"); y_ready = sem("y_ready"); stats = sem("stats")
        mv_ready = sem("mv_ready"); ve_done = sem("ve_done"); rstd_ready = sem("rstd_ready"); zed_step = sem("zed_step")
        res_ready = sem("res_ready"); stored = [sem("stored_even"), sem("stored_odd")]; told_done = sem("told_done")

        block = ctx.enter_context(nc.Block())
        ident = c("ident")

        def over_slots(eng, one):
            one(0, 0, 1)
            one(1, 1, 1)
            with eng.Fori(1, NSLOT // 2) as i:
                for u in range(2):
                    one(i * 2 + u, u, i + 1)

        def later(s):
            return not isinstance(s, int) or s >= 2

        @block.sync
        def _(sp):
            def one(s, u, turn):
                r = sp.value_load(slot_row[0:1, bass.ds(s, 1)], min_val=0, max_val=ROWS - SLOT)
                e = sp.value_load(slot_expert[0:1, bass.ds(s, 1)], min_val=0, max_val=EXPERTS - 1)
                if later(s):
                    sp.wait_ge(res_ready, s - 1)
                sp.dma_start(row[:, u, :, :], rows[bass.ds(r, SLOT), :].rearrange("(p a) r -> p a r", a=2)).then_inc(rows_in[u], 16)
                sp.dma_start(wt[:, u, :], weights[bass.ds(e, 1), :, :].rearrange("o p n -> (o p) n")).then_inc(weights_in[u], 16)
                if layer:
                    sp.dma_start(b2r[0:1, u, :], b2[bass.ds(e, 1), :]).then_inc(weights_in[u], 16)
            over_slots(sp, one)

        @block.gpsimd
        def _(pool):
            nc.gpsimd.memset(one_row[:, :], 1.0).then_inc(one_made, 1)

            def one(s, u, turn):
                if not layer:
                    pool.wait_ge(mv_ready, s + 1)
                    nc.gpsimd.tensor_tensor(ve[:, :], mv[:, :, 1], eps[:, 0:2], ALU.add).then_inc(ve_done, 1)
                    pool.wait_ge(ve_done, s + 1)
                    nc.gpsimd.tensor_tensor(rstd[:, :], ve[:, :], minus_half[:, 0:2], ALU.pow).then_inc(rstd_ready, 1)
                pool.wait_ge(res_ready, s + 1)
                after_previous(pool, told_done, s)
                nc.gpsimd.tensor_tensor(told[:, :], minus_half[:, :], minus_half[:, :], ALU.mult).then_inc(told_done, 1)
                for a in range(2):
                    nc.gpsimd.indirect_dma_start(
                        out=dest, out_offset=bass.IndirectOffsetOnAxis(ap=token[:, u, a:a + 1], axis=0),
                        in_=res[:, u, a, :], in_offset=None, bounds_check=TOKENS - 1, oob_is_err=False).then_inc(stored[u], 16)
            over_slots(pool, one)
            pool.wait_ge(stored[0], 32 * NSLOT // 2)
            pool.wait_ge(stored[1], 32 * NSLOT // 2)

        @block.tensor
        def _(pe):
            pe.wait_ge(one_made, 1)

            def up(s, u, turn):
                pe.wait_ge(rows_in[u], 16 * turn)
                for a in range(2):
                    mm = nc.tensor.transpose(PS[:, u, a * P:(a + 1) * P], row[:, u, a, 0:P], ident)
                mm.then_inc(xT_psum, 1)
                pe.wait_ge(weights_in[u], (16 + 16 * layer) * turn)
                pe.wait_ge(xT_ready, s + 1)
                for f in range(chunks):
                    bank, half = divmod(f, 2)
                    mm = nc.tensor.matmul(PS[:, 2 + 2 * u + bank, half * SLOT:(half + 1) * SLOT],
                                          wt[:, u, f * P:(f + 1) * P], xT[:, u, :], start=True, stop=True)
                mm.then_inc(h_psum, 1)

            def down(s, u):
                pe.wait_ge(hid_ready, s + 1)
                if later(s):
                    pe.wait_ge(res_ready, s - 1)
                for a in range(2):
                    for f in range(chunks):
                        mm = nc.tensor.matmul(PS[:, 6 + u, a * P:(a + 1) * P], hid[:, u, f, a * P:(a + 1) * P],
                                              wt[:, u, (chunks + f) * P:(chunks + f + 1) * P],
                                              start=(f == 0), stop=(f == chunks - 1 and not layer))
                    if layer:
                        mm = nc.tensor.matmul(PS[:, 6 + u, a * P:(a + 1) * P], one_row[:, :], b2r[0:1, u, :],
                                              start=False, stop=True)
                mm.then_inc(out_psum, 1)

            up(0, 0, 1)
            up(1, 1, 1)
            down(0, 0)
            with pe.Fori(1, NSLOT // 2) as i:
                for u in range(2):
                    up(i * 2 + u, u, i + 1)
                    down(i * 2 + (u - 1), 1 - u)
            down(NSLOT - 1, 1)

        @block.scalar
        def _(act):
            nc.scalar.preload_act_table(ACT.Gelu)

            def one(s, u, turn):
                act.wait_ge(xT_psum, s + 1)
                nc.scalar.activation(xT[:, u, :], PS[:, u, 0:SLOT], ACT.Copy).then_inc(xT_ready, 1)
                act.wait_ge(h_psum, s + 1)
                if later(s):
                    act.wait_ge(out_psum, s - 1)
                if layer:
                    for f in range(chunks):
                        bank, half = divmod(f, 2)
                        ins = nc.scalar.activation(hid[:, u, f, :], PS[:, 2 + 2 * u + bank, half * SLOT:(half + 1) * SLOT],
                                                   ACT.Gelu, bias=wt[:, u, B1 + f:B1 + f + 1])
                else:
                    ins = nc.scalar.activation(hid[:, u, :, :].rearrange("p f t -> p (f t)"), PS[:, 2 + 2 * u, :], ACT.Gelu)
                ins.then_inc(hid_ready, 1)
            over_slots(act, one)

        @block.vector
        def _(dve):
            def one(s, u, turn):
                dve.wait_ge(rows_in[u], 16 * turn)
                if later(s):
                    dve.wait_ge(stored[u], 32 * (turn - 1))
                nc.vector.tensor_copy(token[:, u, :].unsqueeze(2), row[:, u, :, COL_ID:COL_ID + 1])
                dve.wait_ge(out_psum, s + 1)
                bank = PS[:, 6 + u, 0:SLOT].rearrange("p (a d) -> p a d", a=2)
                xs = row[:, u, :, COL_X:COL_X + P]
                if layer:
                    nc.vector.tensor_tensor(res[:, u, :, :], bank, xs, ALU.add).then_inc(res_ready, 1)
                    return
                for a in range(2):
                    nc.vector.tensor_scalar(y[:, a, :], bank[:, a, :], row[:, u, a, COL_TV:COL_TV + 1], None,
                                            ALU.mult).then_inc(y_ready, 1)
                dve.wait_ge(y_ready, 2 * s + 2)
                for a in range(2):
                    nc.vector.bn_stats(st[:, a, :], y[:, a, :]).then_inc(stats, 1)
                wait_apart(dve, nc, stats, 2 * s + 2, scratch)
                for a in range(2):
                    ins = nc.vector.bn_aggr(mv[:, a, :], st[:, a, :])
                ins.then_inc(mv_ready, 1)
                dve.wait_ge(rstd_ready, s + 1)
                for a in range(2):
                    ins = nc.vector.tensor_scalar(zed[:, 0, a, :], y[:, a, :], mv[:, a, 0:1], rstd[:, a:a + 1],
                                                  ALU.subtract, ALU.mult)
                ins.then_inc(zed_step, 1)
                wide = lambda v: v.unsqueeze(1).to_broadcast([P, 2, P])
                dve.wait_ge(zed_step, 3 * s + 1)
                nc.vector.tensor_tensor(zed[:, 1, :, :], zed[:, 0, :, :], wide(w("gamma")), ALU.mult).then_inc(zed_step, 1)
                dve.wait_ge(zed_step, 3 * s + 2)
                nc.vector.tensor_tensor(zed[:, 2, :, :], zed[:, 1, :, :], wide(w("beta")), ALU.add).then_inc(zed_step, 1)
                dve.wait_ge(zed_step, 3 * s + 3)
                nc.vector.tensor_tensor(res[:, u, :, :], zed[:, 2, :, :], xs, ALU.add).then_inc(res_ready, 1)
            over_slots(dve, one)


def softmax_attention(nc, X, w, c, PS, before, ones, minus_half, eps, scratch, mid):
    with ExitStack() as ctx:
        def sb(name, shape, dt=F32):
            return ctx.enter_context(nc.sbuf_tensor("s_" + name, shape, dt))

        def sem(name):
            return ctx.enter_context(nc.semaphore("s_" + name))

        qk = sb("qk", [P, P])
        st = sb("st", [P, CT, 6])
        mv = sb("mv", [P, CT, 2])
        ve = sb("ve", [P, CT])
        rstd = sb("rstd", [P, CT])
        xn = sb("xn", [P, CT, P])
        xT = sb("xT", [P, 2, SEQ])
        yT = sb("yT", [P, 2, SEQ])
        v = sb("v", [P, 2, CT, P])
        nmax = sb("nmax", [P, CT])
        total = sb("total", [P, CT])
        inverse = sb("inverse", [P, 2, CT])
        prob = sb("prob", [P, 2, SEQ])
        probT = sb("probT", [P, 2, SEQ])

        x_in = sem("x_in"); qk_psum = sem("qk_psum"); qk_ready = sem("qk_ready")
        ln = sem("ln"); ln_stats = sem("ln_stats"); ve_done = sem("ve_done"); rstd_ready = sem("rstd_ready")
        xn_ready = sem("xn_ready"); xT_psum = sem("xT_psum"); xT_ready = sem("xT_ready")
        y_psum = sem("y_psum"); y_ready = sem("y_ready"); v_psum = sem("v_psum"); v_ready = sem("v_ready")
        score_psum = sem("score_psum"); max_ready = sem("max_ready"); prob_ready = sem("prob_ready")
        pT_psum = sem("pT_psum"); pT_ready = sem("pT_ready"); out_psum = sem("out_psum")
        inv_step = sem("inv_step"); x_ready = sem("x_ready")

        block = ctx.enter_context(nc.Block())
        ident = c("ident")

        def both_stages(f, a):
            for step in f(0, 0):
                step()
            a(0, 0, f(1, 1))
            with a.engine.Fori(0, (BATCHES - 2) // 2) as i:
                for u in range(2):
                    b = i * 2 + (1 + u)
                    a(b, 1 - u, f(b + 1, u))
            a(BATCHES - 1, (BATCHES - 1) % 2, [])

        @block.sync
        def _(sp):
            for b in range(BATCHES):
                if b:
                    sp.wait_ge(x_in, 16 * b)
                sp.dma_start(X[:, b * CT:(b + 1) * CT, :],
                             mid[b * SEQ:(b + 1) * SEQ, :].rearrange("(c p) d -> p c d", p=P)).then_inc(x_in, 16)
            sp.wait_ge(x_in, 16 * BATCHES)

        @block.gpsimd
        def _(pool):
            def f(b, u):
                def rstd_step():
                    pool.wait_ge(ln_stats, b + 1)
                    nc.gpsimd.tensor_tensor(ve[:, :], mv[:, :, 1], eps[:, 0:CT], ALU.add).then_inc(ve_done, 1)
                    pool.wait_ge(ve_done, b + 1)
                    nc.gpsimd.tensor_tensor(rstd[:, :], ve[:, :], minus_half[:, :], ALU.pow).then_inc(rstd_ready, 1)
                return [rstd_step]

            def a(b, u, nxt):
                for step in nxt:
                    step()
            a.engine = pool
            both_stages(f, a)

        @block.tensor
        def _(pe):
            nc.tensor.matmul(PS[:, 1, 0:P], w("q1"), w("k1"), start=True, stop=True).then_inc(qk_psum, 1)

            def f(b, u):
                def transpose_xn():
                    pe.wait_ge(xn_ready, b + 1)
                    after_previous(pe, v_ready, b)
                    for t in range(CT):
                        mm = nc.tensor.transpose(PS[:, 0, t * P:(t + 1) * P], xn[:, t, :], ident)
                    mm.then_inc(xT_psum, 1)

                def project():
                    pe.wait_ge(xT_ready, b + 1)
                    pe.wait_ge(qk_ready, 1)
                    after_previous(pe, y_ready, b)
                    nc.tensor.matmul(PS[:, 1, :], qk[:, :], xT[:, u, :], start=True, stop=True).then_inc(y_psum, 1)
                    for t in range(CT):
                        mm = nc.tensor.matmul(PS[:, 0, t * P:(t + 1) * P], xT[:, u, t * P:(t + 1) * P], w("v1"),
                                              start=True, stop=True)
                    mm.then_inc(v_psum, 1)
                return [transpose_xn, project]

            def a(b, u, nxt):
                nxt = list(nxt)

                def score(t):
                    pe.wait_ge(y_ready, b + 1)
                    if t >= 2:
                        pe.wait_ge(prob_ready, CT * b + t - 1)
                    else:
                        after_previous(pe, prob_ready, b, CT)
                    nc.tensor.matmul(PS[:, 2 + t % 2, :], yT[:, u, t * P:(t + 1) * P], xT[:, u, :],
                                     start=True, stop=True).then_inc(score_psum, 1)

                def attend(t):
                    pe.wait_ge(prob_ready, CT * b + t + 1)
                    if t >= 2:
                        pe.wait_ge(pT_ready, CT * b + t - 1)
                    else:
                        after_previous(pe, pT_ready, b, CT)
                    for m in range(CT):
                        mm = nc.tensor.transpose(PS[:, 4 + t % 2, m * P:(m + 1) * P], prob[:, t % 2, m * P:(m + 1) * P], ident)
                    mm.then_inc(pT_psum, 1)

                def weigh(t):
                    pe.wait_ge(pT_ready, CT * b + t + 1)
                    if t == 0:
                        pe.wait_ge(v_ready, b + 1)
                        after_previous(pe, x_ready, b)
                    for m in range(CT):
                        mm = nc.tensor.matmul(PS[:, 6, t * P:(t + 1) * P], probT[:, t % 2, m * P:(m + 1) * P], v[:, u, m, :],
                                              start=(m == 0), stop=(m == CT - 1))
                    mm.then_inc(out_psum, 1)

                score(0)
                score(1)
                attend(0)
                score(2)
                attend(1)
                weigh(0)
                score(3)
                if nxt:
                    nxt[0]()
                attend(2)
                weigh(1)
                if nxt:
                    nxt[1]()
                attend(3)
                weigh(2)
                weigh(3)
            a.engine = pe
            both_stages(f, a)

        @block.scalar
        def _(act):
            nc.scalar.preload_act_table(ACT.Exp)

            def f(b, u):
                def copy_x():
                    act.wait_ge(xT_psum, b + 1)
                    nc.scalar.activation(xT[:, u, :], PS[:, 0, :], ACT.Copy).then_inc(xT_ready, 1)

                def copy_v():
                    act.wait_ge(v_psum, b + 1)
                    nc.scalar.activation(v[:, u, :, :].rearrange("p c d -> p (c d)"), PS[:, 0, :], ACT.Copy).then_inc(v_ready, 1)
                return [copy_x, copy_v]

            def a(b, u, nxt):
                for t in range(CT):
                    act.wait_ge(max_ready, CT * b + t + 1)
                    if t >= 2:
                        act.wait_ge(pT_psum, CT * b + t - 1)
                    elif not (isinstance(b, int) and b == 0):
                        act.wait_ge(inv_step, 2 * b)
                    nc.scalar.activation(prob[:, t % 2, :], PS[:, 2 + t % 2, :], ACT.Exp, bias=nmax[:, t:t + 1],
                                         accum_out=total[:, t:t + 1]).then_inc(prob_ready, 1)
                    if nxt and t >= 2:
                        nxt[t - 2]()
            a.engine = act
            both_stages(f, a)

        @block.vector
        def _(dve):
            dve.wait_ge(qk_psum, 1)
            nc.vector.tensor_copy(qk[:, :], PS[:, 1, 0:P]).then_inc(qk_ready, 1)

            def f(b, u):
                def stats():
                    dve.wait_ge(x_in, 16 * b + 16)
                    for t in range(CT):
                        nc.vector.bn_stats(st[:, t, :], X[:, bass.ds(b * CT + t, 1), :].rearrange("p o d -> p (o d)")).then_inc(ln, 1)
                    wait_apart(dve, nc, ln, CT * b + CT, scratch)
                    for t in range(CT):
                        ins = nc.vector.bn_aggr(mv[:, t, :], st[:, t, :])
                    ins.then_inc(ln_stats, 1)

                def normalise():
                    dve.wait_ge(rstd_ready, b + 1)
                    for t in range(CT):
                        xt = X[:, bass.ds(b * CT + t, 1), :].rearrange("p o d -> p (o d)")
                        ins = nc.vector.tensor_scalar(xn[:, t, :], xt, mv[:, t, 0:1], rstd[:, t:t + 1],
                                                      ALU.subtract, ALU.mult)
                    ins.then_inc(xn_ready, 1)

                def copy_y():
                    dve.wait_ge(y_psum, b + 1)
                    nc.vector.tensor_copy(yT[:, u, :], PS[:, 1, :]).then_inc(y_ready, 1)
                return [stats, normalise, copy_y]

            def a(b, u, nxt):
                nxt = list(nxt)

                def turn():
                    if nxt:
                        nxt.pop(0)()

                def largest(t):
                    dve.wait_ge(score_psum, CT * b + t + 1)
                    nc.vector.tensor_reduce(nmax[:, t:t + 1], PS[:, 2 + t % 2, :], AX.X, ALU.max,
                                            negate=True).then_inc(max_ready, 1)

                def copy_p(t):
                    dve.wait_ge(pT_psum, CT * b + t + 1)
                    if t >= 2:
                        dve.wait_ge(out_psum, CT * b + t - 1)
                    nc.vector.tensor_copy(probT[:, t % 2, :], PS[:, 4 + t % 2, :]).then_inc(pT_ready, 1)
                largest(0)
                largest(1)
                turn()
                copy_p(0)
                largest(2)
                turn()
                copy_p(1)
                largest(3)
                copy_p(2)
                turn()
                copy_p(3)
                dve.wait_ge(prob_ready, CT * b + CT)
                nc.vector.reciprocal(inverse[:, 0, :], total[:, :]).then_inc(inv_step, 1)
                dve.wait_ge(inv_step, 2 * b + 1)
                nc.vector.tensor_scalar(inverse[:, 1, :], inverse[:, 0, :], float(P) ** -0.5, None, ALU.mult).then_inc(inv_step, 1)
                dve.wait_ge(inv_step, 2 * b + 2)
                dve.wait_ge(out_psum, CT * b + CT)
                for t in range(CT):
                    xt = X[:, bass.ds(b * CT + t, 1), :].rearrange("p o d -> p (o d)")
                    ins = nc.vector.scalar_tensor_tensor(xt, PS[:, 6, t * P:(t + 1) * P], inverse[:, 1, t:t + 1], xt,
                                                         ALU.mult, ALU.add)
                ins.then_inc(x_ready, 1)
            a.engine = dve
            both_stages(f, a)



def _constants():
    t = {}
    p = np.arange(P)
    t["ident"] = np.eye(P)
    inv_freq = (np.float32(1.0) / np.power(np.float32(10000.0), np.arange(0, HD, 2, dtype=np.float32) / np.float32(HD))).astype(np.float32)
    theta = np.arange(SEQ, dtype=np.float32)[None, :] * inv_freq[(p % HD) // 2][:, None]
    t["cos"] = np.cos(theta)
    t["sin"] = np.sin(theta) * np.where(p % 2 == 0, -1.0, 1.0)[:, None]
    t["tri"] = p[:, None] <= p[None, :]
    t["before"] = p[:, None] < p[None, :]
    t["block"] = p[:, None] // HD == p[None, :] // HD
    t["group"] = (p[:, None] % 32) // HD == np.arange(4)[None, :]
    t["heads"] = p[:, None] // HD == np.arange(HEADS)[None, :]
    sel = np.zeros((P, MOE, P))
    for e in range(MOE):
        sel[[e, e + MOE], e, :] = 1.0
    t["sel"] = sel.reshape(P, -1)
    t["ids"] = p[:, None] + P * np.arange(TILES)[None, :]
    t["iota"] = np.broadcast_to(np.arange(EXPERTS), (P, EXPERTS))
    t["region"] = np.broadcast_to(REGION * np.arange(EXPERTS), (P, EXPERTS))
    t["slots"] = np.broadcast_to(np.arange(NSLOT), (P, NSLOT))
    return np.concatenate([np.asarray(t[n], np.float32) for n in CCOLS], axis=1)


def _layout(i):
    qkv = i["L0_attn_w_qkv"]
    swap = np.arange(P) ^ 1
    col = lambda a: a.reshape(-1, 1)
    rows = lambda a: np.broadcast_to(a, (P, a.shape[-1]))
    t = {
        "pw": i["L0_attn_w_pw"].T, "q": qkv[:P].T, "qs": qkv[:P][swap].T, "k": qkv[P:2 * P].T,
        "ks": qkv[P:2 * P][swap].T, "v": qkv[2 * P:].T, "o": i["L0_attn_w_o"].T, "gate": i["L0_attn_w_gate"].T,
        "moe_gate": i["L0_attn_w_moe_gate"].T, "dw": i["L0_attn_w_dw"], "b_gate": col(i["L0_attn_b_gate"]),
        "ln_g": col(i["L0_attn_ln_g"]), "ln_b": col(i["L0_attn_ln_b"]),
        "b1": i["L0_attn_b1"].reshape(MOE * MOE_CHUNKS, P).T, "b2": i["L0_attn_b2"].T,
        "router0": i["L0_ffn_gate_w"].T, "q1": i["L1_attn_Wq"], "k1": i["L1_attn_Wk"], "v1": i["L1_attn_Wv"].T,
        "router1": i["L1_ffn_wr"], "br1": rows(i["L1_ffn_br"]),
        "gamma": rows(i["L0_ffn_ln_gamma"]), "beta": rows(i["L0_ffn_ln_beta"]),
    }
    wsmall = np.concatenate([t[n] for n in WCOLS], axis=1)
    w1t = i["L0_attn_w1"].transpose(2, 0, 1).reshape(P, MOE * 512)
    w2t = i["L0_attn_w2"].reshape(MOE, P, MOE_CHUNKS, P).transpose(3, 0, 2, 1).reshape(P, MOE * 512)

    def experts(w1, w2, *more):
        f = w2.shape[1] // P
        return np.concatenate([w1, w2.reshape(EXPERTS, f, P, P).transpose(0, 2, 1, 3).reshape(EXPERTS, P, f * P), *more], axis=2)

    b1 = i["L1_ffn_b1"].reshape(EXPERTS, 4, P).transpose(0, 2, 1)
    return {
        "x": i["L0_attn_x"], "wsmall": wsmall, "consts": _constants(), "w1t": w1t, "w2t": w2t,
        "wr0": experts(i["L0_ffn_expert_w1"], i["L0_ffn_expert_w2"]),
        "wr1": experts(i["L1_ffn_w1"], i["L1_ffn_w2"], b1), "br2": i["L1_ffn_b2"],
    }


def kernel(**inputs):
    import concourse.bacc as bacc
    from concourse.bass_utils import run_bass_kernel_spmd

    nc = bacc.Bacc("TRN2", target_bir_lowering=False, num_devices=1)
    arrays = {n: np.ascontiguousarray(a) for n, a in _layout({n: np.asarray(a) for n, a in inputs.items()}).items()}
    args = {n: nc.dram_tensor(n, a.shape, mybir.dt.from_np(a.dtype), kind="ExternalInput").ap() for n, a in arrays.items()}
    args["out"] = nc.dram_tensor("out", (TOKENS, P), F32, kind="ExternalOutput").ap()
    program(nc, **args)
    r = run_bass_kernel_spmd(nc, [arrays], core_ids=[0])
    return r.results[0]["out"].reshape(BATCHES, SEQ, P)
```

```python
from contextlib import ExitStack

import numpy as np

import concourse.bass as bass
from concourse import mybir

F32 = mybir.dt.float32
F32R = mybir.dt.float32r
BF16 = mybir.dt.bfloat16
I32 = mybir.dt.int32
U32 = mybir.dt.uint32
ALU = mybir.AluOpType
ACT = mybir.ActivationFunctionType
AX = mybir.AxisListType

P = 128
BATCHES = 16
SEQ = 512
CT = SEQ // P
TOKENS = BATCHES * SEQ
TILES = TOKENS // P
HEADS, HD = 16, 8
MOE = 4
MOE_CHUNKS = 512 // P
EXPERTS = 8
LN_EPS = 1e-5

ROW = 260
COL_X, COL_TV, COL_ID = 128, 256, 257
SLOT = 256
REGION = TOKENS + SLOT
NSLOT = 40
DEPTH = 8
SPARE = (NSLOT - TOKENS // SLOT) * SLOT
ROWS = EXPERTS * REGION + SPARE
NO_TOKEN = 9000.0

WCOLS = {}


def _columns():
    at = 0
    for name, n in [("pw", P), ("q", P), ("qs", P), ("k", P), ("ks", P), ("v", P), ("o", P), ("gate", P),
                    ("moe_gate", MOE), ("dw", 3), ("b_gate", 1), ("ln_g", 1), ("ln_b", 1),
                    ("b1", MOE * MOE_CHUNKS), ("b2", MOE), ("router0", EXPERTS),
                    ("q1", P), ("k1", P), ("v1", P), ("router1", EXPERTS), ("br1", EXPERTS),
                    ("gamma", P), ("beta", P)]:
        WCOLS[name] = (at, at + n)
        at += n
    return at


NW = _columns()
CCOLS = {}


def _const_columns():
    at = 0
    for name, n in [("ident", P), ("cos", SEQ), ("sin", SEQ), ("tri", P), ("block", P), ("group", 4),
                    ("heads", HEADS), ("sel", MOE * P), ("before", P), ("ids", TILES), ("iota", EXPERTS),
                    ("region", EXPERTS), ("slots", NSLOT)]:
        CCOLS[name] = (at, at + n)
        at += n
    return at


NCONST = _const_columns()


def program(nc, x, wsmall, consts, w1t, w2t, wr0, wr1, br2, out):
    rows_dram = [nc.dram_tensor(f"rows{i}", (ROWS, ROW), F32, kind="Internal").ap() for i in range(2)]
    mid_dram = nc.dram_tensor("mid", (TOKENS, P), F32, kind="Internal").ap()

    with ExitStack() as ctx:
        def sb(name, shape, dt=F32):
            return ctx.enter_context(nc.sbuf_tensor(name, shape, dt))

        X = sb("X", [P, TILES, P])
        W = sb("W", [P, NW])
        C = sb("C", [P, NCONST])
        before = sb("before", [P, P], BF16)
        ones = sb("ones", [P, P], BF16)
        minus_half = sb("minus_half", [P, CT])
        eps = sb("eps", [P, CT])
        scratch = sb("scratch", [P, 2])
        slot_row = sb("slot_row", [P, NSLOT], I32)
        slot_expert = sb("slot_expert", [P, NSLOT], I32)
        PS = ctx.enter_context(nc.psum_tensor("PS", [P, 8, 512], F32))

        def w(name):
            a, b = WCOLS[name]
            return W[:, a:b]

        def c(name):
            a, b = CCOLS[name]
            return C[:, a:b]

        scattered = [[ctx.enter_context(nc.semaphore(f"scattered{layer}_{u}")) for u in range(1 + layer)] for layer in range(2)]
        stored = [[ctx.enter_context(nc.semaphore(f"stored{layer}_{u}")) for u in range(DEPTH)] for layer in range(2)]
        shared = dict(nc=nc, X=X, w=w, c=c, PS=PS, before=before, ones=ones,
                      minus_half=minus_half, eps=eps, scratch=scratch)

        slots = dict(slot_row=slot_row, slot_expert=slot_expert)
        with ExitStack() as front:
            HH = front.enter_context(nc.sbuf_tensor("HH", [P, TOKENS], F32R))
            HL = front.enter_context(nc.sbuf_tensor("HL", [P, TOKENS], F32R))
            LG = front.enter_context(nc.sbuf_tensor("LG", [P, TILES * MOE], F32))
            setup(wsmall=wsmall, consts=consts, W=W, C=C, **shared)
            attention_front(x=x, HH=HH, HL=HL, LG=LG, **shared)
            clear_semaphores(nc)
            mixture(HH=HH, HL=HL, LG=LG, w1t=w1t, w2t=w2t, rows=rows_dram[0], scattered=scattered[0], **slots, **shared)
            clear_semaphores(nc)
        routed(0, rows=rows_dram[0], weights=wr0, b2=None, dest=mid_dram, stored=stored[0], **slots, **shared)
        clear_semaphores(nc)
        softmax_attention(mid=mid_dram, rows=rows_dram[1], scattered=scattered[1], **slots, **shared)
        clear_semaphores(nc)
        routed(1, rows=rows_dram[1], weights=wr1, b2=br2, dest=out, stored=stored[1], **slots, **shared)


def clear_semaphores(nc):
    nc.all_engine_barrier()
    used = sorted(nc.released_uncleared_semaphores)
    nc.gpsimd.sem_clear(range(used[0], used[-1] + 1))
    nc.all_engine_barrier()


def after_previous(eng, sem, b, per=1):
    if not (isinstance(b, int) and b == 0):
        eng.wait_ge(sem, b * per)


def wait_apart(dve, nc, sem, value, scratch):
    dve.wait_ge(sem, value)
    nc.vector.memset(scratch[:, 0:1], 0.0)


def setup(nc, wsmall, consts, W, C, X, w, c, PS, before, ones, minus_half, eps, scratch):
    with ExitStack() as ctx:
        sem = lambda n: ctx.enter_context(nc.semaphore(n))
        weights_in, consts_in, made = sem("weights_in"), sem("consts_in"), sem("made")
        block = ctx.enter_context(nc.Block())

        @block.sync
        def _(sp):
            sp.dma_start(W[:, :], wsmall).then_inc(weights_in, 16)
            sp.dma_start(C[:, :], consts).then_inc(consts_in, 16)
            sp.wait_ge(weights_in, 16)
            sp.wait_ge(consts_in, 16)

        @block.vector
        def _(dve):
            nc.vector.memset(ones[:, :], 1.0)
            nc.vector.memset(minus_half[:, :], -0.5)
            nc.vector.memset(eps[:, :], LN_EPS)
            nc.vector.memset(scratch[:, 1:2], 0.0)
            dve.wait_ge(consts_in, 16)
            nc.vector.tensor_copy(before[:, :], c("before"))
            dve.wait_ge(weights_in, 16)
            nc.vector.tensor_scalar(w("b_gate"), w("b_gate"), 0.5, None, ALU.mult)
            nc.vector.tensor_scalar(w("o"), w("o"), 0.5, None, ALU.mult).then_inc(made, 1)


def attention_front(nc, X, w, c, PS, before, ones, minus_half, eps, scratch, HH, HL, LG, x):
    with ExitStack() as ctx:
        def sb(name, shape, dt=F32):
            return ctx.enter_context(nc.sbuf_tensor(name, shape, dt))

        def sem(name):
            return ctx.enter_context(nc.semaphore("a_" + name))

        st = sb("st", [P, CT, 6])
        mv = sb("mv", [P, CT, 2])
        ve = sb("ve", [P, CT])
        rstd = sb("rstd", [P, CT])
        xn = sb("xn", [P, CT, P])
        xnT = sb("xnT", [P, SEQ + 2])
        y = sb("y", [P, 3, SEQ])
        x1T = sb("x1T", [P, 2, SEQ])
        delta = sb("delta", [P, 2, SEQ])
        rot = sb("rot", [P, 3, SEQ])
        ex = sb("ex", [P, SEQ])
        qphi = sb("qphi", [P, 2, SEQ])
        kphi = sb("kphi", [P, 2, SEQ])
        vt = sb("vt", [P, 2, CT, P])
        vm = sb("vm", [P, 2, CT, 4, P])
        ktok = sb("ktok", [P, CT - 1, P])
        km = sb("km", [P, 4, SEQ])
        kp = sb("kp", [P, SEQ])
        prod = sb("prod", [P, SEQ])
        am = sb("am", [P, 3, 4 * P])
        state = sb("state", [P, CT - 1, P])
        den = sb("den", [P, 2, CT * HEADS])
        spread = sb("spread", [P, SEQ])
        rdT = sb("rdT", [P, SEQ])
        attn = sb("attn", [P, SEQ])
        th = sb("th", [P, SEQ])
        gated = sb("gated", [P, SEQ])
        x2T = sb("x2T", [P, SEQ])
        st2 = sb("st2", [P, CT, 6])
        mv2 = sb("mv2", [P, CT, 2])
        ve2 = sb("ve2", [P, CT])
        rstd2 = sb("rstd2", [P, CT])
        z = sb("z", [P, CT, P])
        h = sb("h", [P, SEQ])
        minus_one = sb("minus_one", [P, 1])

        x_in = sem("x_in"); zeroed = sem("zeroed"); act_const = sem("act_const")
        ln1 = sem("ln1"); ln1_stats = sem("ln1_stats"); ve1_done = sem("ve1_done"); rstd1_ready = sem("rstd1_ready")
        xn_ready = sem("xn_ready"); xnT_psum = sem("xnT_psum"); xnT_ready = sem("xnT_ready")
        conv = sem("conv"); pw_psum = sem("pw_psum"); x1_ready = sem("x1_ready")
        delta_ready = sem("delta_ready")
        qk_psum = sem("qk_psum"); qk_read = sem("qk_read"); rot_step = sem("rot_step"); exp_ready = sem("exp_ready")
        phi_ready = sem("phi_ready"); v_psum = sem("v_psum"); v_ready = sem("v_ready")
        kT_psum = sem("kT_psum"); ktok_ready = sem("ktok_ready"); km_ready = sem("km_ready")
        kp_ready = sem("kp_ready"); prod_ready = sem("prod_ready")
        scores_psum = sem("scores_psum"); am_ready = sem("am_ready"); am_used = sem("am_used")
        state_psum = sem("state_psum"); state_ready = sem("state_ready")
        den_psum = sem("den_psum"); den_step = sem("den_step"); spread_ready = sem("spread_ready"); rdT_psum = sem("rdT_psum"); rdT_ready = sem("rdT_ready")
        num_psum = sem("num_psum"); attn_ready = sem("attn_ready"); gate_psum = sem("gate_psum")
        wo_psum = sem("wo_psum"); th_ready = sem("th_ready"); x2_step = sem("x2_step")
        x2_psum = sem("x2_psum"); ln2 = sem("ln2"); ln2_stats = sem("ln2_stats"); ve2_done = sem("ve2_done")
        rstd2_ready = sem("rstd2_ready"); z_ready = sem("z_ready"); zT_psum = sem("zT_psum"); h_ready = sem("h_ready")
        hh_ready = sem("hh_ready"); lg_psum = sem("lg_psum"); lg_ready = sem("lg_ready")

        block = ctx.enter_context(nc.Block())
        ident = c("ident")

        def diagonal(t, u, tile):
            base = t[:, u, tile, 0, 0:1]
            ap = [list(base.ap[0]), [P + HD, 4], [4 * HD, 4], [1, HD]]
            return bass.AP(tensor=base.tensor, offset=base.offset, ap=ap)

        def tokens(t, b):
            return t[:, bass.ds(b * CT, CT), :]

        def both_stages(f, a):
            for step in f(0, 0):
                step()
            a(0, 0, f(1, 1))
            eng = a.engine
            with eng.Fori(0, (BATCHES - 2) // 2) as i:
                for u in range(2):
                    b = i * 2 + (1 + u)
                    a(b, 1 - u, f(b + 1, u))
            a(BATCHES - 1, (BATCHES - 1) % 2, [])

        @block.sync
        def _(sp):
            for b in range(BATCHES):
                if b:
                    sp.wait_ge(x_in, 16 * b)
                sp.dma_start(X[:, b * CT:(b + 1) * CT, :], x[b].rearrange("(c p) d -> p c d", p=P)).then_inc(x_in, 16)
            sp.wait_ge(x_in, 16 * BATCHES)

        @block.gpsimd
        def _(pool):
            nc.gpsimd.memset(minus_one[:, :], -1.0).then_inc(act_const, 1)
            nc.gpsimd.memset(xnT[:, 0:2], 0.0)
            nc.gpsimd.memset(delta[:, :, 0:1], 0.0)
            nc.gpsimd.memset(vm[:, :, :, :, :], 0.0).then_inc(zeroed, 1)

            def f(b, u):
                def rstd_step():
                    pool.wait_ge(ln1_stats, b + 1)
                    nc.gpsimd.tensor_tensor(ve[:, :], mv[:, :, 1], eps[:, 0:CT], ALU.add).then_inc(ve1_done, 1)
                    pool.wait_ge(ve1_done, b + 1)
                    nc.gpsimd.tensor_tensor(rstd[:, :], ve[:, :], minus_half[:, :], ALU.pow).then_inc(rstd1_ready, 1)

                def delta_step():
                    pool.wait_ge(x1_ready, b + 1)
                    nc.gpsimd.tensor_tensor(delta[:, u, 1:], x1T[:, u, 1:], x1T[:, u, 0:SEQ - 1],
                                            ALU.subtract).then_inc(delta_ready, 1)
                return [rstd_step, delta_step]

            def a(b, u, nxt):
                pool.wait_ge(kp_ready, b + 1)
                nc.gpsimd.tensor_tensor(prod[:, :], qphi[:, u, :], kp[:, :], ALU.mult).then_inc(prod_ready, 1)
                for step in nxt:
                    step()
                pool.wait_ge(ln2_stats, b + 1)
                nc.gpsimd.tensor_tensor(ve2[:, :], mv2[:, :, 1], eps[:, 0:CT], ALU.add).then_inc(ve2_done, 1)
                pool.wait_ge(ve2_done, b + 1)
                nc.gpsimd.tensor_tensor(rstd2[:, :], ve2[:, :], minus_half[:, :], ALU.pow).then_inc(rstd2_ready, 1)
            a.engine = pool
            both_stages(f, a)

        @block.tensor
        def _(pe):
            def f(b, u):
                def transpose_xn():
                    pe.wait_ge(xn_ready, b + 1)
                    after_previous(pe, v_ready, b)
                    for t in range(CT):
                        mm = nc.tensor.transpose(PS[:, 0, t * P:(t + 1) * P], xn[:, t, :], ident)
                    mm.then_inc(xnT_psum, 1)

                def pointwise():
                    pe.wait_ge(conv, 3 * b + 3)
                    nc.tensor.matmul(PS[:, 0, :], w("pw"), y[:, 2, :], start=True, stop=True).then_inc(pw_psum, 1)

                def project(name, n):
                    pe.wait_ge(x1_ready, b + 1)
                    if n:
                        pe.wait_ge(qk_read, 2 * b + 1)
                    else:
                        after_previous(pe, qk_read, b, 2)
                    nc.tensor.matmul(PS[:, 1, :], w(name), x1T[:, u, :], start=True, stop=True)
                    nc.tensor.matmul(PS[:, 2, :], w(name + "s"), x1T[:, u, :],
                                     start=True, stop=True).then_inc(qk_psum, 1)

                def values():
                    for t in range(CT):
                        mm = nc.tensor.matmul(PS[:, 0, t * P:(t + 1) * P], x1T[:, u, t * P:(t + 1) * P],
                                              w("v"), start=True, stop=True)
                    mm.then_inc(v_psum, 1)
                return [transpose_xn, pointwise, lambda: project("q", 0), values, lambda: project("k", 1)]

            def a(b, u, nxt):
                nxt = list(nxt)

                def turn():
                    if nxt:
                        nxt.pop(0)()

                pe.wait_ge(phi_ready, 2 * b + 2)
                for t in range(CT - 1):
                    mm = nc.tensor.transpose(PS[:, 7, t * P:(t + 1) * P], kphi[:, u, t * P:(t + 1) * P], ident)
                mm.then_inc(kT_psum, 1)
                pe.wait_ge(v_ready, b + 1)
                pe.wait_ge(km_ready, b + 1)

                def scores(n):
                    t, g = divmod(n, 4)
                    if n >= 2:
                        pe.wait_ge(am_ready, 16 * b + n - 1)
                    else:
                        after_previous(pe, am_ready, b, 16)
                    for j in range(4):
                        mm = nc.tensor.matmul(PS[:, 3 + n % 2, j * P:(j + 1) * P],
                                              km[32 * g:32 * g + 32, j, t * P:(t + 1) * P],
                                              qphi[32 * g:32 * g + 32, u, t * P:(t + 1) * P], start=True, stop=True)
                    mm.then_inc(scores_psum, 1)

                def weigh(n):
                    t, g = divmod(n, 4)
                    if g == 0 and t:
                        pe.wait_ge(state_ready, 3 * b + t)
                        nc.tensor.matmul(PS[:, 5, t * P:(t + 1) * P], state[:, t - 1, :],
                                         qphi[:, u, t * P:(t + 1) * P], start=True, stop=False, skip_group_check=True)
                    pe.wait_ge(am_ready, 16 * b + n + 1)
                    for j in range(4):
                        mm = nc.tensor.matmul(PS[32 * g:32 * g + 32, 5, t * P:(t + 1) * P],
                                              vm[:, u, t, j, 32 * g:32 * g + 32],
                                              am[:, n % 3, j * P:(j + 1) * P],
                                              start=(t == 0 and j == 0), stop=(j == 3), skip_group_check=True)
                    mm.then_inc(am_used, 1)

                for n in range(16):
                    scores(n)
                    if n == 1:
                        pe.wait_ge(ktok_ready, b + 1)
                        after_previous(pe, lg_ready, b)
                    if n in (1, 5, 9):
                        t = n // 4
                        if t:
                            pe.wait_ge(state_ready, 3 * b + t)
                        nc.tensor.matmul(PS[:, 6, 0:P], ktok[:, t, :], vt[:, u, t, :], start=(t == 0), stop=True,
                                         skip_group_check=True).then_inc(state_psum, 1)
                    if n >= 1:
                        weigh(n - 1)
                    if n == 10:
                        pe.wait_ge(prod_ready, b + 1)
                        for t in range(CT):
                            mm = nc.tensor.matmul(PS[:, 7, t * HEADS:(t + 1) * HEADS], prod[:, t * P:(t + 1) * P],
                                                  c("heads"), start=True, stop=True)
                        mm.then_inc(den_psum, 1)
                    if n == 13:
                        pe.wait_ge(spread_ready, b + 1)
                        for t in range(CT):
                            mm = nc.tensor.transpose(PS[:, 7, t * P:(t + 1) * P], spread[:, t * P:(t + 1) * P], ident)
                        mm.then_inc(rdT_psum, 1)
                    if n == 14:
                        pe.wait_ge(state_ready, 3 * b + 3)
                        pe.wait_ge(delta_ready, b + 1)
                        nc.tensor.matmul(PS[:, 6, :], w("gate"), delta[:, u, :], start=True, stop=True).then_inc(gate_psum, 1)
                    if n in (4, 6, 8, 11, 12):
                        turn()
                weigh(15)
                pe.wait_ge(attn_ready, b + 1)
                pe.wait_ge(rdT_ready, b + 1)
                nc.tensor.matmul(PS[:, 7, :], w("o"), attn[:, :], start=True, stop=True).then_inc(wo_psum, 1)
                pe.wait_ge(x2_step, 2 * b + 2)
                for t in range(CT):
                    mm = nc.tensor.transpose(PS[:, 7, t * P:(t + 1) * P], x2T[:, t * P:(t + 1) * P], ident)
                mm.then_inc(x2_psum, 1)
                pe.wait_ge(z_ready, b + 1)
                pe.wait_ge(th_ready, b + 1)
                for t in range(CT):
                    mm = nc.tensor.transpose(PS[:, 6, t * P:(t + 1) * P], z[:, t, :], ident)
                mm.then_inc(zT_psum, 1)
                pe.wait_ge(h_ready, b + 1)
                for t in range(CT):
                    mm = nc.tensor.matmul(PS[:, 6, t * MOE:(t + 1) * MOE], h[:, t * P:(t + 1) * P], w("moe_gate"),
                                          start=True, stop=True)
                mm.then_inc(lg_psum, 1)
            a.engine = pe
            both_stages(f, a)

        @block.scalar
        def _(act):
            nc.scalar.preload_act_table(ACT.Exp)
            act.wait_ge(act_const, 1)
            act.wait_ge(zeroed, 1)

            def f(b, u):
                def copy_xnT():
                    act.wait_ge(xnT_psum, b + 1)
                    after_previous(act, x1_ready, b)
                    nc.scalar.activation(xnT[:, 2:], PS[:, 0, :], ACT.Copy).then_inc(xnT_ready, 1)
                    act.wait_ge(xnT_ready, b + 1)
                    nc.scalar.activation(y[:, 0, :], xnT[:, 0:SEQ], ACT.Copy, scale=w("dw")[:, 0:1]).then_inc(conv, 1)

                def copy_v():
                    act.wait_ge(v_psum, b + 1)
                    if not isinstance(b, int) or b >= 2:
                        act.wait_ge(am_used, 16 * (b - 1))
                    nc.scalar.activation(vt[:, u, :, :].rearrange("p c d -> p (c d)"), PS[:, 0, :], ACT.Copy)
                    for t in range(CT):
                        src = PS[:, 0, t * P:(t + 1) * P].rearrange("p (g j m) -> p j g m", j=4, m=HD)
                        ins = nc.scalar.activation(diagonal(vm, u, t), src, ACT.Copy)
                    ins.then_inc(v_ready, 1)

                def exps(n):
                    act.wait_ge(rot_step, 6 * b + 3 * n + 3)
                    nc.scalar.activation(ex[:, :], rot[:, 2, :], ACT.Exp, bias=minus_one[:, 0:1]).then_inc(exp_ready, 1)
                return [copy_xnT, lambda: exps(0), copy_v, lambda: exps(1)]

            def a(b, u, nxt):
                nxt = list(nxt)

                def turn():
                    if nxt:
                        nxt.pop(0)()
                act.wait_ge(kT_psum, b + 1)
                nc.scalar.activation(ktok[:, :, :].rearrange("p c d -> p (c d)"), PS[:, 7, 0:(CT - 1) * P],
                                     ACT.Copy).then_inc(ktok_ready, 1)
                turn()
                turn()
                turn()
                turn()
                act.wait_ge(den_step, 2 * b + 2)
                nc.scalar.activation(spread[:, :].rearrange("p (h m) -> p h m", m=HD),
                                     den[:, 1, :].unsqueeze(2).to_broadcast([P, CT * HEADS, HD]),
                                     ACT.Copy).then_inc(spread_ready, 1)
                act.wait_ge(rdT_psum, b + 1)
                nc.scalar.activation(rdT[:, :], PS[:, 7, :], ACT.Copy).then_inc(rdT_ready, 1)
                act.wait_ge(gate_psum, b + 1)
                nc.scalar.activation(th[:, :], PS[:, 6, :], ACT.Tanh, bias=w("b_gate"), scale=0.5).then_inc(th_ready, 1)
                act.wait_ge(zT_psum, b + 1)
                after_previous(act, hh_ready, b, 2)
                nc.scalar.activation(h[:, :], PS[:, 6, :], ACT.Identity, bias=w("ln_b"), scale=w("ln_g")).then_inc(h_ready, 1)
                act.wait_ge(lg_psum, b + 1)
                nc.scalar.activation(LG[:, bass.ds(b * (CT * MOE), CT * MOE)], PS[:, 6, 0:CT * MOE],
                                     ACT.Copy).then_inc(lg_ready, 1)
            a.engine = act
            both_stages(f, a)

        @block.vector
        def _(dve):
            def f(b, u):
                def stats():
                    dve.wait_ge(x_in, 16 * b + 16)
                    for t in range(CT):
                        xt = X[:, bass.ds(b * CT + t, 1), :].rearrange("p o d -> p (o d)")
                        nc.vector.bn_stats(st[:, t, :], xt).then_inc(ln1, 1)
                    wait_apart(dve, nc, ln1, CT * b + CT, scratch)
                    for t in range(CT):
                        ins = nc.vector.bn_aggr(mv[:, t, :], st[:, t, :])
                    ins.then_inc(ln1_stats, 1)

                def normalise():
                    dve.wait_ge(rstd1_ready, b + 1)
                    for t in range(CT):
                        xt = X[:, bass.ds(b * CT + t, 1), :].rearrange("p o d -> p (o d)")
                        ins = nc.vector.tensor_scalar(xn[:, t, :], xt, mv[:, t, 0:1], rstd[:, t:t + 1],
                                                      ALU.subtract, ALU.mult)
                    ins.then_inc(xn_ready, 1)

                def convolve():
                    for k in (1, 2):
                        dve.wait_ge(conv, 3 * b + k)
                        nc.vector.scalar_tensor_tensor(y[:, k, :], xnT[:, k:k + SEQ], w("dw")[:, k:k + 1],
                                                       y[:, k - 1, :], ALU.mult, ALU.add).then_inc(conv, 1)

                def residual():
                    dve.wait_ge(pw_psum, b + 1)
                    nc.vector.tensor_tensor(x1T[:, u, :], PS[:, 0, :], xnT[:, 2:], ALU.add).then_inc(x1_ready, 1)

                def rotate(n, dst):
                    dve.wait_ge(qk_psum, 2 * b + n + 1)
                    nc.vector.tensor_tensor(rot[:, 0, :], PS[:, 1, :], c("cos"), ALU.mult).then_inc(rot_step, 1)
                    nc.vector.tensor_tensor(rot[:, 1, :], PS[:, 2, :], c("sin"), ALU.mult).then_inc(qk_read, 1)
                    dve.wait_ge(rot_step, 6 * b + 3 * n + 1)
                    dve.wait_ge(qk_read, 2 * b + n + 1)
                    nc.vector.scalar_tensor_tensor(rot[:, 2, :], rot[:, 0, :], 1.0, rot[:, 1, :],
                                                   ALU.add, ALU.add).then_inc(rot_step, 2)

                def phi(n, dst):
                    dve.wait_ge(exp_ready, 2 * b + n + 1)
                    nc.vector.scalar_tensor_tensor(dst[:, u, :], ex[:, :], 1.0, rot[:, 2, :], ALU.min,
                                                   ALU.max).then_inc(phi_ready, 1)
                return [stats, normalise, convolve, residual, lambda: rotate(0, qphi), lambda: phi(0, qphi),
                        lambda: rotate(1, kphi), lambda: phi(1, kphi)]

            def a(b, u, nxt):
                nxt = list(nxt)

                def turn():
                    if nxt:
                        nxt.pop(0)()
                dve.wait_ge(phi_ready, 2 * b + 2)
                after_previous(dve, am_used, b, 16)
                for j in range(4):
                    ins = nc.vector.tensor_scalar(km[:, j, :], kphi[:, u, :], c("group")[:, j:j + 1], None, ALU.mult)
                ins.then_inc(km_ready, 1)
                nc.vector.tensor_tensor_scan(kp[:, :], kphi[:, u, :], kphi[:, u, :], 0.0,
                                             ALU.add, ALU.max).then_inc(kp_ready, 1)
                for n in range(16):
                    if n in (2, 6, 10):
                        t = n // 4
                        dve.wait_ge(state_psum, 3 * b + t + 1)
                        nc.vector.tensor_tensor(state[:, t, :], PS[:, 6, 0:P], c("block"), ALU.mult).then_inc(state_ready, 1)
                    if n == 12:
                        dve.wait_ge(den_psum, b + 1)
                        nc.vector.tensor_scalar(den[:, 0, :], PS[:, 7, 0:CT * HEADS], 1e-6, None, ALU.add).then_inc(den_step, 1)
                        dve.wait_ge(den_step, 2 * b + 1)
                        nc.vector.reciprocal(den[:, 1, :], den[:, 0, :]).then_inc(den_step, 1)
                    dve.wait_ge(scores_psum, 16 * b + n + 1)
                    if n >= 3:
                        dve.wait_ge(am_used, 16 * b + n - 2)
                    nc.vector.tensor_tensor(am[:, n % 3, :].rearrange("p (j q) -> p j q", j=4),
                                            PS[:, 3 + n % 2, :].rearrange("p (j q) -> p j q", j=4),
                                            c("tri").unsqueeze(1).to_broadcast([P, 4, P]), ALU.mult).then_inc(am_ready, 1)
                    if n in (1, 3, 5, 7, 9, 11, 13, 14):
                        turn()
                dve.wait_ge(am_used, 16 * b + 16)
                dve.wait_ge(rdT_ready, b + 1)
                nc.vector.tensor_tensor(attn[:, :], PS[:, 5, :], rdT[:, :], ALU.mult).then_inc(attn_ready, 1)
                dve.wait_ge(wo_psum, b + 1)
                dve.wait_ge(th_ready, b + 1)
                nc.vector.scalar_tensor_tensor(gated[:, :], th[:, :], 1.0, PS[:, 7, :], ALU.add, ALU.mult).then_inc(x2_step, 1)
                dve.wait_ge(x2_step, 2 * b + 1)
                nc.vector.tensor_tensor(x2T[:, :], gated[:, :], x1T[:, u, :], ALU.add).then_inc(x2_step, 1)
                dve.wait_ge(x2_psum, b + 1)
                for t in range(CT):
                    nc.vector.bn_stats(st2[:, t, :], PS[:, 7, t * P:(t + 1) * P]).then_inc(ln2, 1)
                wait_apart(dve, nc, ln2, CT * b + CT, scratch)
                for t in range(CT):
                    ins = nc.vector.bn_aggr(mv2[:, t, :], st2[:, t, :])
                ins.then_inc(ln2_stats, 1)
                nc.vector.tensor_tensor(tokens(X, b), tokens(X, b), PS[:, 7, :].rearrange("p (c d) -> p c d", c=CT),
                                        ALU.add)
                dve.wait_ge(rstd2_ready, b + 1)
                for t in range(CT):
                    ins = nc.vector.tensor_scalar(z[:, t, :], PS[:, 7, t * P:(t + 1) * P], mv2[:, t, 0:1],
                                                  rstd2[:, t:t + 1], ALU.subtract, ALU.mult)
                ins.then_inc(z_ready, 1)
                dve.wait_ge(h_ready, b + 1)
                nc.vector.tensor_copy(HH[:, bass.ds(b * SEQ, SEQ)], h[:, :]).then_inc(hh_ready, 1)
                dve.wait_ge(hh_ready, 2 * b + 1)
                nc.vector.tensor_tensor(HL[:, bass.ds(b * SEQ, SEQ)], h[:, :],
                                        HH[:, bass.ds(b * SEQ, SEQ)].bitcast(F32), ALU.subtract).then_inc(hh_ready, 1)
            a.engine = dve
            both_stages(f, a)


def mixture(nc, X, w, c, PS, before, ones, minus_half, eps, scratch, HH, HL, LG, w1t, w2t, rows, slot_row, slot_expert, scattered):
    with ExitStack() as ctx:
        def sb(name, shape, dt=F32):
            return ctx.enter_context(nc.sbuf_tensor("m_" + name, shape, dt))

        def sem(name):
            return ctx.enter_context(nc.semaphore("m_" + name))

        FF = MOE * 512
        raw1 = sb("raw1", [P, FF])
        raw2 = sb("raw2", [P, FF])
        w1h, w1l, w2h, w2l = (sb(n, [P, FF], F32R) for n in ("w1h", "w1l", "w2h", "w2l"))
        gate = sb("gate", [P, TILES, MOE])
        top = sb("top", [P, TILES])
        total = sb("total", [P, TILES])
        gparts = sb("gparts", [P, TILES, 2 * MOE])
        gp = sb("gp", [P, CT * 2 * MOE])
        gT = sb("gT", [2 * MOE, SEQ], F32R)
        selr = sb("selr", [2 * MOE, MOE * P], F32R)
        gb = raw2[:, 0:2 * SEQ].rearrange("p (u t) -> p u t", u=2)
        S = sb("S", [P, 3, SEQ])
        Sh = sb("Sh", [P, 4, SEQ], F32R)
        Sl = sb("Sl", [P, 4, SEQ], F32R)
        oe = raw2[:, 2 * SEQ:4 * SEQ].rearrange("p (u t) -> p u t", u=2)

        w1_in = sem("w1_in"); w2_in = sem("w2_in"); w_split = sem("w_split")
        gate_step = sem("gate_step"); exp_done = sem("exp_done"); gates_ready = sem("gates_ready")
        gp_ready = sem("gp_ready"); gT_psum = sem("gT_psum"); gT_ready = sem("gT_ready")
        gb_psum = sem("gb_psum"); gb_ready = sem("gb_ready")
        h_psum = sem("h_psum"); s_ready = sem("s_ready"); sh_ready = sem("sh_ready"); sl_ready = sem("sl_ready")
        s_used = sem("s_used"); out_psum = sem("out_psum"); oe_ready = sem("oe_ready"); back_psum = sem("back_psum")
        oe_used = sem("oe_used"); x_ready = sem("x_ready")

        block = ctx.enter_context(nc.Block())
        ident = c("ident")
        N = MOE * MOE_CHUNKS
        routing = Routing(0, ctx, nc, X, w, c, PS, before, ones, minus_half, eps, scratch, rows, slot_row, slot_expert,
                          bank=5, scattered=scattered, x_ready=x_ready)

        SPREAD = (3, 6, 9, 13)

        def over_batches(eng, one):
            one(0, None, None)
            one(1, 0, None)
            one(2, 1, 0)
            with eng.Fori(3, BATCHES) as b:
                one(b, b + (-1), b + (-2))
            one(None, BATCHES - 1, BATCHES - 2)
            one(None, None, BATCHES - 1)

        def two_before(eng, sem, b, e):
            if e >= 2 or not isinstance(b, int) or b:
                eng.wait_ge(sem, MOE * b + (e - 1))

        def route(step, eng, b):
            if b is not None:
                step(eng, b, 0, b)

        def chunk(b, p, n, lag):
            b, n = (b, n - lag) if n >= lag else (p, n - lag + N)
            return None if b is None else (b, n)

        @block.sync
        def _(sp):
            sp.dma_start(raw1[:, :], w1t).then_inc(w1_in, 16)
            sp.dma_start(raw2[:, :], w2t).then_inc(w2_in, 16)
            routing.sp_padding(sp)

        @block.gpsimd
        def _(pool):
            routing.pool_begin(pool)

            def one(b, p, r):
                route(routing.pool_scatter, pool, r)
                route(routing.pool_inverse_deviation, pool, p)
                route(routing.pool_exp, pool, p)
            over_batches(pool, one)
            routing.pool_end(pool)

        @block.tensor
        def _(pe):
            pe.wait_ge(w_split, 3)

            def up(b, n):
                if n >= 3:
                    pe.wait_ge(s_ready, N * b + n - 2)
                else:
                    after_previous(pe, s_ready, b, N)
                tok = bass.ds(b * SEQ, SEQ)
                bank = PS[:, n % 3, :]
                f = slice(n * P, (n + 1) * P)
                nc.tensor.matmul(bank, w1h[:, f], HH[:, tok], start=True, stop=False)
                nc.tensor.matmul(bank, w1h[:, f], HL[:, tok], start=False, stop=False)
                nc.tensor.matmul(bank, w1l[:, f], HH[:, tok], start=False, stop=True).then_inc(h_psum, 1)

            def down(b, n):
                e, k = divmod(n, MOE_CHUNKS)
                bank = PS[:, 3 + e % 2, :]
                if k == 0:
                    two_before(pe, oe_ready, b, e)
                f = slice(n * P, (n + 1) * P)
                pe.wait_ge(sh_ready, N * b + n + 1)
                nc.tensor.matmul(bank, w2h[:, f], Sh[:, n % 4, :], start=(k == 0), stop=False)
                nc.tensor.matmul(bank, w2l[:, f], Sh[:, n % 4, :], start=False, stop=False)
                pe.wait_ge(sl_ready, N * b + n + 1)
                last = nc.tensor.matmul(bank, w2h[:, f], Sl[:, n % 4, :], start=False, stop=(k == MOE_CHUNKS - 1))
                if k == MOE_CHUNKS - 1:
                    last.then_inc(out_psum, 1)
                else:
                    last.then_inc(s_used, 1)

            def back(b, e):
                pe.wait_ge(oe_ready, MOE * b + e + 1)
                if e == 0:
                    after_previous(pe, x_ready, b)
                for t in range(CT):
                    mm = nc.tensor.matmul(PS[:, 7, t * P:(t + 1) * P], oe[:, e % 2, t * P:(t + 1) * P], ident,
                                          is_transpose=True, start=(e == 0 and t == 0), stop=(e == MOE - 1),
                                          skip_group_check=True)
                mm.then_inc(back_psum, 1)

            def gates(b):
                pe.wait_ge(gp_ready, b + 1)
                after_previous(pe, gb_ready, b, MOE)
                for t in range(CT):
                    mm = nc.tensor.transpose(PS[0:2 * MOE, 6, t * P:(t + 1) * P],
                                             gp[:, t * 2 * MOE:(t + 1) * 2 * MOE], ident)
                mm.then_inc(gT_psum, 1)

            def spread(b, e):
                pe.wait_ge(gT_ready, b + 1)
                if e:
                    pe.wait_ge(gb_ready, MOE * b + e)
                nc.tensor.matmul(PS[:, 6, :], selr[:, e * P:(e + 1) * P], gT[:, :], start=True,
                                 stop=True).then_inc(gb_psum, 1)

            beside = {11: routing.pe_turn, 13: routing.pe_scores}

            def one(b, p, r):
                for n in range(N):
                    if n == 1:
                        route(routing.pe_count, pe, r)
                    if b is not None:
                        up(b, n)
                        if n == 1:
                            if isinstance(b, int) and b == 0:
                                pe.wait_ge(w_split, 5)
                            gates(b)
                        if n in SPREAD:
                            spread(b, SPREAD.index(n))
                    lagging = chunk(b, p, n, 3)
                    if lagging:
                        down(*lagging)
                    if n % 4 == 1:
                        lagging = chunk(b, p, n, 9)
                        if lagging:
                            back(lagging[0], lagging[1] // 4)
                    if n in beside:
                        route(beside[n], pe, p)
            over_batches(pe, one)

        @block.scalar
        def _(act):
            nc.scalar.preload_act_table(ACT.Exp)
            act.wait_ge(gate_step, 2)
            nc.scalar.activation(gate[:, :, :], gate[:, :, :], ACT.Exp).then_inc(exp_done, 1)
            nc.scalar.preload_act_table(ACT.Silu)

            def wait_used(b, n):
                e, k = divmod(n, MOE_CHUNKS)
                if k == MOE_CHUNKS - 1:
                    act.wait_ge(out_psum, MOE * b + e + 1)
                else:
                    act.wait_ge(s_used, (N - MOE) * b + e * (MOE_CHUNKS - 1) + k + 1)

            def hidden(b, p, n):
                act.wait_ge(h_psum, N * b + n + 1)
                held = chunk(b, p, n, 4)
                if held:
                    wait_used(*held)
                nc.scalar.activation(Sh[:, n % 4, :], PS[:, n % 3, :], ACT.Silu, bias=w("b1")[:, n:n + 1]).then_inc(sh_ready, 1)
                if n >= 3:
                    act.wait_ge(sl_ready, N * b + n - 2)
                else:
                    after_previous(act, sl_ready, b, N)
                nc.scalar.activation(S[:, n % 3, :], PS[:, n % 3, :], ACT.Silu, bias=w("b1")[:, n:n + 1]).then_inc(s_ready, 1)

            def one(b, p, r):
                for n in range(N):
                    if n == 12:
                        route(routing.act_copy, act, p)
                    if b is None:
                        continue
                    hidden(b, p, n)
                    if n == 2:
                        act.wait_ge(gT_psum, b + 1)
                        nc.scalar.activation(gT[:, :], PS[0:2 * MOE, 6, :], ACT.Copy).then_inc(gT_ready, 1)
                    if n - 1 in SPREAD:
                        e = SPREAD.index(n - 1)
                        act.wait_ge(gb_psum, MOE * b + e + 1)
                        two_before(act, oe_ready, b, e)
                        nc.scalar.activation(gb[:, e % 2, :], PS[:, 6, :], ACT.Copy).then_inc(gb_ready, 1)
            over_batches(act, one)

        @block.vector
        def _(dve):
            nc.vector.tensor_copy(selr[:, :], c("sel")[0:2 * MOE, :]).then_inc(w_split, 1)
            lg = LG[:, :].rearrange("p (t e) -> p t e", e=MOE)
            wide = lambda a: a.unsqueeze(2).to_broadcast([P, TILES, MOE])
            nc.vector.tensor_reduce(top[:, :], lg, AX.X, ALU.max).then_inc(gate_step, 1)
            dve.wait_ge(gate_step, 1)
            nc.vector.tensor_tensor(gate[:, :, :], lg, wide(top[:, :]), ALU.subtract).then_inc(gate_step, 1)
            dve.wait_ge(exp_done, 1)
            nc.vector.tensor_reduce(total[:, :], gate[:, :, :], AX.X, ALU.add).then_inc(gate_step, 1)
            dve.wait_ge(gate_step, 3)
            nc.vector.reciprocal(top[:, :], total[:, :]).then_inc(gate_step, 1)
            dve.wait_ge(gate_step, 4)
            nc.vector.tensor_tensor(gate[:, :, :], gate[:, :, :], wide(top[:, :]), ALU.mult).then_inc(gate_step, 1)
            dve.wait_ge(gate_step, 5)
            nc.vector.tensor_copy(gparts[:, :, 0:MOE].bitcast(F32R), gate[:, :, :]).then_inc(gate_step, 1)
            dve.wait_ge(gate_step, 6)
            nc.vector.tensor_tensor(gparts[:, :, MOE:], gate[:, :, :], gparts[:, :, 0:MOE], ALU.subtract).then_inc(gates_ready, 1)
            for k, (raw, hi, lo, arrived) in enumerate([(raw1, w1h, w1l, w1_in), (raw2, w2h, w2l, w2_in)]):
                dve.wait_ge(arrived, 16)
                nc.vector.tensor_copy(hi[:, :], raw[:, :]).then_inc(w_split, 1)
                dve.wait_ge(w_split, 2 * k + 2)
                nc.vector.tensor_tensor(lo[:, :], raw[:, :], hi[:, :].bitcast(F32), ALU.subtract).then_inc(w_split, 1)
            dve.wait_ge(gates_ready, 1)
            routing.dve_begin(dve)
            beside = {7: routing.dve_statistics, 9: routing.dve_normalise, 15: routing.dve_pick}

            def gated(b, e):
                dve.wait_ge(out_psum, MOE * b + e + 1)
                dve.wait_ge(gb_ready, MOE * b + e + 1)
                two_before(dve, back_psum, b, e)
                nc.vector.scalar_tensor_tensor(oe[:, e % 2, :], PS[:, 3 + e % 2, :], w("b2")[:, e:e + 1],
                                               gb[:, e % 2, :], ALU.add, ALU.mult).then_inc(oe_ready, 1)

            def one(b, p, r):
                for n in range(N):
                    if n == 3:
                        route(routing.dve_place, dve, r)
                        route(routing.dve_gate, dve, r)
                    if n == 7 and p is not None:
                        dve.wait_ge(back_psum, MOE * p + MOE)
                        xb = X[:, bass.ds(p * CT, CT), :]
                        nc.vector.tensor_tensor(xb, xb, PS[:, 7, :].rearrange("p (c d) -> p c d", c=CT), ALU.add).then_inc(x_ready, 1)
                    if n in beside:
                        route(beside[n], dve, p)
                    if b is not None:
                        if n == 0:
                            after_previous(dve, gT_psum, b)
                            nc.vector.tensor_copy(gp[:, :].rearrange("p (t e) -> p t e", t=CT),
                                                  gparts[:, bass.ds(b * CT, CT), :]).then_inc(gp_ready, 1)
                        dve.wait_ge(sh_ready, N * b + n + 1)
                        dve.wait_ge(s_ready, N * b + n + 1)
                        nc.vector.tensor_tensor(Sl[:, n % 4, :], S[:, n % 3, :], Sh[:, n % 4, :].bitcast(F32),
                                                ALU.subtract).then_inc(sl_ready, 1)
                    if n % 4 == 3:
                        lagging = chunk(b, p, n, 7)
                        if lagging:
                            gated(lagging[0], lagging[1] // 4)
            over_batches(dve, one)
            routing.dve_end(dve)


class Routing:

    def __init__(self, layer, ctx, nc, X, w, c, PS, before, ones, minus_half, eps, scratch, rows, slot_row, slot_expert,
                 bank, scattered, x_ready):
        self.layer, self.nc, self.X, self.c, self.before, self.ones = layer, nc, X, c, before, ones
        self.minus_half, self.eps, self.scratch, self.rows = minus_half, eps, scratch, rows
        self.slot_row, self.slot_expert, self.x_ready = slot_row, slot_expert, x_ready
        self.buffers = buffers = len(scattered)
        self.router = w(f"router{layer}")
        self.bias = w("br1")
        self.bank = PS[:, bank, :]

        def sb(name, shape, dt=F32):
            return ctx.enter_context(nc.sbuf_tensor(f"r{layer}_" + name, shape, dt))

        def sem(name):
            return ctx.enter_context(nc.semaphore(f"r{layer}_" + name))

        self.st = sb("st", [P, CT, 6])
        self.mv = sb("mv", [P, CT, 2])
        self.ve = sb("ve", [P, CT])
        self.rstd = sb("rstd", [P, CT])
        self.row = sb("row", [P, buffers, CT, ROW])
        self.xT = sb("xT", [P, SEQ])
        self.lg = sb("lg", [P, CT, EXPERTS])
        self.top = sb("top", [P, CT, 8])
        self.at = sb("at", [P, CT, 8], U32)
        self.first = sb("first", [P, CT])
        self.hot = sb("hot", [P, CT, EXPERTS], BF16)
        self.hot32 = sb("hot32", [P, CT, EXPERTS])
        self.soft = sb("soft", [P, 2, CT, EXPERTS])
        self.small = sb("small", [P, 4, CT])
        self.euler = sb("euler", [P, CT, EXPERTS])
        self.base = sb("base", [P, EXPERTS])
        self.place = sb("place", [P, 2, CT, EXPERTS])
        self.pos = sb("pos", [P, CT])
        self.posi = sb("posi", [P, buffers, CT], I32)
        self.padding = sb("padding", [P, 2, ROW])
        self.told = sb("told", [P, CT])
        self.got = sb("got", [P, EXPERTS])
        self.tiles = sb("tiles", [P, EXPERTS])
        self.ends = sb("ends", [P, EXPERTS])
        self.jump = sb("jump", [P, EXPERTS])
        self.slot_at = sb("slot_at", [P, NSLOT])
        self.number = sb("number", [P, NSLOT])
        self.skipped = sb("skipped", [P, NSLOT])
        self.over = sb("over", [P, EXPERTS, NSLOT])
        self.passed = sb("passed", [P, NSLOT, EXPERTS])
        self.padi = sb("padi", [P, EXPERTS], I32)

        self.cleared = sem("cleared")
        self.ln = sem("ln")
        self.ln_stats = sem("ln_stats")
        self.ve_done = sem("ve_done")
        self.rstd_ready = sem("rstd_ready")
        self.xn_ready = sem("xn_ready")
        self.x_copied = sem("x_copied")
        self.xT_psum = sem("xT_psum")
        self.xT_ready = sem("xT_ready")
        self.lg_psum = sem("lg_psum")
        self.lg_ready = sem("lg_ready")
        self.pick = sem("pick")
        self.hot_ready = sem("hot_ready")
        self.count_psum = sem("count_psum")
        self.place_step = sem("place_step")
        self.pos_ready = sem("pos_ready")
        self.soft_ready = sem("soft_ready")
        self.exp_ready = sem("exp_ready")
        self.gate_step = sem("gate_step")
        self.tv_ready = sem("tv_ready")
        self.scattered = scattered
        self.told_done = sem("told_done")
        self.ends_ready = sem("ends_ready")
        self.padded = sem("padded")
        self.table = sem("table")


    def dve_begin(self, dve):
        nc = self.nc
        nc.vector.tensor_copy(self.base[:, :], self.c("region")).then_inc(self.place_step, 1)
        nc.vector.memset(self.row[:, :, :, COL_TV:ROW], 0.0).then_inc(self.place_step, 1)
        dve.wait_ge(self.place_step, 2)

    def dve_statistics(self, dve, b, u, turn):
        nc = self.nc
        wait_apart(dve, nc, self.x_ready, b + 1, self.scratch)
        for t in range(CT):
            xt = self.X[:, bass.ds(b * CT + t, 1), :].rearrange("p o d -> p (o d)")
            nc.vector.bn_stats(self.st[:, t, :], xt).then_inc(self.ln, 1)
        wait_apart(dve, nc, self.ln, CT * b + CT, self.scratch)
        for t in range(CT):
            ins = nc.vector.bn_aggr(self.mv[:, t, :], self.st[:, t, :])
        ins.then_inc(self.ln_stats, 1)

    def dve_normalise(self, dve, b, u, turn):
        nc = self.nc
        dve.wait_ge(self.rstd_ready, b + 1)
        if not isinstance(turn, int) or turn:
            dve.wait_ge(self.scattered[u], 16 * CT * turn)
        for t in range(CT):
            xt = self.X[:, bass.ds(b * CT + t, 1), :].rearrange("p o d -> p (o d)")
            ins = nc.vector.tensor_scalar(self.row[:, u, t, 0:P], xt, self.mv[:, t, 0:1], self.rstd[:, t:t + 1],
                                          ALU.subtract, ALU.mult)
        ins.then_inc(self.xn_ready, 1)
        nc.vector.tensor_copy(self.row[:, u, :, COL_ID:COL_ID + 1], self.c("ids")[:, bass.ds(b * CT, CT)].unsqueeze(2))

    def dve_pick(self, dve, b, u, turn):
        nc = self.nc
        picks = 3
        dve.wait_ge(self.lg_psum, b + 1)
        scores = self.bank[:, 0:CT * EXPERTS].rearrange("p (t e) -> p t e", t=CT)
        wide = [P, CT, EXPERTS]
        if self.layer:
            nc.vector.tensor_tensor(self.lg[:, :, :], scores, self.bias.unsqueeze(1).to_broadcast(wide),
                                    ALU.add).then_inc(self.lg_ready, 1)
        else:
            nc.vector.tensor_copy(self.lg[:, :, :], scores).then_inc(self.lg_ready, 1)
        wait_apart(dve, nc, self.lg_ready, b + 1, self.scratch)
        for t in range(CT):
            ins = nc.vector.max(self.top[:, t, :], self.lg[:, t, :])
        ins.then_inc(self.pick, 1)
        wait_apart(dve, nc, self.pick, picks * b + 1, self.scratch)
        for t in range(CT):
            ins = nc.vector.max_index(self.at[:, t, :], self.top[:, t, :], self.lg[:, t, :])
        ins.then_inc(self.pick, 1)
        if not self.layer:
            nc.vector.tensor_tensor(self.soft[:, 0, :, :], self.lg[:, :, :], self.top[:, :, 0:1].to_broadcast(wide),
                                    ALU.subtract).then_inc(self.soft_ready, 1)
        dve.wait_ge(self.pick, picks * b + 2)
        nc.vector.tensor_copy(self.first[:, :], self.at[:, :, 0]).then_inc(self.pick, 1)
        dve.wait_ge(self.pick, picks * b + 3)
        for hot in (self.hot32, self.hot):
            ins = nc.vector.tensor_tensor(hot[:, :, :], self.c("iota").unsqueeze(1).to_broadcast(wide),
                                          self.first[:, :].unsqueeze(2).to_broadcast(wide), ALU.is_equal)
        ins.then_inc(self.hot_ready, 1)

    def dve_gate(self, dve, b, u, turn):
        if self.layer:
            return
        nc, small = self.nc, self.small
        dve.wait_ge(self.exp_ready, b + 1)
        nc.vector.tensor_reduce(small[:, 0, :], self.soft[:, 1, :, :], AX.X, ALU.add).then_inc(self.gate_step, 1)
        dve.wait_ge(self.gate_step, 4 * b + 1)
        nc.vector.reciprocal(small[:, 1, :], small[:, 0, :]).then_inc(self.gate_step, 1)
        dve.wait_ge(self.gate_step, 4 * b + 2)
        nc.vector.tensor_scalar(small[:, 2, :], small[:, 1, :], 1e-8, None, ALU.add).then_inc(self.gate_step, 1)
        dve.wait_ge(self.gate_step, 4 * b + 3)
        nc.vector.reciprocal(small[:, 3, :], small[:, 2, :]).then_inc(self.gate_step, 1)
        dve.wait_ge(self.gate_step, 4 * b + 4)
        nc.vector.tensor_tensor(self.row[:, u, :, COL_TV:COL_TV + 1], small[:, 1, :].unsqueeze(2),
                                small[:, 3, :].unsqueeze(2), ALU.mult).then_inc(self.tv_ready, 1)

    def dve_place(self, dve, b, u, turn):
        nc, place, base = self.nc, self.place, self.base
        dve.wait_ge(self.count_psum, b + 1)
        counts = self.bank[:, CT * EXPERTS:2 * CT * EXPERTS].rearrange("p (t e) -> p t e", t=CT)
        totals = self.bank[:, 2 * CT * EXPERTS:(2 * CT + 1) * EXPERTS]
        nc.vector.tensor_tensor(place[:, 0, :, :], counts, base[:, :].unsqueeze(1).to_broadcast([P, CT, EXPERTS]),
                                ALU.add).then_inc(self.place_step, 1)
        dve.wait_ge(self.place_step, 4 * b + 3)
        nc.vector.tensor_tensor(place[:, 1, :, :], place[:, 0, :, :], self.hot32[:, :, :], ALU.mult).then_inc(self.place_step, 1)
        nc.vector.tensor_tensor(base[:, :], base[:, :], totals, ALU.add).then_inc(self.place_step, 1)
        dve.wait_ge(self.place_step, 4 * b + 4)
        nc.vector.tensor_reduce(self.pos[:, :], place[:, 1, :, :], AX.X, ALU.add).then_inc(self.place_step, 1)
        dve.wait_ge(self.place_step, 4 * b + 6)
        nc.vector.tensor_copy(self.posi[:, u, :], self.pos[:, :]).then_inc(self.pos_ready, 1)

    def dve_end(self, dve):
        nc, table = self.nc, self.table
        nc.vector.tensor_copy(self.padi[:, :], self.base[:, :]).then_inc(self.ends_ready, 1)
        nc.vector.tensor_tensor(self.got[:, :], self.base[:, :], self.c("region"), ALU.subtract).then_inc(table, 1)
        nc.vector.tensor_scalar(self.slot_at[:, :], self.c("slots"), float(SLOT), None, ALU.mult).then_inc(table, 1)
        dve.wait_ge(table, 2)
        by_expert = [P, EXPERTS, NSLOT]
        nc.vector.tensor_tensor(self.over[:, :, :], self.got[:, :].unsqueeze(2).to_broadcast(by_expert),
                                self.slot_at[:, :].unsqueeze(1).to_broadcast(by_expert), ALU.is_gt).then_inc(table, 1)
        dve.wait_ge(table, 3)
        nc.vector.tensor_reduce(self.tiles[:, :], self.over[:, :, :], AX.X, ALU.add).then_inc(table, 1)
        dve.wait_ge(table, 4)
        nc.vector.tensor_tensor_scan(self.ends[:, :], self.tiles[:, :], self.tiles[:, :], 0.0, ALU.add, ALU.max).then_inc(table, 1)
        nc.vector.tensor_scalar(self.jump[:, :], self.tiles[:, :], -float(SLOT), float(REGION), ALU.mult, ALU.add).then_inc(table, 1)
        dve.wait_ge(table, 6)
        by_slot = [P, NSLOT, EXPERTS]
        nc.vector.tensor_tensor(self.passed[:, :, :], self.c("slots").unsqueeze(2).to_broadcast(by_slot),
                                self.ends[:, :].unsqueeze(1).to_broadcast(by_slot), ALU.is_ge).then_inc(table, 1)
        dve.wait_ge(table, 7)
        nc.vector.tensor_reduce(self.number[:, :], self.passed[:, :, :], AX.X, ALU.add).then_inc(table, 1)
        dve.wait_ge(table, 8)
        nc.vector.tensor_scalar(self.slot_expert[:, :], self.number[:, :], float(EXPERTS - 1), None, ALU.min).then_inc(table, 1)
        nc.vector.tensor_tensor(self.passed[:, :, :], self.passed[:, :, :], self.jump[:, :].unsqueeze(1).to_broadcast(by_slot),
                                ALU.mult).then_inc(table, 1)
        dve.wait_ge(table, 10)
        nc.vector.tensor_reduce(self.skipped[:, :], self.passed[:, :, :], AX.X, ALU.add).then_inc(table, 1)
        dve.wait_ge(table, 11)
        nc.vector.tensor_tensor(self.slot_row[:, :], self.skipped[:, :], self.slot_at[:, :], ALU.add).then_inc(table, 1)
        dve.wait_ge(table, 12)


    def pool_begin(self, pool):
        nc = self.nc
        nc.gpsimd.memset(self.euler[:, :, :], float(np.e))
        nc.gpsimd.memset(self.padding[:, :, :], 0.0).then_inc(self.ve_done, 1)
        pool.wait_ge(self.ve_done, 1)
        nc.gpsimd.memset(self.padding[:, :, COL_ID:COL_ID + 1], NO_TOKEN).then_inc(self.cleared, 1)
        pool.wait_ge(self.cleared, 1)

    def pool_inverse_deviation(self, pool, b, u, turn):
        nc = self.nc
        pool.wait_ge(self.ln_stats, b + 1)
        nc.gpsimd.tensor_tensor(self.ve[:, :], self.mv[:, :, 1], self.eps[:, 0:CT], ALU.add).then_inc(self.ve_done, 1)
        pool.wait_ge(self.ve_done, b + 2)
        nc.gpsimd.tensor_tensor(self.rstd[:, :], self.ve[:, :], self.minus_half[:, :], ALU.pow).then_inc(self.rstd_ready, 1)

    def pool_exp(self, pool, b, u, turn):
        pool.wait_ge(self.soft_ready, b + 1)
        self.nc.gpsimd.tensor_tensor(self.soft[:, 1, :, :], self.euler[:, :, :], self.soft[:, 0, :, :],
                                     ALU.pow).then_inc(self.exp_ready, 1)

    def pool_scatter(self, pool, b, u, turn):
        nc = self.nc
        if not self.layer:
            pool.wait_ge(self.tv_ready, b + 1)
        pool.wait_ge(self.pos_ready, b + 1)
        pool.wait_ge(self.x_copied, b + 1)
        after_previous(pool, self.told_done, b)
        nc.gpsimd.tensor_tensor(self.told[:, :], self.minus_half[:, :], self.minus_half[:, :], ALU.mult).then_inc(self.told_done, 1)
        for t in range(CT):
            nc.gpsimd.indirect_dma_start(
                out=self.rows, out_offset=bass.IndirectOffsetOnAxis(ap=self.posi[:, u, t:t + 1], axis=0),
                in_=self.row[:, u, t, :], in_offset=None).then_inc(self.scattered[u], 16)

    def pool_end(self, pool):
        for u in range(self.buffers):
            pool.wait_ge(self.scattered[u], 16 * TILES // self.buffers)


    def pe_turn(self, pe, b, u, turn):
        nc = self.nc
        pe.wait_ge(self.xn_ready, b + 1)
        after_previous(pe, self.pos_ready, b)
        for t in range(CT):
            mm = nc.tensor.transpose(self.bank[:, t * P:(t + 1) * P], self.row[:, u, t, 0:P], self.c("ident"))
        mm.then_inc(self.xT_psum, 1)

    def pe_scores(self, pe, b, u, turn):
        nc = self.nc
        pe.wait_ge(self.xT_ready, b + 1)
        for t in range(CT):
            mm = nc.tensor.matmul(self.bank[:, t * EXPERTS:(t + 1) * EXPERTS], self.xT[:, t * P:(t + 1) * P], self.router,
                                  start=True, stop=True)
        mm.then_inc(self.lg_psum, 1)

    def pe_count(self, pe, b, u, turn):
        nc = self.nc
        pe.wait_ge(self.hot_ready, b + 1)
        flat = self.hot[:, :, :].rearrange("p t e -> p (t e)")
        C0 = CT * EXPERTS
        nc.tensor.matmul(self.bank[:, C0:2 * C0], self.before[:, :], flat, start=True, stop=True, skip_group_check=True)
        for d in range(1, CT):
            nc.tensor.matmul(self.bank[:, C0 + d * EXPERTS:2 * C0], self.ones[:, :], flat[:, 0:(CT - d) * EXPERTS],
                             start=False, stop=True, skip_group_check=True)
        for t in range(CT):
            mm = nc.tensor.matmul(self.bank[:, 2 * C0:2 * C0 + EXPERTS], self.ones[:, :], self.hot[:, t, :],
                                  start=(t == 0), stop=(t == CT - 1))
        mm.then_inc(self.count_psum, 1)


    def act_copy(self, act, b, u, turn):
        nc = self.nc
        act.wait_ge(self.xT_psum, b + 1)
        after_previous(act, self.lg_psum, b)
        nc.scalar.activation(self.xT[:, :], self.bank, ACT.Copy).then_inc(self.xT_ready, 1)
        nc.scalar.activation(self.row[:, u, :, COL_X:COL_X + P], self.X[:, bass.ds(b * CT, CT), :], ACT.Copy).then_inc(self.x_copied, 1)


    def sp_padding(self, sp):
        sp.wait_ge(self.cleared, 1)
        spare = self.rows[EXPERTS * REGION:, :].rearrange("(n p) r -> p n r", p=P)
        for s in range(SPARE // SLOT):
            sp.dma_start(spare[:, 2 * s:2 * s + 2, :], self.padding[:, :, :]).then_inc(self.padded, 16)
        sp.wait_ge(self.ends_ready, 1)
        for e in range(EXPERTS):
            end = sp.value_load(self.padi[0:1, e:e + 1], min_val=e * REGION, max_val=e * REGION + TOKENS)
            sp.dma_start(self.rows[bass.ds(end, SLOT), :].rearrange("(n p) r -> p n r", p=P),
                         self.padding[:, :, :]).then_inc(self.padded, 16)
        sp.wait_ge(self.padded, 16 * (SPARE // SLOT + EXPERTS))


def routed(layer, nc, X, w, c, PS, before, ones, minus_half, eps, scratch, rows, weights, b2, dest, slot_row, slot_expert, stored):
    chunks = (2, 4)[layer]
    B1 = 2 * chunks * P
    with ExitStack() as ctx:
        def sb(name, shape, dt=F32):
            return ctx.enter_context(nc.sbuf_tensor(f"f{layer}_" + name, shape, dt))

        def sem(name):
            return ctx.enter_context(nc.semaphore(f"f{layer}_" + name))

        row = sb("row", [P, DEPTH, 2, ROW])
        wt = sb("wt", [P, DEPTH, weights.shape[2]])
        b2r = sb("b2r", [1, DEPTH, P])
        one_row = sb("one_row", [1, P])
        xT = sb("xT", [P, 2, SLOT])
        hid = sb("hid", [P, 2, chunks, SLOT])
        y = sb("y", [P, 2, 2, P])
        xb = sb("xb", [P, 2, 2, P])
        st = sb("st", [P, 2, 2, 6])
        mv = sb("mv", [P, 2, 2, 2])
        ve = sb("ve", [P, 2, 2])
        rstd = sb("rstd", [P, 2, 2])
        centred = sb("centred", [P, 2, 2, P])
        res = sb("res", [P, DEPTH, 2, P])
        token = sb("token", [P, DEPTH, 2], I32)
        told = sb("told", [P, CT])

        rows_in = [sem(f"rows_in{u}") for u in range(DEPTH)]
        weights_in = [sem(f"weights_in{u}") for u in range(DEPTH)]
        one_made = sem("one_made"); xT_psum = sem("xT_psum"); xT_ready = sem("xT_ready"); h_psum = sem("h_psum")
        hid_ready = sem("hid_ready"); out_psum = sem("out_psum"); y_ready = sem("y_ready"); stats = sem("stats")
        mv_ready = sem("mv_ready"); ve_done = sem("ve_done"); rstd_ready = sem("rstd_ready")
        xb_ready = sem("xb_ready"); centred_ready = sem("centred_ready")
        res_ready = sem("res_ready"); told_done = sem("told_done")

        block = ctx.enter_context(nc.Block())
        ident = c("ident")

        def over_slots(eng, step):
            turns = NSLOT // DEPTH
            for s in range(DEPTH):
                step(s, s, 0)
            with eng.Fori(1, turns - 1) as i:
                for u in range(DEPTH):
                    step(i * DEPTH + u, u, i)
            for u in range(DEPTH):
                step(NSLOT - DEPTH + u, u, turns - 1)

        def since(s, n):
            return not isinstance(s, int) or s >= n

        def last(s):
            return isinstance(s, int) and s == NSLOT - 1

        @block.sync
        def _(sp):
            def step(s, u, turn):
                r = sp.value_load(slot_row[0:1, bass.ds(s, 1)], min_val=0, max_val=ROWS - SLOT)
                e = sp.value_load(slot_expert[0:1, bass.ds(s, 1)], min_val=0, max_val=EXPERTS - 1)
                if since(s, DEPTH):
                    sp.wait_ge(res_ready, s - (DEPTH - 1))
                sp.dma_start(row[:, u, :, :], rows[bass.ds(r, SLOT), :].rearrange("(p a) r -> p a r", a=2)).then_inc(rows_in[u], 16)
                sp.dma_start(wt[:, u, :], weights[bass.ds(e, 1), :, :].rearrange("o p n -> (o p) n")).then_inc(weights_in[u], 16)
                if layer:
                    sp.dma_start(b2r[0:1, u, :], b2[bass.ds(e, 1), :]).then_inc(weights_in[u], 16)
            over_slots(sp, step)

        @block.gpsimd
        def _(pool):
            nc.gpsimd.memset(one_row[:, :], 1.0).then_inc(one_made, 1)

            def inverse_deviation(s, v):
                pool.wait_ge(mv_ready, s + 1)
                nc.gpsimd.tensor_tensor(ve[:, v, :], mv[:, v, :, 1], eps[:, 0:2], ALU.add).then_inc(ve_done, 1)
                pool.wait_ge(ve_done, s + 1)
                nc.gpsimd.tensor_tensor(rstd[:, v, :], ve[:, v, :], minus_half[:, 0:2], ALU.pow).then_inc(rstd_ready, 1)

            def store(s, u):
                pool.wait_ge(res_ready, s + 1)
                after_previous(pool, told_done, s)
                nc.gpsimd.tensor_tensor(told[:, :], minus_half[:, :], minus_half[:, :], ALU.mult).then_inc(told_done, 1)
                for a in range(2):
                    nc.gpsimd.indirect_dma_start(
                        out=dest, out_offset=bass.IndirectOffsetOnAxis(ap=token[:, u, a:a + 1], axis=0),
                        in_=res[:, u, a, :], in_offset=None, bounds_check=TOKENS - 1, oob_is_err=False).then_inc(stored[u], 16)

            def step(s, u, turn):
                if layer:
                    store(s, u)
                    return
                inverse_deviation(s, u % 2)
                if since(s, 1):
                    store(s - 1 if isinstance(s, int) else s + (-1), (u - 1) % DEPTH)
            over_slots(pool, step)
            if not layer:
                store(NSLOT - 1, DEPTH - 1)
            for u in range(DEPTH):
                pool.wait_ge(stored[u], 32 * NSLOT // DEPTH)

        @block.tensor
        def _(pe):
            pe.wait_ge(one_made, 1)

            def turn_rows(s, u, turn):
                pe.wait_ge(rows_in[u], 16 * (turn + 1))
                for a in range(2):
                    mm = nc.tensor.transpose(PS[:, u % 2, a * P:(a + 1) * P], row[:, u, a, 0:P], ident)
                mm.then_inc(xT_psum, 1)

            def up(s, u, turn):
                pe.wait_ge(weights_in[u], (16 + 16 * layer) * (turn + 1))
                pe.wait_ge(xT_ready, s + 1)
                for f in range(chunks):
                    bank, half = divmod(f, 2)
                    mm = nc.tensor.matmul(PS[:, 2 + 2 * (u % 2) + bank, half * SLOT:(half + 1) * SLOT],
                                          wt[:, u, f * P:(f + 1) * P], xT[:, u % 2, :], start=True, stop=True)
                mm.then_inc(h_psum, 1)

            def down(s, u):
                pe.wait_ge(hid_ready, s + 1)
                if since(s, 2):
                    pe.wait_ge(res_ready if layer else y_ready, s - 1)
                v = u % 2
                for a in range(2):
                    for f in range(chunks):
                        mm = nc.tensor.matmul(PS[:, 6 + v, a * P:(a + 1) * P], hid[:, v, f, a * P:(a + 1) * P],
                                              wt[:, u, (chunks + f) * P:(chunks + f + 1) * P],
                                              start=(f == 0), stop=(f == chunks - 1 and not layer))
                    if layer:
                        mm = nc.tensor.matmul(PS[:, 6 + v, a * P:(a + 1) * P], one_row[:, :], b2r[0:1, u, :],
                                              start=False, stop=True)
                mm.then_inc(out_psum, 1)

            turn_rows(0, 0, 0)

            def step(s, u, turn):
                if not last(s):
                    turn_rows(s + 1, (u + 1) % DEPTH, turn + (u + 1) // DEPTH)
                up(s, u, turn)
                if since(s, 1):
                    down(s + (-1), (u - 1) % DEPTH)
            over_slots(pe, step)
            down(NSLOT - 1, DEPTH - 1)

        @block.scalar
        def _(act):
            nc.scalar.preload_act_table(ACT.Gelu)

            def copy_xT(s, v):
                act.wait_ge(xT_psum, s + 1)
                nc.scalar.activation(xT[:, v, :], PS[:, v, 0:SLOT], ACT.Copy).then_inc(xT_ready, 1)

            def gelu(s, u):
                act.wait_ge(h_psum, s + 1)
                if since(s, 2):
                    act.wait_ge(out_psum, s - 1)
                v = u % 2
                if layer:
                    for f in range(chunks):
                        bank, half = divmod(f, 2)
                        ins = nc.scalar.activation(hid[:, v, f, :], PS[:, 2 + 2 * v + bank, half * SLOT:(half + 1) * SLOT],
                                                   ACT.Gelu, bias=wt[:, u, B1 + f:B1 + f + 1])
                else:
                    ins = nc.scalar.activation(hid[:, v, :, :].rearrange("p f t -> p (f t)"), PS[:, 2 + 2 * v, :], ACT.Gelu)
                ins.then_inc(hid_ready, 1)

            def gate(s, u, turn):
                act.wait_ge(out_psum, s + 1)
                if since(s, 2):
                    act.wait_ge(centred_ready, s - 1)
                v = u % 2
                for a in range(2):
                    ins = nc.scalar.activation(y[:, v, a, :], PS[:, 6 + v, a * P:(a + 1) * P], ACT.Copy,
                                               scale=row[:, u, a, COL_TV:COL_TV + 1])
                ins.then_inc(y_ready, 1)

            copy_xT(0, 0)

            def step(s, u, turn):
                if not last(s):
                    copy_xT(s + 1, (u + 1) % 2)
                gelu(s, u)
                if not layer and since(s, 1):
                    gate(s + (-1), (u - 1) % DEPTH, turn)
            over_slots(act, step)
            if not layer:
                gate(NSLOT - 1, DEPTH - 1, None)

        @block.vector
        def _(dve):
            def take_token(s, u, turn):
                dve.wait_ge(rows_in[u], 16 * (turn + 1))
                if since(s, DEPTH):
                    dve.wait_ge(stored[u], 32 * turn)
                nc.vector.tensor_copy(token[:, u, :].unsqueeze(2), row[:, u, :, COL_ID:COL_ID + 1])

            def add_x(s, u):
                dve.wait_ge(out_psum, s + 1)
                nc.vector.tensor_tensor(res[:, u, :, :], PS[:, 6 + u % 2, 0:SLOT].rearrange("p (a d) -> p a d", a=2),
                                        row[:, u, :, COL_X:COL_X + P], ALU.add).then_inc(res_ready, 1)

            def statistics(s, u):
                v = u % 2
                if since(s, 2):
                    dve.wait_ge(res_ready, s - 1)
                nc.vector.tensor_tensor(xb[:, v, :, :], row[:, u, :, COL_X:COL_X + P],
                                        w("beta").unsqueeze(1).to_broadcast([P, 2, P]), ALU.add).then_inc(xb_ready, 1)
                dve.wait_ge(y_ready, s + 1)
                for a in range(2):
                    nc.vector.bn_stats(st[:, v, a, :], y[:, v, a, :]).then_inc(stats, 1)
                wait_apart(dve, nc, stats, 2 * s + 2, scratch)
                for a in range(2):
                    ins = nc.vector.bn_aggr(mv[:, v, a, :], st[:, v, a, :])
                ins.then_inc(mv_ready, 1)

            def close(s, u):
                v = u % 2
                dve.wait_ge(mv_ready, s + 1)
                for a in range(2):
                    ins = nc.vector.scalar_tensor_tensor(centred[:, v, a, :], y[:, v, a, :], mv[:, v, a, 0:1], w("gamma"),
                                                         ALU.subtract, ALU.mult)
                ins.then_inc(centred_ready, 1)
                dve.wait_ge(centred_ready, s + 1)
                dve.wait_ge(xb_ready, s + 1)
                dve.wait_ge(rstd_ready, s + 1)
                for a in range(2):
                    ins = nc.vector.scalar_tensor_tensor(res[:, u, a, :], centred[:, v, a, :], rstd[:, v, a:a + 1],
                                                         xb[:, v, a, :], ALU.mult, ALU.add)
                ins.then_inc(res_ready, 1)

            def step(s, u, turn):
                take_token(s, u, turn)
                if layer:
                    add_x(s, u)
                    return
                statistics(s, u)
                if since(s, 1):
                    close(s + (-1), (u - 1) % DEPTH)
            over_slots(dve, step)
            if not layer:
                close(NSLOT - 1, DEPTH - 1)


def softmax_attention(nc, X, w, c, PS, before, ones, minus_half, eps, scratch, mid, rows, slot_row, slot_expert, scattered):
    with ExitStack() as ctx:
        def sb(name, shape, dt=F32):
            return ctx.enter_context(nc.sbuf_tensor("s_" + name, shape, dt))

        def sem(name):
            return ctx.enter_context(nc.semaphore("s_" + name))

        qk = sb("qk", [P, P])
        st = sb("st", [P, CT, 6])
        mv = sb("mv", [P, CT, 2])
        ve = sb("ve", [P, CT])
        rstd = sb("rstd", [P, CT])
        xn = sb("xn", [P, CT, P])
        xT = sb("xT", [P, 2, SEQ])
        yT = sb("yT", [P, 2, SEQ])
        v = sb("v", [P, 2, CT, P])
        nmax = sb("nmax", [P, CT])
        total = sb("total", [P, CT])
        inverse = sb("inverse", [P, 2, CT])
        prob = sb("prob", [P, 2, SEQ])
        probT = sb("probT", [P, 2, SEQ])

        x_in = sem("x_in"); qk_psum = sem("qk_psum"); qk_ready = sem("qk_ready")
        ln = sem("ln"); ln_stats = sem("ln_stats"); ve_done = sem("ve_done"); rstd_ready = sem("rstd_ready")
        xn_ready = sem("xn_ready"); xT_psum = sem("xT_psum"); xT_ready = sem("xT_ready")
        y_psum = sem("y_psum"); y_ready = sem("y_ready"); v_psum = sem("v_psum"); v_ready = sem("v_ready")
        score_psum = sem("score_psum"); max_ready = sem("max_ready"); prob_ready = sem("prob_ready")
        pT_psum = sem("pT_psum"); pT_ready = sem("pT_ready"); out_psum = sem("out_psum")
        inv_step = sem("inv_step"); x_ready = sem("x_ready")

        block = ctx.enter_context(nc.Block())
        ident = c("ident")

        routing = Routing(1, ctx, nc, X, w, c, PS, before, ones, minus_half, eps, scratch, rows, slot_row, slot_expert,
                          bank=7, scattered=scattered, x_ready=x_ready)

        def stages(eng, f, a, route):
            for step in f(0, 0):
                step()
            a(0, 0, f(1, 1), [])
            a(1, 1, f(2, 0), route(0, 0, 0))
            a(2, 0, f(3, 1), route(1, 1, 0))
            with eng.Fori(1, (BATCHES - 2) // 2) as i:
                for u in range(2):
                    b = i * 2 + (1 + u)
                    a(b, 1 - u, f(b + 1, u), route(i * 2 + u, u, i))
            a(BATCHES - 1, 1, [], route(BATCHES - 2, 0, BATCHES // 2 - 1))
            for step in route(BATCHES - 1, 1, BATCHES // 2 - 1):
                step()

        def steps(eng, *which):
            return lambda b, u, turn: [lambda step=step: step(eng, b, u, turn) for step in which]

        @block.sync
        def _(sp):
            for b in range(BATCHES):
                if b:
                    sp.wait_ge(x_in, 16 * b)
                sp.dma_start(X[:, b * CT:(b + 1) * CT, :],
                             mid[b * SEQ:(b + 1) * SEQ, :].rearrange("(c p) d -> p c d", p=P)).then_inc(x_in, 16)
            sp.wait_ge(x_in, 16 * BATCHES)
            routing.sp_padding(sp)

        @block.gpsimd
        def _(pool):
            def f(b, u):
                def rstd_step():
                    pool.wait_ge(ln_stats, b + 1)
                    nc.gpsimd.tensor_tensor(ve[:, :], mv[:, :, 1], eps[:, 0:CT], ALU.add).then_inc(ve_done, 1)
                    pool.wait_ge(ve_done, b + 1)
                    nc.gpsimd.tensor_tensor(rstd[:, :], ve[:, :], minus_half[:, :], ALU.pow).then_inc(rstd_ready, 1)
                return [rstd_step]

            def a(b, u, nxt, sent):
                for step in sent[:1] + nxt + sent[1:]:
                    step()
            routing.pool_begin(pool)
            stages(pool, f, a, steps(pool, routing.pool_inverse_deviation, routing.pool_scatter))
            routing.pool_end(pool)

        @block.tensor
        def _(pe):
            nc.tensor.matmul(PS[:, 1, 0:P], w("q1"), w("k1"), start=True, stop=True).then_inc(qk_psum, 1)

            def f(b, u):
                def transpose_xn():
                    pe.wait_ge(xn_ready, b + 1)
                    after_previous(pe, v_ready, b)
                    for t in range(CT):
                        mm = nc.tensor.transpose(PS[:, 0, t * P:(t + 1) * P], xn[:, t, :], ident)
                    mm.then_inc(xT_psum, 1)

                def project():
                    pe.wait_ge(xT_ready, b + 1)
                    pe.wait_ge(qk_ready, 1)
                    after_previous(pe, y_ready, b)
                    nc.tensor.matmul(PS[:, 1, :], qk[:, :], xT[:, u, :], start=True, stop=True).then_inc(y_psum, 1)
                    for t in range(CT):
                        mm = nc.tensor.matmul(PS[:, 0, t * P:(t + 1) * P], xT[:, u, t * P:(t + 1) * P], w("v1"),
                                              start=True, stop=True)
                    mm.then_inc(v_psum, 1)
                return [transpose_xn, project]

            def a(b, u, nxt, sent):
                def score(t):
                    pe.wait_ge(y_ready, b + 1)
                    if t >= 2:
                        pe.wait_ge(prob_ready, CT * b + t - 1)
                    else:
                        after_previous(pe, prob_ready, b, CT)
                    nc.tensor.matmul(PS[:, 2 + t % 2, :], yT[:, u, t * P:(t + 1) * P], xT[:, u, :],
                                     start=True, stop=True).then_inc(score_psum, 1)

                def attend(t):
                    pe.wait_ge(prob_ready, CT * b + t + 1)
                    if t >= 2:
                        pe.wait_ge(pT_ready, CT * b + t - 1)
                    else:
                        after_previous(pe, pT_ready, b, CT)
                    for m in range(CT):
                        mm = nc.tensor.transpose(PS[:, 4 + t % 2, m * P:(m + 1) * P], prob[:, t % 2, m * P:(m + 1) * P], ident)
                    mm.then_inc(pT_psum, 1)

                def weigh(t):
                    pe.wait_ge(pT_ready, CT * b + t + 1)
                    if t == 0:
                        pe.wait_ge(v_ready, b + 1)
                        after_previous(pe, x_ready, b)
                    for m in range(CT):
                        mm = nc.tensor.matmul(PS[:, 6, t * P:(t + 1) * P], probT[:, t % 2, m * P:(m + 1) * P], v[:, u, m, :],
                                              start=(m == 0), stop=(m == CT - 1))
                    mm.then_inc(out_psum, 1)

                score(0)
                score(1)
                attend(0)
                score(2)
                attend(1)
                weigh(0)
                if sent:
                    sent[0]()
                score(3)
                if nxt:
                    nxt[0]()
                attend(2)
                if sent:
                    sent[1]()
                weigh(1)
                if nxt:
                    nxt[1]()
                attend(3)
                weigh(2)
                if sent:
                    sent[2]()
                weigh(3)
            stages(pe, f, a, steps(pe, routing.pe_turn, routing.pe_scores, routing.pe_count))

        @block.scalar
        def _(act):
            nc.scalar.preload_act_table(ACT.Exp)

            def f(b, u):
                def copy_x():
                    act.wait_ge(xT_psum, b + 1)
                    nc.scalar.activation(xT[:, u, :], PS[:, 0, :], ACT.Copy).then_inc(xT_ready, 1)

                def copy_v():
                    act.wait_ge(v_psum, b + 1)
                    nc.scalar.activation(v[:, u, :, :].rearrange("p c d -> p (c d)"), PS[:, 0, :], ACT.Copy).then_inc(v_ready, 1)
                return [copy_x, copy_v]

            def a(b, u, nxt, sent):
                for t in range(CT):
                    act.wait_ge(max_ready, CT * b + t + 1)
                    if t >= 2:
                        act.wait_ge(pT_psum, CT * b + t - 1)
                    elif not (isinstance(b, int) and b == 0):
                        act.wait_ge(inv_step, 2 * b)
                    nc.scalar.activation(prob[:, t % 2, :], PS[:, 2 + t % 2, :], ACT.Exp, bias=nmax[:, t:t + 1],
                                         accum_out=total[:, t:t + 1]).then_inc(prob_ready, 1)
                    if sent and t == 2:
                        sent[0]()
                    if nxt and t >= 2:
                        nxt[t - 2]()
            stages(act, f, a, steps(act, routing.act_copy))

        @block.vector
        def _(dve):
            dve.wait_ge(qk_psum, 1)
            nc.vector.tensor_copy(qk[:, :], PS[:, 1, 0:P]).then_inc(qk_ready, 1)

            def f(b, u):
                def stats():
                    dve.wait_ge(x_in, 16 * b + 16)
                    for t in range(CT):
                        nc.vector.bn_stats(st[:, t, :], X[:, bass.ds(b * CT + t, 1), :].rearrange("p o d -> p (o d)")).then_inc(ln, 1)
                    wait_apart(dve, nc, ln, CT * b + CT, scratch)
                    for t in range(CT):
                        ins = nc.vector.bn_aggr(mv[:, t, :], st[:, t, :])
                    ins.then_inc(ln_stats, 1)

                def normalise():
                    dve.wait_ge(rstd_ready, b + 1)
                    for t in range(CT):
                        xt = X[:, bass.ds(b * CT + t, 1), :].rearrange("p o d -> p (o d)")
                        ins = nc.vector.tensor_scalar(xn[:, t, :], xt, mv[:, t, 0:1], rstd[:, t:t + 1],
                                                      ALU.subtract, ALU.mult)
                    ins.then_inc(xn_ready, 1)

                def copy_y():
                    dve.wait_ge(y_psum, b + 1)
                    nc.vector.tensor_copy(yT[:, u, :], PS[:, 1, :]).then_inc(y_ready, 1)
                return [stats, normalise, copy_y]

            def a(b, u, nxt, sent):
                def turn(n):
                    if nxt:
                        nxt[n]()

                def route(n):
                    if sent:
                        sent[n]()

                def largest(t):
                    dve.wait_ge(score_psum, CT * b + t + 1)
                    nc.vector.tensor_reduce(nmax[:, t:t + 1], PS[:, 2 + t % 2, :], AX.X, ALU.max,
                                            negate=True).then_inc(max_ready, 1)

                def copy_p(t):
                    dve.wait_ge(pT_psum, CT * b + t + 1)
                    if t >= 2:
                        dve.wait_ge(out_psum, CT * b + t - 1)
                    nc.vector.tensor_copy(probT[:, t % 2, :], PS[:, 4 + t % 2, :]).then_inc(pT_ready, 1)
                largest(0)
                route(0)
                largest(1)
                turn(0)
                copy_p(0)
                route(1)
                largest(2)
                turn(1)
                copy_p(1)
                largest(3)
                copy_p(2)
                route(2)
                turn(2)
                copy_p(3)
                route(3)
                dve.wait_ge(prob_ready, CT * b + CT)
                nc.vector.reciprocal(inverse[:, 0, :], total[:, :]).then_inc(inv_step, 1)
                dve.wait_ge(inv_step, 2 * b + 1)
                nc.vector.tensor_scalar(inverse[:, 1, :], inverse[:, 0, :], float(P) ** -0.5, None, ALU.mult).then_inc(inv_step, 1)
                dve.wait_ge(inv_step, 2 * b + 2)
                dve.wait_ge(out_psum, CT * b + CT)
                for t in range(CT):
                    xt = X[:, bass.ds(b * CT + t, 1), :].rearrange("p o d -> p (o d)")
                    ins = nc.vector.scalar_tensor_tensor(xt, PS[:, 6, t * P:(t + 1) * P], inverse[:, 1, t:t + 1], xt,
                                                         ALU.mult, ALU.add)
                ins.then_inc(x_ready, 1)
            routing.dve_begin(dve)
            stages(dve, f, a, steps(dve, routing.dve_statistics, routing.dve_normalise, routing.dve_pick, routing.dve_place))
            routing.dve_end(dve)



def _constants():
    t = {}
    p = np.arange(P)
    t["ident"] = np.eye(P)
    inv_freq = (np.float32(1.0) / np.power(np.float32(10000.0), np.arange(0, HD, 2, dtype=np.float32) / np.float32(HD))).astype(np.float32)
    theta = np.arange(SEQ, dtype=np.float32)[None, :] * inv_freq[(p % HD) // 2][:, None]
    t["cos"] = np.cos(theta)
    t["sin"] = np.sin(theta) * np.where(p % 2 == 0, -1.0, 1.0)[:, None]
    t["tri"] = p[:, None] <= p[None, :]
    t["before"] = p[:, None] < p[None, :]
    t["block"] = p[:, None] // HD == p[None, :] // HD
    t["group"] = (p[:, None] % 32) // HD == np.arange(4)[None, :]
    t["heads"] = p[:, None] // HD == np.arange(HEADS)[None, :]
    sel = np.zeros((P, MOE, P))
    for e in range(MOE):
        sel[[e, e + MOE], e, :] = 1.0
    t["sel"] = sel.reshape(P, -1)
    t["ids"] = p[:, None] + P * np.arange(TILES)[None, :]
    t["iota"] = np.broadcast_to(np.arange(EXPERTS), (P, EXPERTS))
    t["region"] = np.broadcast_to(REGION * np.arange(EXPERTS), (P, EXPERTS))
    t["slots"] = np.broadcast_to(np.arange(NSLOT), (P, NSLOT))
    return np.concatenate([np.asarray(t[n], np.float32) for n in CCOLS], axis=1)


def _layout(i):
    qkv = i["L0_attn_w_qkv"]
    swap = np.arange(P) ^ 1
    col = lambda a: a.reshape(-1, 1)
    rows = lambda a: np.broadcast_to(a, (P, a.shape[-1]))
    t = {
        "pw": i["L0_attn_w_pw"].T, "q": qkv[:P].T, "qs": qkv[:P][swap].T, "k": qkv[P:2 * P].T,
        "ks": qkv[P:2 * P][swap].T, "v": qkv[2 * P:].T, "o": i["L0_attn_w_o"].T, "gate": i["L0_attn_w_gate"].T,
        "moe_gate": i["L0_attn_w_moe_gate"].T, "dw": i["L0_attn_w_dw"], "b_gate": col(i["L0_attn_b_gate"]),
        "ln_g": col(i["L0_attn_ln_g"]), "ln_b": col(i["L0_attn_ln_b"]),
        "b1": i["L0_attn_b1"].reshape(MOE * MOE_CHUNKS, P).T, "b2": i["L0_attn_b2"].T,
        "router0": i["L0_ffn_gate_w"].T, "q1": i["L1_attn_Wq"], "k1": i["L1_attn_Wk"], "v1": i["L1_attn_Wv"].T,
        "router1": i["L1_ffn_wr"], "br1": rows(i["L1_ffn_br"]),
        "gamma": rows(i["L0_ffn_ln_gamma"]), "beta": rows(i["L0_ffn_ln_beta"]),
    }
    wsmall = np.concatenate([t[n] for n in WCOLS], axis=1)
    w1t = i["L0_attn_w1"].transpose(2, 0, 1).reshape(P, MOE * 512)
    w2t = i["L0_attn_w2"].reshape(MOE, P, MOE_CHUNKS, P).transpose(3, 0, 2, 1).reshape(P, MOE * 512)

    def experts(w1, w2, *more):
        f = w2.shape[1] // P
        return np.concatenate([w1, w2.reshape(EXPERTS, f, P, P).transpose(0, 2, 1, 3).reshape(EXPERTS, P, f * P), *more], axis=2)

    b1 = i["L1_ffn_b1"].reshape(EXPERTS, 4, P).transpose(0, 2, 1)
    return {
        "x": i["L0_attn_x"], "wsmall": wsmall, "consts": _constants(), "w1t": w1t, "w2t": w2t,
        "wr0": experts(i["L0_ffn_expert_w1"], i["L0_ffn_expert_w2"]),
        "wr1": experts(i["L1_ffn_w1"], i["L1_ffn_w2"], b1), "br2": i["L1_ffn_b2"],
    }


def kernel(**inputs):
    import concourse.bacc as bacc
    from concourse.bass_utils import run_bass_kernel_spmd

    nc = bacc.Bacc("TRN2", target_bir_lowering=False, num_devices=1)
    arrays = {n: np.ascontiguousarray(a) for n, a in _layout({n: np.asarray(a) for n, a in inputs.items()}).items()}
    args = {n: nc.dram_tensor(n, a.shape, mybir.dt.from_np(a.dtype), kind="ExternalInput").ap() for n, a in arrays.items()}
    args["out"] = nc.dram_tensor("out", (TOKENS, P), F32, kind="ExternalOutput").ap()
    program(nc, **args)
    r = run_bass_kernel_spmd(nc, [arrays], core_ids=[0])
    return r.results[0]["out"].reshape(BATCHES, SEQ, P)
```

```python
from contextlib import ExitStack

import numpy as np

import concourse.bass as bass
from concourse import mybir

F32 = mybir.dt.float32
F32R = mybir.dt.float32r
BF16 = mybir.dt.bfloat16
I32 = mybir.dt.int32
U32 = mybir.dt.uint32
ALU = mybir.AluOpType
ACT = mybir.ActivationFunctionType
AX = mybir.AxisListType

P = 128
BATCHES = 16
SEQ = 512
CT = SEQ // P
TOKENS = BATCHES * SEQ
TILES = TOKENS // P
HEADS, HD = 16, 8
MOE = 4
MOE_CHUNKS = 512 // P
EXPERTS = 8
LN_EPS = 1e-5

ROW = 260
COL_X, COL_TV, COL_ID = 128, 256, 257
SLOT = 256
REGION = TOKENS + SLOT
NSLOT = 40
DEPTH = 8
SPARE = (NSLOT - TOKENS // SLOT) * SLOT
ROWS = EXPERTS * REGION + SPARE
NO_TOKEN = 9000.0

WCOLS = {}


def _columns():
    at = 0
    for name, n in [("pw", P), ("q", P), ("qs", P), ("k", P), ("ks", P), ("v", P), ("o", P), ("gate", P),
                    ("moe_gate", MOE), ("dw", 3), ("b_gate", 1), ("ln_g", 1), ("ln_b", 1),
                    ("b1", MOE * MOE_CHUNKS), ("b2", MOE), ("router0", EXPERTS),
                    ("q1", P), ("k1", P), ("v1", P), ("router1", EXPERTS), ("br1", EXPERTS),
                    ("gamma", P), ("beta", P)]:
        WCOLS[name] = (at, at + n)
        at += n
    return at


NW = _columns()
CCOLS = {}


def _const_columns():
    at = 0
    for name, n in [("ident", P), ("cos", SEQ), ("sin", SEQ), ("tri", P), ("block", P), ("group", 4),
                    ("heads", HEADS), ("sel", MOE * P), ("before", P), ("ids", TILES), ("iota", EXPERTS),
                    ("region", EXPERTS), ("slots", NSLOT)]:
        CCOLS[name] = (at, at + n)
        at += n
    return at


NCONST = _const_columns()


def program(nc, x, wsmall, consts, w1t, w2t, wr0, wr1, br2, out):
    rows_dram = [nc.dram_tensor(f"rows{i}", (ROWS, ROW), F32, kind="Internal").ap() for i in range(2)]
    turned_dram = nc.dram_tensor("turned", (2, 2, P, SEQ), F32, kind="Internal").ap()
    mid_dram = nc.dram_tensor("mid", (TOKENS, P), F32, kind="Internal").ap()

    with ExitStack() as ctx:
        def sb(name, shape, dt=F32):
            return ctx.enter_context(nc.sbuf_tensor(name, shape, dt))

        X = sb("X", [P, TILES, P])
        W = sb("W", [P, NW])
        C = sb("C", [P, NCONST])
        before = sb("before", [P, P], BF16)
        ones = sb("ones", [P, P], BF16)
        minus_half = sb("minus_half", [P, CT])
        eps = sb("eps", [P, CT])
        scratch = sb("scratch", [P, 2])
        slot_row = sb("slot_row", [P, NSLOT], I32)
        slot_expert = sb("slot_expert", [P, NSLOT], I32)
        PS = ctx.enter_context(nc.psum_tensor("PS", [P, 8, 512], F32))

        def w(name):
            a, b = WCOLS[name]
            return W[:, a:b]

        def c(name):
            a, b = CCOLS[name]
            return C[:, a:b]

        scattered = [[ctx.enter_context(nc.semaphore(f"scattered{layer}_{u}")) for u in range(1 + layer)] for layer in range(2)]
        stored = [[ctx.enter_context(nc.semaphore(f"stored{layer}_{u}")) for u in range(DEPTH)] for layer in range(2)]
        shared = dict(nc=nc, X=X, w=w, c=c, PS=PS, before=before, ones=ones,
                      minus_half=minus_half, eps=eps, scratch=scratch)

        slots = dict(slot_row=slot_row, slot_expert=slot_expert)
        with ExitStack() as front, ExitStack() as sems:
            H = front.enter_context(nc.sbuf_tensor("H", [P, TOKENS], F32))
            LG = front.enter_context(nc.sbuf_tensor("LG", [P, TILES * MOE], F32))
            setup(sems=sems, wsmall=wsmall, consts=consts, W=W, C=C, **shared)
            attention_front(sems=sems, x=x, turned=turned_dram, H=H, LG=LG, **shared)
            mixture(sems=sems, H=H, LG=LG, w1t=w1t, w2t=w2t, rows=rows_dram[0], scattered=scattered[0], **slots, **shared)
        clear_semaphores(nc)
        with ExitStack() as sems:
            routed(0, sems=sems, rows=rows_dram[0], weights=wr0, b2=None, dest=mid_dram, stored=stored[0], **slots, **shared)
            softmax_attention(sems=sems, mid=mid_dram, rows=rows_dram[1], scattered=scattered[1], **slots, **shared)
            routed(1, sems=sems, rows=rows_dram[1], weights=wr1, b2=br2, dest=out, stored=stored[1], **slots, **shared)



def clear_semaphores(nc):
    nc.all_engine_barrier()
    used = sorted(nc.released_uncleared_semaphores)
    nc.gpsimd.sem_clear(range(used[0], used[-1] + 1))
    nc.all_engine_barrier()


def after_previous(eng, sem, b, per=1):
    if not (isinstance(b, int) and b == 0):
        eng.wait_ge(sem, b * per)


def wait_apart(dve, nc, sem, value, scratch):
    dve.wait_ge(sem, value)
    nc.vector.memset(scratch[:, 0:1], 0.0)


def setup(nc, sems, wsmall, consts, W, C, X, w, c, PS, before, ones, minus_half, eps, scratch):
    with ExitStack() as ctx:
        sem = lambda n: sems.enter_context(nc.semaphore(n))
        weights_in, consts_in, made = sem("weights_in"), sem("consts_in"), sem("made")
        block = ctx.enter_context(nc.Block())

        @block.sync
        def _(sp):
            sp.dma_start(W[:, :], wsmall).then_inc(weights_in, 16)
            sp.dma_start(C[:, :], consts).then_inc(consts_in, 16)
            sp.wait_ge(weights_in, 16)
            sp.wait_ge(consts_in, 16)

        @block.vector
        def _(dve):
            nc.vector.memset(ones[:, :], 1.0)
            nc.vector.memset(minus_half[:, :], -0.5)
            nc.vector.memset(eps[:, :], LN_EPS)
            nc.vector.memset(scratch[:, 1:2], 0.0)
            dve.wait_ge(consts_in, 16)
            nc.vector.tensor_copy(before[:, :], c("before"))
            dve.wait_ge(weights_in, 16)
            nc.vector.tensor_scalar(w("b_gate"), w("b_gate"), 0.5, None, ALU.mult)
            nc.vector.tensor_scalar(w("o"), w("o"), 0.5, None, ALU.mult).then_inc(made, 1)


def attention_front(nc, sems, X, w, c, PS, before, ones, minus_half, eps, scratch, H, LG, x, turned):
    with ExitStack() as ctx:
        def sb(name, shape, dt=F32):
            return ctx.enter_context(nc.sbuf_tensor(name, shape, dt))

        def sem(name):
            return sems.enter_context(nc.semaphore("a_" + name))

        st = sb("st", [P, CT, 6])
        mv = sb("mv", [P, CT, 2])
        ve = sb("ve", [P, CT])
        rstd = sb("rstd", [P, CT])
        xn = sb("xn", [P, CT, P])
        carrier = sb("carrier", [P, CT])
        act_scratch = sb("act_scratch", [P, 1])
        x1c = sb("x1c", [P, SEQ])
        xnT = sb("xnT", [P, SEQ + 2])
        y = sb("y", [P, 2, SEQ])
        x1T = sb("x1T", [P, 2, SEQ])
        delta = sb("delta", [P, 2, SEQ])
        rot = sb("rot", [P, 2, SEQ])
        ex = sb("ex", [P, SEQ])
        qphi = sb("qphi", [P, 2, SEQ])
        kphi = sb("kphi", [P, 2, SEQ])
        vt = sb("vt", [P, 2, CT, P])
        vm = sb("vm", [P, 2, CT, 4, P])
        ktok = sb("ktok", [P, CT - 1, P])
        parts = sb("parts", [P, 2, 2, SEQ], F32R)
        ks = sb("ks", [3 * 32, 4, SEQ])
        qs = sb("qs", [3 * 32, 4, SEQ])
        kr = sb("kr", [3 * 32, 2, 4, P], F32R)
        qm = sb("qm", [3 * 32, 2, 4, 4, P], F32R)
        kp = sb("kp", [P, SEQ])
        prod = sb("prod", [P, SEQ])
        am = sb("am", [P, 3, 4 * P])
        state = sb("state", [P, CT - 1, P])
        den = sb("den", [P, 2, CT * HEADS])
        spread = sb("spread", [P, SEQ])
        rdT = spread
        attn = sb("attn", [P, SEQ])
        th = sb("th", [P, SEQ])
        x2T = sb("x2T", [P, SEQ])
        st2 = sb("st2", [P, CT, 6])
        mv2 = sb("mv2", [P, CT, 2])
        ve2 = sb("ve2", [P, CT])
        rstd2 = sb("rstd2", [P, CT])
        z = sb("z", [P, CT, P])
        h = z[:, :, :].rearrange("p c d -> p (c d)")
        minus_one = sb("minus_one", [P, 1])

        x_in = sem("x_in"); zeroed = sem("zeroed"); act_const = sem("act_const")
        ln1 = sem("ln1"); ln1_stats = sem("ln1_stats"); ve1_done = sem("ve1_done"); rstd1_ready = sem("rstd1_ready")
        xn_ready = sem("xn_ready"); xnT_psum = sem("xnT_psum"); xnT_ready = sem("xnT_ready")
        conv = sem("conv"); pw_psum = sem("pw_psum"); x1_ready = sem("x1_ready")
        delta_ready = sem("delta_ready")
        qk_psum = sem("qk_psum"); qk_read = sem("qk_read"); rot_step = sem("rot_step"); exp_ready = sem("exp_ready")
        phi_ready = sem("phi_ready"); v_psum = sem("v_psum"); v_ready = sem("v_ready")
        kT_psum = sem("kT_psum"); ktok_ready = sem("ktok_ready"); hi_ready = sem("hi_ready"); parts_ready = sem("parts_ready"); q_stacked = sem("q_stacked")
        parked = sem("parked"); x1_copied = sem("x1_copied"); stack_read = sem("stack_read"); carried = sem("carried"); k_stacked = sem("k_stacked"); operands_ready = sem("operands_ready")
        kp_ready = sem("kp_ready"); prod_ready = sem("prod_ready")
        scores_psum = sem("scores_psum"); am_ready = sem("am_ready"); am_used = sem("am_used")
        state_psum = sem("state_psum"); state_ready = sem("state_ready")
        den_psum = sem("den_psum"); den_step = sem("den_step"); spread_ready = sem("spread_ready"); rdT_psum = sem("rdT_psum"); rdT_ready = sem("rdT_ready")
        num_psum = sem("num_psum"); attn_ready = sem("attn_ready"); gate_psum = sem("gate_psum")
        wo_psum = sem("wo_psum"); th_ready = sem("th_ready"); x2_step = sem("x2_step")
        x2_psum = sem("x2_psum"); ln2 = sem("ln2"); ln2_stats = sem("ln2_stats"); ve2_done = sem("ve2_done")
        rstd2_ready = sem("rstd2_ready"); z_ready = sem("z_ready"); zT_psum = sem("zT_psum"); h_ready = sem("h_ready")
        lg_psum = sem("lg_psum"); lg_ready = sem("lg_ready")

        block = ctx.enter_context(nc.Block())
        ident = c("ident")

        SCORE_BANK = [3, 4] * 4 + [1, 2, 3, 4] * 2

        def diagonal(t, u, tile):
            base = t[:, u, tile, 0, 0:1]
            ap = [list(base.ap[0]), [P + HD, 4], [4 * HD, 4], [1, HD]]
            return bass.AP(tensor=base.tensor, offset=base.offset, ap=ap)

        def tokens(t, b):
            return t[:, bass.ds(b * CT, CT), :]

        def stages(eng, steps):
            steps(None, 0, 0, None, None)
            steps(None, 1, 1, 0, None)
            steps(0, 0, 2, 1, None)
            steps(1, 1, 3, 2, 0)
            with eng.Fori(0, (BATCHES - 4) // 2) as i:
                for u in range(2):
                    b = i * 2 + (2 + u)
                    steps(b, u, b + 2, b + 1, b + (-1))
            steps(BATCHES - 2, 0, None, BATCHES - 1, BATCHES - 3)
            steps(BATCHES - 1, 1, None, None, BATCHES - 2)
            steps(None, 0, None, None, BATCHES - 1)

        @block.sync
        def _(sp):
            def load(b):
                after_previous(sp, x_in, b, 16)
                src = x[bass.ds(b, 1), :, :].rearrange("o (c p) d -> p (o c) d", p=P)
                sp.dma_start(X[:, bass.ds(b * CT, CT), :], src).then_inc(x_in, 16)

            def stack(b):
                for which in range(2):
                    sp.wait_ge(parts_ready, 2 * b + which + 1)
                    sp.dma_start(turned[which].rearrange("s p t -> p s t"), parts[:, which, :, :].bitcast(F32)).then_inc(parked, 16)
                sp.wait_ge(parked, 32 * b + 32)
                sp.wait_ge(stack_read, 32 * b + 32)
                for which, (dst, order, signal) in enumerate([(qs, (0, 1, 0), q_stacked), (ks, (0, 0, 1), k_stacked)]):
                    by_group = turned[which].rearrange("s (g p) t -> s p g t", g=4)
                    for slot, part in enumerate(order):
                        sp.dma_start(dst[32 * slot:32 * slot + 32, :, :], by_group[part]).then_inc(signal, 16)

            def steps(b, u, n, f, c_):
                if n is not None:
                    load(n)
                if f is not None:
                    stack(f)
            stages(sp, steps)
            sp.wait_ge(x_in, 16 * BATCHES)

        @block.gpsimd
        def _(pool):
            nc.gpsimd.memset(minus_one[:, :], -1.0).then_inc(act_const, 1)
            nc.gpsimd.memset(carrier[:, :], 0.0).then_inc(stack_read, 32)
            nc.gpsimd.memset(xnT[:, 0:2], 0.0)
            nc.gpsimd.memset(delta[:, :, 0:1], 0.0)
            nc.gpsimd.memset(vm[:, :, :, :, :], 0.0).then_inc(zeroed, 1)

            def inverse_deviation(b, stats_ready, mean_var, sums, done, result, ready):
                pool.wait_ge(stats_ready, b + 1)
                nc.gpsimd.tensor_tensor(sums[:, :], mean_var[:, :, 1], eps[:, 0:CT], ALU.add).then_inc(done, 1)
                pool.wait_ge(done, b + 1)
                nc.gpsimd.tensor_tensor(result[:, :], sums[:, :], minus_half[:, :], ALU.pow).then_inc(ready, 1)

            def low_part(b, u, which, full):
                pool.wait_ge(hi_ready, 2 * b + which + 1)
                nc.gpsimd.tensor_tensor(parts[:, which, 1, :], full[:, u, :], parts[:, which, 0, :].bitcast(F32),
                                        ALU.subtract).then_inc(parts_ready, 1)

            def steps(b, u, n, f, c_):
                if b is not None:
                    pool.wait_ge(kp_ready, b + 1)
                    nc.gpsimd.tensor_tensor(prod[:, :], qphi[:, u, :], kp[:, :], ALU.mult).then_inc(prod_ready, 1)
                if n is not None:
                    inverse_deviation(n, ln1_stats, mv, ve, ve1_done, rstd, rstd1_ready)
                if f is not None:
                    low_part(f, 1 - u, 0, qphi)
                if b is not None:
                    after_previous(pool, x2_step, b, 2)
                    after_previous(pool, carried, b)
                    nc.gpsimd.tensor_tensor(carrier[:, :], minus_half[:, :], minus_half[:, :], ALU.mult).then_inc(carried, 1)
                    nc.gpsimd.tensor_copy(x1c[:, :], x1T[:, u, :]).then_inc(x1_copied, 1)
                if c_ is not None:
                    inverse_deviation(c_, ln2_stats, mv2, ve2, ve2_done, rstd2, rstd2_ready)
                if f is not None:
                    low_part(f, 1 - u, 1, kphi)
                if f is not None:
                    pool.wait_ge(x1_ready, f + 1)
                    if c_ is not None:
                        pool.wait_ge(gate_psum, c_ + 1)
                    nc.gpsimd.tensor_tensor(delta[:, 1 - u, 1:], x1T[:, 1 - u, 1:], x1T[:, 1 - u, 0:SEQ - 1],
                                            ALU.subtract).then_inc(delta_ready, 1)
            stages(pool, steps)

        @block.tensor
        def _(pe):
            def turn_xn(b):
                pe.wait_ge(xn_ready, b + 1)
                after_previous(pe, v_ready, b)
                for t in range(CT):
                    mm = nc.tensor.transpose(PS[:, 0, t * P:(t + 1) * P], xn[:, t, :], ident)
                mm.then_inc(xnT_psum, 1)

            def pointwise(b):
                pe.wait_ge(conv, 3 * b + 3)
                nc.tensor.matmul(PS[:, 0, :], w("pw"), y[:, 0, :], start=True, stop=True).then_inc(pw_psum, 1)

            def project(b, u, name, n):
                pe.wait_ge(x1_ready, b + 1)
                if n:
                    pe.wait_ge(qk_read, 2 * b + 1)
                else:
                    after_previous(pe, qk_read, b, 2)
                    if not isinstance(b, int) or b >= 2:
                        pe.wait_ge(am_ready, 16 * (b + (-1)))
                nc.tensor.matmul(PS[:, 1, :], w(name), x1T[:, u, :], start=True, stop=True)
                nc.tensor.matmul(PS[:, 2, :], w(name + "s"), x1T[:, u, :],
                                 start=True, stop=True).then_inc(qk_psum, 1)

            def values(b, u):
                for t in range(CT):
                    mm = nc.tensor.matmul(PS[:, 0, t * P:(t + 1) * P], x1T[:, u, t * P:(t + 1) * P],
                                          w("v"), start=True, stop=True)
                mm.then_inc(v_psum, 1)

            def turn_k(b, u):
                pe.wait_ge(phi_ready, 2 * b + 2)
                for t in range(CT - 1):
                    mm = nc.tensor.transpose(PS[:, 6, (t + 1) * P:(t + 2) * P], kphi[:, u, t * P:(t + 1) * P], ident)
                mm.then_inc(kT_psum, 1)

            def scores(b, u, n, f):
                t, g = divmod(n, 4)
                if n >= 2 and n not in (8, 9):
                    pe.wait_ge(am_ready, 16 * b + n - (1 if n < 8 else 3))
                elif n < 2:
                    after_previous(pe, am_ready, b, 16)
                elif f is not None:
                    pe.wait_ge(qk_read, 2 * f + 2)
                if g == 0:
                    pe.wait_ge(operands_ready, 4 * b + t + 1)
                mm = nc.tensor.matmul(PS[:, SCORE_BANK[n], :], kr[:, t % 2, g, :],
                                      qm[:, t % 2, g, :, :].rearrange("p j q -> p (j q)"), start=True, stop=True)
                mm.then_inc(scores_psum, 1)

            def update_state(b, u, t):
                if t:
                    pe.wait_ge(state_ready, 3 * b + t)
                    pe.wait_ge(den_step, 2 * b + 1)
                else:
                    pe.wait_ge(ktok_ready, b + 1)
                nc.tensor.matmul(PS[:, 6, 0:P], ktok[:, t, :], vt[:, u, t, :], start=(t == 0), stop=True,
                                 skip_group_check=True).then_inc(state_psum, 1)

            def weigh(b, u, n):
                t, g = divmod(n, 4)
                if n == 0:
                    after_previous(pe, attn_ready, b)
                if g == 0 and t:
                    pe.wait_ge(state_ready, 3 * b + t)
                    nc.tensor.matmul(PS[:, 5, t * P:(t + 1) * P], state[:, t - 1, :],
                                     qphi[:, u, t * P:(t + 1) * P], start=True, stop=False, skip_group_check=True)
                pe.wait_ge(am_ready, 16 * b + n + 1)
                for j in range(4):
                    mm = nc.tensor.matmul(PS[32 * g:32 * g + 32, 5, t * P:(t + 1) * P],
                                          vm[:, u, t, j, 32 * g:32 * g + 32],
                                          am[:, n % 3, j * P:(j + 1) * P],
                                          start=(t == 0 and j == 0), stop=(j == 3), skip_group_check=True)
                mm.then_inc(am_used, 1)

            def denominators(b):
                pe.wait_ge(prod_ready, b + 1)
                pe.wait_ge(state_ready, 3 * b + 1)
                for t in range(CT):
                    mm = nc.tensor.matmul(PS[:, 6, P + t * HEADS:P + (t + 1) * HEADS], prod[:, t * P:(t + 1) * P],
                                          c("heads"), start=False, stop=True, skip_group_check=True)
                mm.then_inc(den_psum, 1)

            def turn_spread(b):
                pe.wait_ge(spread_ready, b + 1)
                after_previous(pe, lg_ready, b)
                for t in range(CT):
                    mm = nc.tensor.transpose(PS[:, 7, t * P:(t + 1) * P], spread[:, t * P:(t + 1) * P], ident)
                mm.then_inc(rdT_psum, 1)

            def gate(b, u):
                pe.wait_ge(rdT_ready, b + 1)
                pe.wait_ge(delta_ready, b + 1)
                nc.tensor.matmul(PS[:, 7, :], w("gate"), delta[:, u, :], start=True, stop=True).then_inc(gate_psum, 1)

            def project_out(b):
                pe.wait_ge(attn_ready, b + 1)
                pe.wait_ge(th_ready, b + 1)
                nc.tensor.matmul(PS[:, 7, :], w("o"), attn[:, :], start=True, stop=True).then_inc(wo_psum, 1)

            def turn_x2(b):
                pe.wait_ge(x2_step, 2 * b + 2)
                for t in range(CT):
                    mm = nc.tensor.transpose(PS[:, 7, t * P:(t + 1) * P], x2T[:, t * P:(t + 1) * P], ident)
                mm.then_inc(x2_psum, 1)

            def turn_z(b):
                pe.wait_ge(z_ready, b + 1)
                for t in range(CT):
                    mm = nc.tensor.transpose(PS[:, 7, t * P:(t + 1) * P], z[:, t, :], ident)
                mm.then_inc(zT_psum, 1)

            def logits(b):
                pe.wait_ge(h_ready, b + 1)
                for t in range(CT):
                    mm = nc.tensor.matmul(PS[:, 7, t * MOE:(t + 1) * MOE], h[:, t * P:(t + 1) * P], w("moe_gate"),
                                          start=True, stop=True)
                mm.then_inc(lg_psum, 1)

            def steps(b, u, n_, f, c_):
                if b is not None:
                    turn_k(b, u)
                    pe.wait_ge(v_ready, b + 1)
                for n in range(16):
                    if b is not None:
                        if n < 8:
                            scores(b, u, n, f)
                        if 7 <= n < 15:
                            scores(b, u, n + 1, f)
                    if c_ is not None:
                        if n == 0:
                            gate(c_, 1 - u)
                        if n == 2:
                            project_out(c_)
                        if n == 5:
                            turn_x2(c_)
                        if n == 9:
                            turn_z(c_)
                        if n == 11:
                            logits(c_)
                    if f is not None:
                        if n == 0:
                            project(f, 1 - u, "q", 0)
                        if n == 1:
                            values(f, 1 - u)
                        if n == 4:
                            project(f, 1 - u, "k", 1)
                    if n_ is not None:
                        if n == 9:
                            turn_xn(n_)
                        if n == 13:
                            pointwise(n_)
                    if b is not None:
                        if n in (1, 5, 9):
                            update_state(b, u, n // 4)
                        if n >= 1:
                            weigh(b, u, n - 1)
                        if n == 3:
                            denominators(b)
                        if n == 12:
                            turn_spread(b)
                if b is not None:
                    weigh(b, u, 15)
            stages(pe, steps)

        @block.scalar
        def _(act):
            nc.scalar.preload_act_table(ACT.Exp)
            act.wait_ge(act_const, 1)
            act.wait_ge(zeroed, 1)

            def copy_xnT(b):
                act.wait_ge(xnT_psum, b + 1)
                after_previous(act, x1_ready, b)
                nc.scalar.activation(xnT[:, 2:], PS[:, 0, :], ACT.Copy).then_inc(xnT_ready, 1)
                act.wait_ge(xnT_ready, b + 1)
                nc.scalar.activation(y[:, 0, :], xnT[:, 0:SEQ], ACT.Copy, scale=w("dw")[:, 0:1]).then_inc(conv, 1)

            def copy_v(b, u):
                act.wait_ge(v_psum, b + 1)
                if not isinstance(b, int) or b >= 2:
                    act.wait_ge(am_used, 16 * (b + (-1)))
                nc.scalar.activation(vt[:, u, :, :].rearrange("p c d -> p (c d)"), PS[:, 0, :], ACT.Copy)
                for t in range(CT):
                    src = PS[:, 0, t * P:(t + 1) * P].rearrange("p (g j m) -> p j g m", j=4, m=HD)
                    ins = nc.scalar.activation(diagonal(vm, u, t), src, ACT.Copy)
                ins.then_inc(v_ready, 1)

            def exps(b, n):
                act.wait_ge(rot_step, 6 * b + 3 * n + 3)
                nc.scalar.activation(ex[:, :], rot[:, 0, :], ACT.Exp, bias=minus_one[:, 0:1]).then_inc(exp_ready, 1)

            def high_part(b, u, which, full):
                act.wait_ge(phi_ready, 2 * b + which + 1)
                after_previous(act, (q_stacked, k_stacked)[which], b, 48)
                nc.scalar.activation(parts[:, which, 0, :], full[:, u, :], ACT.Copy).then_inc(hi_ready, 1)

            def score_operands(b, t):
                if t == 0:
                    act.wait_ge(q_stacked, 48 * b + 48)
                    act.wait_ge(k_stacked, 48 * b + 48)
                    if not isinstance(b, int) or b:
                        act.wait_ge(scores_psum, 16 * (b + (-1)) + 12)
                elif t == 1:
                    after_previous(act, scores_psum, b, 16)
                else:
                    act.wait_ge(scores_psum, 16 * b + 4 * (t - 1))
                ins = nc.scalar.activation(kr[:, t % 2, :, :], ks[:, :, t * P:(t + 1) * P], ACT.Copy)
                for j in range(4):
                    ins = nc.scalar.activation(qm[:, t % 2, :, j, :], qs[:, :, t * P:(t + 1) * P], ACT.Copy,
                                               scale=c("group")[0:3 * 32, j:j + 1])
                ins.then_inc(operands_ready, 1)
                if t == CT - 1:
                    act.wait_ge(operands_ready, 4 * b + CT)
                    nc.scalar.activation(act_scratch[:, :], minus_one[:, :], ACT.Copy).then_inc(stack_read, 32)

            def copy_k(b):
                act.wait_ge(kT_psum, b + 1)
                nc.scalar.activation(ktok[:, :, :].rearrange("p c d -> p (c d)"), PS[:, 6, P:CT * P],
                                     ACT.Copy).then_inc(ktok_ready, 1)

            def spread_out(b):
                act.wait_ge(den_step, 2 * b + 2)
                nc.scalar.activation(spread[:, :].rearrange("p (h m) -> p h m", m=HD),
                                     den[:, 1, :].unsqueeze(2).to_broadcast([P, CT * HEADS, HD]),
                                     ACT.Copy).then_inc(spread_ready, 1)

            def copy_rdT(b):
                act.wait_ge(rdT_psum, b + 1)
                nc.scalar.activation(rdT[:, :], PS[:, 7, :], ACT.Copy).then_inc(rdT_ready, 1)

            def gate_tanh(b):
                act.wait_ge(gate_psum, b + 1)
                nc.scalar.activation(th[:, :], PS[:, 7, :], ACT.Tanh, bias=w("b_gate"), scale=0.5).then_inc(th_ready, 1)

            def scale_h(b):
                act.wait_ge(zT_psum, b + 1)
                nc.scalar.activation(H[:, bass.ds(b * SEQ, SEQ)], PS[:, 7, :], ACT.Identity, bias=w("ln_b"), scale=w("ln_g"))
                nc.scalar.activation(h[:, :], PS[:, 7, :], ACT.Identity, bias=w("ln_b"), scale=w("ln_g")).then_inc(h_ready, 1)

            def copy_logits(b):
                act.wait_ge(lg_psum, b + 1)
                nc.scalar.activation(LG[:, bass.ds(b * (CT * MOE), CT * MOE)], PS[:, 7, 0:CT * MOE],
                                     ACT.Copy).then_inc(lg_ready, 1)

            def steps(b, u, n_, f, c_):
                if b is not None:
                    copy_k(b)
                    score_operands(b, 1)
                if c_ is not None:
                    gate_tanh(c_)
                if f is not None:
                    copy_v(f, 1 - u)
                    exps(f, 0)
                    high_part(f, 1 - u, 0, qphi)
                if b is not None:
                    spread_out(b)
                    score_operands(b, 2)
                if f is not None:
                    exps(f, 1)
                    high_part(f, 1 - u, 1, kphi)
                if b is not None:
                    score_operands(b, 3)
                if c_ is not None:
                    scale_h(c_)
                if n_ is not None:
                    copy_xnT(n_)
                if c_ is not None:
                    copy_logits(c_)
                if b is not None:
                    copy_rdT(b)
                if f is not None:
                    score_operands(f, 0)
            stages(act, steps)

        @block.vector
        def _(dve):
            def stats(b):
                dve.wait_ge(x_in, 16 * b + 16)
                for t in range(CT):
                    xt = X[:, bass.ds(b * CT + t, 1), :].rearrange("p o d -> p (o d)")
                    nc.vector.bn_stats(st[:, t, :], xt).then_inc(ln1, 1)
                wait_apart(dve, nc, ln1, CT * b + CT, scratch)
                for t in range(CT):
                    ins = nc.vector.bn_aggr(mv[:, t, :], st[:, t, :])
                ins.then_inc(ln1_stats, 1)

            def normalise(b):
                dve.wait_ge(rstd1_ready, b + 1)
                for t in range(CT):
                    xt = X[:, bass.ds(b * CT + t, 1), :].rearrange("p o d -> p (o d)")
                    ins = nc.vector.tensor_scalar(xn[:, t, :], xt, mv[:, t, 0:1], rstd[:, t:t + 1],
                                                  ALU.subtract, ALU.mult)
                ins.then_inc(xn_ready, 1)

            def convolve(b):
                for k in (1, 2):
                    dve.wait_ge(conv, 3 * b + k)
                    nc.vector.scalar_tensor_tensor(y[:, k % 2, :], xnT[:, k:k + SEQ], w("dw")[:, k:k + 1],
                                                   y[:, 1 - k % 2, :], ALU.mult, ALU.add).then_inc(conv, 1)

            def residual(b, u):
                dve.wait_ge(pw_psum, b + 1)
                if not isinstance(b, int) or b >= 2:
                    dve.wait_ge(x1_copied, b + (-1))
                    dve.wait_ge(delta_ready, b + (-1))
                nc.vector.tensor_tensor(x1T[:, u, :], PS[:, 0, :], xnT[:, 2:], ALU.add).then_inc(x1_ready, 1)

            def rotate(b, n):
                if n:
                    dve.wait_ge(phi_ready, 2 * b + 1)
                else:
                    after_previous(dve, phi_ready, b, 2)
                dve.wait_ge(qk_psum, 2 * b + n + 1)
                nc.vector.tensor_tensor(rot[:, 0, :], PS[:, 1, :], c("cos"), ALU.mult).then_inc(rot_step, 1)
                nc.vector.tensor_tensor(rot[:, 1, :], PS[:, 2, :], c("sin"), ALU.mult).then_inc(qk_read, 1)

            def rotated(b, n):
                dve.wait_ge(rot_step, 6 * b + 3 * n + 1)
                dve.wait_ge(qk_read, 2 * b + n + 1)
                nc.vector.scalar_tensor_tensor(rot[:, 0, :], rot[:, 0, :], 1.0, rot[:, 1, :],
                                               ALU.add, ALU.add).then_inc(rot_step, 2)

            def phi(b, u, n, dst):
                dve.wait_ge(exp_ready, 2 * b + n + 1)
                nc.vector.scalar_tensor_tensor(dst[:, u, :], ex[:, :], 1.0, rot[:, 0, :], ALU.min,
                                               ALU.max).then_inc(phi_ready, 1)

            def prefix(b, u):
                dve.wait_ge(phi_ready, 2 * b + 2)
                nc.vector.tensor_tensor_scan(kp[:, :], kphi[:, u, :], kphi[:, u, :], 0.0,
                                             ALU.add, ALU.max).then_inc(kp_ready, 1)

            def mask_state(b, t):
                dve.wait_ge(state_psum, 3 * b + t + 1)
                nc.vector.tensor_tensor(state[:, t, :], PS[:, 6, 0:P], c("block"), ALU.mult).then_inc(state_ready, 1)

            def invert(b):
                dve.wait_ge(den_psum, b + 1)
                nc.vector.tensor_scalar(den[:, 0, :], PS[:, 6, P:P + CT * HEADS], 1e-6, None, ALU.add).then_inc(den_step, 1)
                dve.wait_ge(den_step, 2 * b + 1)
                nc.vector.reciprocal(den[:, 1, :], den[:, 0, :]).then_inc(den_step, 1)

            def mask_scores(b, n):
                dve.wait_ge(scores_psum, 16 * b + n + 1)
                if n >= 3:
                    dve.wait_ge(am_used, 16 * b + n - 2)
                nc.vector.tensor_tensor(am[:, n % 3, :].rearrange("p (j q) -> p j q", j=4),
                                        PS[:, SCORE_BANK[n], :].rearrange("p (j q) -> p j q", j=4),
                                        c("tri").unsqueeze(1).to_broadcast([P, 4, P]), ALU.mult).then_inc(am_ready, 1)

            def divide(b):
                dve.wait_ge(am_used, 16 * b + 16)
                dve.wait_ge(rdT_ready, b + 1)
                nc.vector.tensor_tensor(attn[:, :], PS[:, 5, :], rdT[:, :], ALU.mult).then_inc(attn_ready, 1)

            def close(b):
                dve.wait_ge(wo_psum, b + 1)
                dve.wait_ge(th_ready, b + 1)
                nc.vector.scalar_tensor_tensor(x2T[:, :], th[:, :], 1.0, PS[:, 7, :], ALU.add, ALU.mult).then_inc(x2_step, 1)
                dve.wait_ge(x2_step, 2 * b + 1)
                dve.wait_ge(x1_copied, b + 1)
                nc.vector.tensor_tensor(x2T[:, :], x2T[:, :], x1c[:, :], ALU.add).then_inc(x2_step, 1)

            def stats2(b):
                dve.wait_ge(x2_psum, b + 1)
                for t in range(CT):
                    nc.vector.bn_stats(st2[:, t, :], PS[:, 7, t * P:(t + 1) * P]).then_inc(ln2, 1)
                wait_apart(dve, nc, ln2, CT * b + CT, scratch)
                for t in range(CT):
                    ins = nc.vector.bn_aggr(mv2[:, t, :], st2[:, t, :])
                ins.then_inc(ln2_stats, 1)

            def residual2(b):
                nc.vector.tensor_tensor(tokens(X, b), tokens(X, b), PS[:, 7, :].rearrange("p (c d) -> p c d", c=CT),
                                        ALU.add)

            def normalise2(b):
                dve.wait_ge(rstd2_ready, b + 1)
                for t in range(CT):
                    ins = nc.vector.tensor_scalar(z[:, t, :], PS[:, 7, t * P:(t + 1) * P], mv2[:, t, 0:1],
                                                  rstd2[:, t:t + 1], ALU.subtract, ALU.mult)
                ins.then_inc(z_ready, 1)

            def steps(b, u, n_, f, c_):
                if c_ is not None:
                    divide(c_)
                if b is not None:
                    prefix(b, u)
                for n in range(16):
                    if b is not None:
                        if n in (2, 6, 10):
                            mask_state(b, n // 4)
                        if n == 4:
                            invert(b)
                        mask_scores(b, n)
                    if f is not None:
                        if n == 1:
                            rotate(f, 0)
                        if n == 2:
                            rotated(f, 0)
                        if n == 4:
                            phi(f, 1 - u, 0, qphi)
                        if n == 6:
                            rotate(f, 1)
                        if n == 6:
                            rotated(f, 1)
                        if n == 6:
                            phi(f, 1 - u, 1, kphi)
                    if c_ is not None:
                        if n == 3:
                            close(c_)
                        if n == 4:
                            stats2(c_)
                        if n == 7:
                            residual2(c_)
                        if n == 8:
                            normalise2(c_)
                    if n_ is not None:
                        if n == 0:
                            stats(n_)
                        if n == 9:
                            normalise(n_)
                        if n == 11:
                            convolve(n_)
                        if n == 14:
                            residual(n_, u)
            stages(dve, steps)


def mixture(nc, sems, X, w, c, PS, before, ones, minus_half, eps, scratch, H, LG, w1t, w2t, rows, slot_row, slot_expert, scattered):
    with ExitStack() as ctx:
        def sb(name, shape, dt=F32):
            return ctx.enter_context(nc.sbuf_tensor("m_" + name, shape, dt))

        def sem(name):
            return sems.enter_context(nc.semaphore("m_" + name))

        FF = MOE * 512
        raw1 = sb("raw1", [P, FF])
        raw2 = sb("raw2", [P, FF])
        w1h, w1l, w2h, w2l = (sb(n, [P, FF], F32R) for n in ("w1h", "w1l", "w2h", "w2l"))
        HH = sb("HH", [P, 2, SEQ], F32R)
        HL = sb("HL", [P, 2, SEQ], F32R)
        gate = sb("gate", [P, TILES, MOE])
        top = sb("top", [P, TILES])
        total = sb("total", [P, TILES])
        gparts = sb("gparts", [P, TILES, 2 * MOE])
        gp = sb("gp", [P, CT * 2 * MOE])
        gT = sb("gT", [2 * MOE, SEQ], F32R)
        selr = sb("selr", [2 * MOE, MOE * P], F32R)
        gb = raw2[:, 0:2 * SEQ].rearrange("p (u t) -> p u t", u=2)
        S = sb("S", [P, 3, SEQ])
        Sh = sb("Sh", [P, 4, SEQ], F32R)
        Sl = sb("Sl", [P, 4, SEQ], F32R)
        oe = raw2[:, 2 * SEQ:4 * SEQ].rearrange("p (u t) -> p u t", u=2)

        w1_in = sem("w1_in"); w2_in = sem("w2_in"); w_split = sem("w_split")
        parts = sem("parts")
        gate_step = sem("gate_step"); exp_done = sem("exp_done"); gates_ready = sem("gates_ready")
        gp_ready = sem("gp_ready"); gT_psum = sem("gT_psum"); gT_ready = sem("gT_ready")
        gb_psum = sem("gb_psum"); gb_ready = sem("gb_ready")
        h_psum = sem("h_psum"); s_ready = sem("s_ready"); sh_ready = sem("sh_ready"); rounded = sem("rounded"); sl_ready = sem("sl_ready")
        s_used = sem("s_used"); out_psum = sem("out_psum"); oe_ready = sem("oe_ready"); back_psum = sem("back_psum")
        oe_used = sem("oe_used"); x_ready = sem("x_ready")

        block = ctx.enter_context(nc.Block())
        ident = c("ident")
        N = MOE * MOE_CHUNKS
        routing = Routing(0, ctx, nc, sems, X, w, c, PS, before, ones, minus_half, eps, scratch, rows, slot_row, slot_expert,
                          bank=5, scattered=scattered, x_ready=x_ready)

        ROUNDED = (1, 3)
        SPREAD = (3, 6, 9, 14)

        def over_batches(eng, one):
            one(0, 0, None, None)
            one(1, 1, 0, None)
            one(2, 0, 1, 0)
            with eng.Fori(0, (BATCHES - 4) // 2) as i:
                for u in range(2):
                    b = i * 2 + (3 + u)
                    one(b, 1 - u, b + (-1), b + (-2))
            one(BATCHES - 1, 1, BATCHES - 2, BATCHES - 3)
            one(None, 0, BATCHES - 1, BATCHES - 2)
            one(None, 1, None, BATCHES - 1)

        def two_before(eng, sem, b, e):
            if e >= 2 or not isinstance(b, int) or b:
                eng.wait_ge(sem, MOE * b + (e - 1))

        def route(step, eng, b):
            if b is not None:
                step(eng, b, 0, b)

        def chunk(b, p, n, lag):
            b, n = (b, n - lag) if n >= lag else (p, n - lag + N)
            return None if b is None else (b, n)

        def by_vector(n):
            return n % MOE_CHUNKS in ROUNDED

        def wait_high(eng, b, n):
            e, k = divmod(n, MOE_CHUNKS)
            vector_so_far = len(ROUNDED) * e + sum(r <= k for r in ROUNDED)
            if by_vector(n):
                eng.wait_ge(rounded, MOE * len(ROUNDED) * b + vector_so_far)
            else:
                eng.wait_ge(sh_ready, (N - MOE * len(ROUNDED)) * b + n + 1 - vector_so_far)

        def wait_used(eng, b, n):
            e, k = divmod(n, MOE_CHUNKS)
            if k == MOE_CHUNKS - 1:
                eng.wait_ge(out_psum, MOE * b + e + 1)
            else:
                eng.wait_ge(s_used, (N - MOE) * b + e * (MOE_CHUNKS - 1) + k + 1)

        @block.sync
        def _(sp):
            sp.dma_start(raw1[:, :], w1t).then_inc(w1_in, 16)
            sp.dma_start(raw2[:, :], w2t).then_inc(w2_in, 16)
            routing.sp_padding(sp)

        @block.gpsimd
        def _(pool):
            routing.pool_begin(pool)

            def one(b, v, p, r):
                route(routing.pool_scatter, pool, r)
                route(routing.pool_inverse_deviation, pool, p)
                route(routing.pool_exp, pool, p)
            over_batches(pool, one)
            routing.pool_end(pool)

        @block.tensor
        def _(pe):
            pe.wait_ge(w_split, 3)

            def up(b, v, n):
                if n == 0:
                    pe.wait_ge(parts, 2 * b + 2)
                if n >= 3:
                    pe.wait_ge(s_ready, N * b + n - 2)
                else:
                    after_previous(pe, s_ready, b, N)
                bank = PS[:, n % 3, :]
                f = slice(n * P, (n + 1) * P)
                nc.tensor.matmul(bank, w1h[:, f], HH[:, v, :], start=True, stop=False)
                nc.tensor.matmul(bank, w1h[:, f], HL[:, v, :], start=False, stop=False)
                nc.tensor.matmul(bank, w1l[:, f], HH[:, v, :], start=False, stop=True).then_inc(h_psum, 1)

            def down(b, n):
                e, k = divmod(n, MOE_CHUNKS)
                bank = PS[:, 3 + e % 2, :]
                if k == 0:
                    two_before(pe, oe_ready, b, e)
                f = slice(n * P, (n + 1) * P)
                wait_high(pe, b, n)
                nc.tensor.matmul(bank, w2h[:, f], Sh[:, n % 4, :], start=(k == 0), stop=False)
                nc.tensor.matmul(bank, w2l[:, f], Sh[:, n % 4, :], start=False, stop=False)
                pe.wait_ge(sl_ready, N * b + n + 1)
                last = nc.tensor.matmul(bank, w2h[:, f], Sl[:, n % 4, :], start=False, stop=(k == MOE_CHUNKS - 1))
                if k == MOE_CHUNKS - 1:
                    last.then_inc(out_psum, 1)
                else:
                    last.then_inc(s_used, 1)

            def back(b, e):
                pe.wait_ge(oe_ready, MOE * b + e + 1)
                if e == 0:
                    after_previous(pe, x_ready, b)
                for t in range(CT):
                    mm = nc.tensor.matmul(PS[:, 7, t * P:(t + 1) * P], oe[:, e % 2, t * P:(t + 1) * P], ident,
                                          is_transpose=True, start=(e == 0 and t == 0), stop=(e == MOE - 1),
                                          skip_group_check=True)
                mm.then_inc(back_psum, 1)

            def gates(b):
                pe.wait_ge(gp_ready, b + 1)
                after_previous(pe, gb_ready, b, MOE)
                for t in range(CT):
                    mm = nc.tensor.transpose(PS[0:2 * MOE, 6, t * P:(t + 1) * P],
                                             gp[:, t * 2 * MOE:(t + 1) * 2 * MOE], ident)
                mm.then_inc(gT_psum, 1)

            def spread(b, e):
                pe.wait_ge(gT_ready, b + 1)
                if e:
                    pe.wait_ge(gb_ready, MOE * b + e)
                nc.tensor.matmul(PS[:, 6, :], selr[:, e * P:(e + 1) * P], gT[:, :], start=True,
                                 stop=True).then_inc(gb_psum, 1)

            beside = {11: routing.pe_turn, 13: routing.pe_scores}

            def one(b, v, p, r):
                for n in range(N):
                    if n == 0:
                        route(routing.pe_count, pe, r)
                    if b is not None:
                        up(b, v, n)
                        if n == 2:
                            if isinstance(b, int) and b == 0:
                                pe.wait_ge(w_split, 5)
                            gates(b)
                        if n in SPREAD:
                            spread(b, SPREAD.index(n))
                    lagging = chunk(b, p, n, 3)
                    if lagging:
                        down(*lagging)
                    if n % 4 == 2:
                        lagging = chunk(b, p, n, 10)
                        if lagging:
                            back(lagging[0], lagging[1] // 4)
                    if n in beside:
                        route(beside[n], pe, p)
            over_batches(pe, one)

        @block.scalar
        def _(act):
            nc.scalar.preload_act_table(ACT.Exp)
            act.wait_ge(gate_step, 2)
            nc.scalar.activation(gate[:, :, :], gate[:, :, :], ACT.Exp).then_inc(exp_done, 1)
            nc.scalar.preload_act_table(ACT.Silu)

            def hidden(b, p, n):
                act.wait_ge(h_psum, N * b + n + 1)
                if not by_vector(n):
                    held = chunk(b, p, n, 4)
                    if held:
                        wait_used(act, *held)
                    nc.scalar.activation(Sh[:, n % 4, :], PS[:, n % 3, :], ACT.Silu, bias=w("b1")[:, n:n + 1]).then_inc(sh_ready, 1)
                if n >= 3:
                    act.wait_ge(sl_ready, N * b + n - 2)
                else:
                    after_previous(act, sl_ready, b, N)
                nc.scalar.activation(S[:, n % 3, :], PS[:, n % 3, :], ACT.Silu, bias=w("b1")[:, n:n + 1]).then_inc(s_ready, 1)

            def one(b, v, p, r):
                for n in range(N):
                    if n == 12:
                        route(routing.act_copy_xT, act, p)
                    if n == 15:
                        route(routing.act_copy_x, act, p)
                    if b is None:
                        continue
                    hidden(b, p, n)
                    if n == 2:
                        act.wait_ge(gT_psum, b + 1)
                        nc.scalar.activation(gT[:, :], PS[0:2 * MOE, 6, :], ACT.Copy).then_inc(gT_ready, 1)
                    if n - 1 in SPREAD:
                        e = SPREAD.index(n - 1)
                        act.wait_ge(gb_psum, MOE * b + e + 1)
                        two_before(act, oe_ready, b, e)
                        nc.scalar.activation(gb[:, e % 2, :], PS[:, 6, :], ACT.Copy).then_inc(gb_ready, 1)
            over_batches(act, one)

        @block.vector
        def _(dve):
            nc.vector.tensor_copy(selr[:, :], c("sel")[0:2 * MOE, :]).then_inc(w_split, 1)
            lg = LG[:, :].rearrange("p (t e) -> p t e", e=MOE)
            wide = lambda a: a.unsqueeze(2).to_broadcast([P, TILES, MOE])
            nc.vector.tensor_reduce(top[:, :], lg, AX.X, ALU.max).then_inc(gate_step, 1)
            dve.wait_ge(gate_step, 1)
            nc.vector.tensor_tensor(gate[:, :, :], lg, wide(top[:, :]), ALU.subtract).then_inc(gate_step, 1)
            dve.wait_ge(exp_done, 1)
            nc.vector.tensor_reduce(total[:, :], gate[:, :, :], AX.X, ALU.add).then_inc(gate_step, 1)
            dve.wait_ge(gate_step, 3)
            nc.vector.reciprocal(top[:, :], total[:, :]).then_inc(gate_step, 1)
            dve.wait_ge(gate_step, 4)
            nc.vector.tensor_tensor(gate[:, :, :], gate[:, :, :], wide(top[:, :]), ALU.mult).then_inc(gate_step, 1)
            dve.wait_ge(gate_step, 5)
            nc.vector.tensor_copy(gparts[:, :, 0:MOE].bitcast(F32R), gate[:, :, :]).then_inc(gate_step, 1)
            dve.wait_ge(gate_step, 6)
            nc.vector.tensor_tensor(gparts[:, :, MOE:], gate[:, :, :], gparts[:, :, 0:MOE], ALU.subtract).then_inc(gates_ready, 1)
            for k, (raw, hi, lo, arrived) in enumerate([(raw1, w1h, w1l, w1_in), (raw2, w2h, w2l, w2_in)]):
                dve.wait_ge(arrived, 16)
                nc.vector.tensor_copy(hi[:, :], raw[:, :]).then_inc(w_split, 1)
                dve.wait_ge(w_split, 2 * k + 2)
                nc.vector.tensor_tensor(lo[:, :], raw[:, :], hi[:, :].bitcast(F32), ALU.subtract).then_inc(w_split, 1)
            dve.wait_ge(gates_ready, 1)
            routing.dve_begin(dve)

            def split_rows(b, v):
                rows = H[:, bass.ds(b * SEQ, SEQ)]
                nc.vector.tensor_copy(HH[:, v, :], rows).then_inc(parts, 1)
                dve.wait_ge(parts, 2 * b + 1)
                nc.vector.tensor_tensor(HL[:, v, :], rows, HH[:, v, :].bitcast(F32), ALU.subtract).then_inc(parts, 1)
            split_rows(0, 0)
            beside = {7: routing.dve_statistics, 9: routing.dve_normalise, 14: routing.dve_pick}

            def gated(b, e):
                dve.wait_ge(out_psum, MOE * b + e + 1)
                dve.wait_ge(gb_ready, MOE * b + e + 1)
                two_before(dve, back_psum, b, e)
                nc.vector.scalar_tensor_tensor(oe[:, e % 2, :], PS[:, 3 + e % 2, :], w("b2")[:, e:e + 1],
                                               gb[:, e % 2, :], ALU.add, ALU.mult).then_inc(oe_ready, 1)

            def one(b, v, p, r):
                for n in range(N):
                    if n == 1:
                        route(routing.dve_place, dve, r)
                        route(routing.dve_gate, dve, r)
                    if n == 7 and p is not None:
                        dve.wait_ge(back_psum, MOE * p + MOE)
                        xb = X[:, bass.ds(p * CT, CT), :]
                        nc.vector.tensor_tensor(xb, xb, PS[:, 7, :].rearrange("p (c d) -> p c d", c=CT), ALU.add).then_inc(x_ready, 1)
                    if n in beside:
                        route(beside[n], dve, p)
                    if b is not None:
                        if n == 0:
                            after_previous(dve, gT_psum, b)
                            nc.vector.tensor_copy(gp[:, :].rearrange("p (t e) -> p t e", t=CT),
                                                  gparts[:, bass.ds(b * CT, CT), :]).then_inc(gp_ready, 1)
                        dve.wait_ge(s_ready, N * b + n + 1)
                        if by_vector(n):
                            held = chunk(b, p, n, 4)
                            if held:
                                wait_used(dve, *held)
                            nc.vector.tensor_copy(Sh[:, n % 4, :], S[:, n % 3, :]).then_inc(rounded, 1)
                        wait_high(dve, b, n)
                        nc.vector.tensor_tensor(Sl[:, n % 4, :], S[:, n % 3, :], Sh[:, n % 4, :].bitcast(F32),
                                                ALU.subtract).then_inc(sl_ready, 1)
                    if n == 5 and b is not None and not (isinstance(b, int) and b == BATCHES - 1):
                        split_rows(b + 1, 1 - v)
                    if n % 4 == 3:
                        lagging = chunk(b, p, n, 7)
                        if lagging:
                            gated(lagging[0], lagging[1] // 4)
            over_batches(dve, one)
            routing.dve_end(dve)


class Routing:

    def __init__(self, layer, ctx, nc, sems, X, w, c, PS, before, ones, minus_half, eps, scratch, rows, slot_row, slot_expert,
                 bank, scattered, x_ready):
        self.layer, self.nc, self.X, self.c, self.before, self.ones = layer, nc, X, c, before, ones
        self.minus_half, self.eps, self.scratch, self.rows = minus_half, eps, scratch, rows
        self.slot_row, self.slot_expert, self.x_ready = slot_row, slot_expert, x_ready
        self.buffers = buffers = len(scattered)
        self.router = w(f"router{layer}")
        self.bias = w("br1")
        self.bank = PS[:, bank, :]

        def sb(name, shape, dt=F32):
            return ctx.enter_context(nc.sbuf_tensor(f"r{layer}_" + name, shape, dt))

        def sem(name):
            return sems.enter_context(nc.semaphore(f"r{layer}_" + name))

        self.st = sb("st", [P, CT, 6])
        self.mv = sb("mv", [P, CT, 2])
        self.ve = sb("ve", [P, CT])
        self.rstd = sb("rstd", [P, CT])
        self.row = sb("row", [P, buffers, CT, ROW])
        self.xT = sb("xT", [P, SEQ])
        self.lg = sb("lg", [P, CT, EXPERTS])
        self.top = sb("top", [P, CT, 8])
        self.at = sb("at", [P, CT, 8], U32)
        self.first = sb("first", [P, CT])
        self.hot = sb("hot", [P, CT, EXPERTS], BF16)
        self.hot32 = sb("hot32", [P, CT, EXPERTS])
        self.soft = sb("soft", [P, 2, CT, EXPERTS])
        self.small = sb("small", [P, 4, CT])
        self.euler = sb("euler", [P, CT, EXPERTS])
        self.base = sb("base", [P, EXPERTS])
        self.place = sb("place", [P, 2, CT, EXPERTS])
        self.pos = sb("pos", [P, CT])
        self.posi = sb("posi", [P, buffers, CT], I32)
        self.padding = sb("padding", [P, 2, ROW])
        self.told = sb("told", [P, CT])
        self.got = sb("got", [P, EXPERTS])
        self.tiles = sb("tiles", [P, EXPERTS])
        self.ends = sb("ends", [P, EXPERTS])
        self.jump = sb("jump", [P, EXPERTS])
        self.slot_at = sb("slot_at", [P, NSLOT])
        self.number = sb("number", [P, NSLOT])
        self.skipped = sb("skipped", [P, NSLOT])
        self.over = sb("over", [P, EXPERTS, NSLOT])
        self.passed = sb("passed", [P, NSLOT, EXPERTS])
        self.padi = sb("padi", [P, EXPERTS], I32)

        self.cleared = sem("cleared")
        self.ln = sem("ln")
        self.ln_stats = sem("ln_stats")
        self.ve_done = sem("ve_done")
        self.rstd_ready = sem("rstd_ready")
        self.xn_ready = sem("xn_ready")
        self.x_copied = sem("x_copied")
        self.xT_psum = sem("xT_psum")
        self.xT_ready = sem("xT_ready")
        self.lg_psum = sem("lg_psum")
        self.lg_ready = sem("lg_ready")
        self.pick = sem("pick")
        self.hot_ready = sem("hot_ready")
        self.count_psum = sem("count_psum")
        self.place_step = sem("place_step")
        self.pos_ready = sem("pos_ready")
        self.soft_ready = sem("soft_ready")
        self.exp_ready = sem("exp_ready")
        self.gate_step = sem("gate_step")
        self.tv_ready = sem("tv_ready")
        self.scattered = scattered
        self.told_done = sem("told_done")
        self.ends_ready = sem("ends_ready")
        self.padded = sem("padded")
        self.table = sem("table")


    def dve_begin(self, dve):
        nc = self.nc
        nc.vector.tensor_copy(self.base[:, :], self.c("region")).then_inc(self.place_step, 1)
        nc.vector.memset(self.row[:, :, :, COL_TV:ROW], 0.0).then_inc(self.place_step, 1)
        dve.wait_ge(self.place_step, 2)

    def dve_statistics(self, dve, b, u, turn):
        nc = self.nc
        wait_apart(dve, nc, self.x_ready, b + 1, self.scratch)
        for t in range(CT):
            xt = self.X[:, bass.ds(b * CT + t, 1), :].rearrange("p o d -> p (o d)")
            nc.vector.bn_stats(self.st[:, t, :], xt).then_inc(self.ln, 1)
        wait_apart(dve, nc, self.ln, CT * b + CT, self.scratch)
        for t in range(CT):
            ins = nc.vector.bn_aggr(self.mv[:, t, :], self.st[:, t, :])
        ins.then_inc(self.ln_stats, 1)

    def dve_normalise(self, dve, b, u, turn):
        nc = self.nc
        dve.wait_ge(self.rstd_ready, b + 1)
        if not isinstance(turn, int) or turn:
            dve.wait_ge(self.scattered[u], 16 * CT * turn)
        for t in range(CT):
            xt = self.X[:, bass.ds(b * CT + t, 1), :].rearrange("p o d -> p (o d)")
            ins = nc.vector.tensor_scalar(self.row[:, u, t, 0:P], xt, self.mv[:, t, 0:1], self.rstd[:, t:t + 1],
                                          ALU.subtract, ALU.mult)
        ins.then_inc(self.xn_ready, 1)
        nc.vector.tensor_copy(self.row[:, u, :, COL_ID:COL_ID + 1], self.c("ids")[:, bass.ds(b * CT, CT)].unsqueeze(2))

    def dve_pick(self, dve, b, u, turn):
        nc = self.nc
        picks = 3
        dve.wait_ge(self.lg_psum, b + 1)
        scores = self.bank[:, 0:CT * EXPERTS].rearrange("p (t e) -> p t e", t=CT)
        wide = [P, CT, EXPERTS]
        if self.layer:
            nc.vector.tensor_tensor(self.lg[:, :, :], scores, self.bias.unsqueeze(1).to_broadcast(wide),
                                    ALU.add).then_inc(self.lg_ready, 1)
        else:
            nc.vector.tensor_copy(self.lg[:, :, :], scores).then_inc(self.lg_ready, 1)
        wait_apart(dve, nc, self.lg_ready, b + 1, self.scratch)
        for t in range(CT):
            ins = nc.vector.max(self.top[:, t, :], self.lg[:, t, :])
        ins.then_inc(self.pick, 1)
        wait_apart(dve, nc, self.pick, picks * b + 1, self.scratch)
        for t in range(CT):
            ins = nc.vector.max_index(self.at[:, t, :], self.top[:, t, :], self.lg[:, t, :])
        ins.then_inc(self.pick, 1)
        if not self.layer:
            nc.vector.tensor_tensor(self.soft[:, 0, :, :], self.lg[:, :, :], self.top[:, :, 0:1].to_broadcast(wide),
                                    ALU.subtract).then_inc(self.soft_ready, 1)
        dve.wait_ge(self.pick, picks * b + 2)
        nc.vector.tensor_copy(self.first[:, :], self.at[:, :, 0]).then_inc(self.pick, 1)
        dve.wait_ge(self.pick, picks * b + 3)
        for hot in (self.hot32, self.hot):
            ins = nc.vector.tensor_tensor(hot[:, :, :], self.c("iota").unsqueeze(1).to_broadcast(wide),
                                          self.first[:, :].unsqueeze(2).to_broadcast(wide), ALU.is_equal)
        ins.then_inc(self.hot_ready, 1)

    def dve_gate(self, dve, b, u, turn):
        if self.layer:
            return
        nc, small = self.nc, self.small
        dve.wait_ge(self.exp_ready, b + 1)
        nc.vector.tensor_reduce(small[:, 0, :], self.soft[:, 1, :, :], AX.X, ALU.add).then_inc(self.gate_step, 1)
        dve.wait_ge(self.gate_step, 4 * b + 1)
        nc.vector.reciprocal(small[:, 1, :], small[:, 0, :]).then_inc(self.gate_step, 1)
        dve.wait_ge(self.gate_step, 4 * b + 2)
        nc.vector.tensor_scalar(small[:, 2, :], small[:, 1, :], 1e-8, None, ALU.add).then_inc(self.gate_step, 1)
        dve.wait_ge(self.gate_step, 4 * b + 3)
        nc.vector.reciprocal(small[:, 3, :], small[:, 2, :]).then_inc(self.gate_step, 1)
        dve.wait_ge(self.gate_step, 4 * b + 4)
        nc.vector.tensor_tensor(self.row[:, u, :, COL_TV:COL_TV + 1], small[:, 1, :].unsqueeze(2),
                                small[:, 3, :].unsqueeze(2), ALU.mult).then_inc(self.tv_ready, 1)

    def dve_place(self, dve, b, u, turn):
        nc, place, base = self.nc, self.place, self.base
        dve.wait_ge(self.count_psum, b + 1)
        counts = self.bank[:, CT * EXPERTS:2 * CT * EXPERTS].rearrange("p (t e) -> p t e", t=CT)
        totals = self.bank[:, 2 * CT * EXPERTS:(2 * CT + 1) * EXPERTS]
        nc.vector.tensor_tensor(place[:, 0, :, :], counts, base[:, :].unsqueeze(1).to_broadcast([P, CT, EXPERTS]),
                                ALU.add).then_inc(self.place_step, 1)
        dve.wait_ge(self.place_step, 4 * b + 3)
        nc.vector.tensor_tensor(place[:, 1, :, :], place[:, 0, :, :], self.hot32[:, :, :], ALU.mult).then_inc(self.place_step, 1)
        nc.vector.tensor_tensor(base[:, :], base[:, :], totals, ALU.add).then_inc(self.place_step, 1)
        dve.wait_ge(self.place_step, 4 * b + 4)
        nc.vector.tensor_reduce(self.pos[:, :], place[:, 1, :, :], AX.X, ALU.add).then_inc(self.place_step, 1)
        dve.wait_ge(self.place_step, 4 * b + 6)
        nc.vector.tensor_copy(self.posi[:, u, :], self.pos[:, :]).then_inc(self.pos_ready, 1)

    def dve_end(self, dve):
        nc, table = self.nc, self.table
        nc.vector.tensor_copy(self.padi[:, :], self.base[:, :]).then_inc(self.ends_ready, 1)
        nc.vector.tensor_tensor(self.got[:, :], self.base[:, :], self.c("region"), ALU.subtract).then_inc(table, 1)
        nc.vector.tensor_scalar(self.slot_at[:, :], self.c("slots"), float(SLOT), None, ALU.mult).then_inc(table, 1)
        dve.wait_ge(table, 2)
        by_expert = [P, EXPERTS, NSLOT]
        nc.vector.tensor_tensor(self.over[:, :, :], self.got[:, :].unsqueeze(2).to_broadcast(by_expert),
                                self.slot_at[:, :].unsqueeze(1).to_broadcast(by_expert), ALU.is_gt).then_inc(table, 1)
        dve.wait_ge(table, 3)
        nc.vector.tensor_reduce(self.tiles[:, :], self.over[:, :, :], AX.X, ALU.add).then_inc(table, 1)
        dve.wait_ge(table, 4)
        nc.vector.tensor_tensor_scan(self.ends[:, :], self.tiles[:, :], self.tiles[:, :], 0.0, ALU.add, ALU.max).then_inc(table, 1)
        nc.vector.tensor_scalar(self.jump[:, :], self.tiles[:, :], -float(SLOT), float(REGION), ALU.mult, ALU.add).then_inc(table, 1)
        dve.wait_ge(table, 6)
        by_slot = [P, NSLOT, EXPERTS]
        nc.vector.tensor_tensor(self.passed[:, :, :], self.c("slots").unsqueeze(2).to_broadcast(by_slot),
                                self.ends[:, :].unsqueeze(1).to_broadcast(by_slot), ALU.is_ge).then_inc(table, 1)
        dve.wait_ge(table, 7)
        nc.vector.tensor_reduce(self.number[:, :], self.passed[:, :, :], AX.X, ALU.add).then_inc(table, 1)
        dve.wait_ge(table, 8)
        nc.vector.tensor_scalar(self.slot_expert[:, :], self.number[:, :], float(EXPERTS - 1), None, ALU.min).then_inc(table, 1)
        nc.vector.tensor_tensor(self.passed[:, :, :], self.passed[:, :, :], self.jump[:, :].unsqueeze(1).to_broadcast(by_slot),
                                ALU.mult).then_inc(table, 1)
        dve.wait_ge(table, 10)
        nc.vector.tensor_reduce(self.skipped[:, :], self.passed[:, :, :], AX.X, ALU.add).then_inc(table, 1)
        dve.wait_ge(table, 11)
        nc.vector.tensor_tensor(self.slot_row[:, :], self.skipped[:, :], self.slot_at[:, :], ALU.add).then_inc(table, 1)
        dve.wait_ge(table, 12)


    def pool_begin(self, pool):
        nc = self.nc
        nc.gpsimd.memset(self.euler[:, :, :], float(np.e))
        nc.gpsimd.memset(self.padding[:, :, :], 0.0).then_inc(self.ve_done, 1)
        pool.wait_ge(self.ve_done, 1)
        nc.gpsimd.memset(self.padding[:, :, COL_ID:COL_ID + 1], NO_TOKEN).then_inc(self.cleared, 1)
        pool.wait_ge(self.cleared, 1)

    def pool_inverse_deviation(self, pool, b, u, turn):
        nc = self.nc
        pool.wait_ge(self.ln_stats, b + 1)
        nc.gpsimd.tensor_tensor(self.ve[:, :], self.mv[:, :, 1], self.eps[:, 0:CT], ALU.add).then_inc(self.ve_done, 1)
        pool.wait_ge(self.ve_done, b + 2)
        nc.gpsimd.tensor_tensor(self.rstd[:, :], self.ve[:, :], self.minus_half[:, :], ALU.pow).then_inc(self.rstd_ready, 1)

    def pool_exp(self, pool, b, u, turn):
        pool.wait_ge(self.soft_ready, b + 1)
        self.nc.gpsimd.tensor_tensor(self.soft[:, 1, :, :], self.euler[:, :, :], self.soft[:, 0, :, :],
                                     ALU.pow).then_inc(self.exp_ready, 1)

    def pool_scatter(self, pool, b, u, turn):
        nc = self.nc
        if not self.layer:
            pool.wait_ge(self.tv_ready, b + 1)
        pool.wait_ge(self.pos_ready, b + 1)
        pool.wait_ge(self.x_copied, b + 1)
        after_previous(pool, self.told_done, b)
        nc.gpsimd.tensor_tensor(self.told[:, :], self.minus_half[:, :], self.minus_half[:, :], ALU.mult).then_inc(self.told_done, 1)
        for t in range(CT):
            nc.gpsimd.indirect_dma_start(
                out=self.rows, out_offset=bass.IndirectOffsetOnAxis(ap=self.posi[:, u, t:t + 1], axis=0),
                in_=self.row[:, u, t, :], in_offset=None).then_inc(self.scattered[u], 16)

    def pool_end(self, pool):
        for u in range(self.buffers):
            pool.wait_ge(self.scattered[u], 16 * TILES // self.buffers)


    def pe_turn(self, pe, b, u, turn):
        nc = self.nc
        pe.wait_ge(self.xn_ready, b + 1)
        after_previous(pe, self.pos_ready, b)
        for t in range(CT):
            mm = nc.tensor.transpose(self.bank[:, t * P:(t + 1) * P], self.row[:, u, t, 0:P], self.c("ident"))
        mm.then_inc(self.xT_psum, 1)

    def pe_scores(self, pe, b, u, turn):
        nc = self.nc
        pe.wait_ge(self.xT_ready, b + 1)
        for t in range(CT):
            mm = nc.tensor.matmul(self.bank[:, t * EXPERTS:(t + 1) * EXPERTS], self.xT[:, t * P:(t + 1) * P], self.router,
                                  start=True, stop=True)
        mm.then_inc(self.lg_psum, 1)

    def pe_count(self, pe, b, u, turn):
        nc = self.nc
        pe.wait_ge(self.hot_ready, b + 1)
        flat = self.hot[:, :, :].rearrange("p t e -> p (t e)")
        C0 = CT * EXPERTS
        nc.tensor.matmul(self.bank[:, C0:2 * C0], self.before[:, :], flat, start=True, stop=True, skip_group_check=True)
        for d in range(1, CT):
            nc.tensor.matmul(self.bank[:, C0 + d * EXPERTS:2 * C0], self.ones[:, :], flat[:, 0:(CT - d) * EXPERTS],
                             start=False, stop=True, skip_group_check=True)
        for t in range(CT):
            mm = nc.tensor.matmul(self.bank[:, 2 * C0:2 * C0 + EXPERTS], self.ones[:, :], self.hot[:, t, :],
                                  start=(t == 0), stop=(t == CT - 1))
        mm.then_inc(self.count_psum, 1)


    def act_copy_xT(self, act, b, u, turn):
        nc = self.nc
        act.wait_ge(self.xT_psum, b + 1)
        after_previous(act, self.lg_psum, b)
        nc.scalar.activation(self.xT[:, :], self.bank, ACT.Copy).then_inc(self.xT_ready, 1)

    def act_copy_x(self, act, b, u, turn):
        nc = self.nc
        nc.scalar.activation(self.row[:, u, :, COL_X:COL_X + P], self.X[:, bass.ds(b * CT, CT), :], ACT.Copy).then_inc(self.x_copied, 1)


    def sp_padding(self, sp):
        sp.wait_ge(self.cleared, 1)
        spare = self.rows[EXPERTS * REGION:, :].rearrange("(n p) r -> p n r", p=P)
        for s in range(SPARE // SLOT):
            sp.dma_start(spare[:, 2 * s:2 * s + 2, :], self.padding[:, :, :]).then_inc(self.padded, 16)
        sp.wait_ge(self.ends_ready, 1)
        for e in range(EXPERTS):
            end = sp.value_load(self.padi[0:1, e:e + 1], min_val=e * REGION, max_val=e * REGION + TOKENS)
            sp.dma_start(self.rows[bass.ds(end, SLOT), :].rearrange("(n p) r -> p n r", p=P),
                         self.padding[:, :, :]).then_inc(self.padded, 16)
        sp.wait_ge(self.padded, 16 * (SPARE // SLOT + EXPERTS))


def routed(layer, nc, sems, X, w, c, PS, before, ones, minus_half, eps, scratch, rows, weights, b2, dest, slot_row, slot_expert, stored):
    chunks = (2, 4)[layer]
    B1 = 2 * chunks * P
    with ExitStack() as ctx:
        def sb(name, shape, dt=F32):
            return ctx.enter_context(nc.sbuf_tensor(f"f{layer}_" + name, shape, dt))

        def sem(name):
            return sems.enter_context(nc.semaphore(f"f{layer}_" + name))

        row = sb("row", [P, DEPTH, 2, ROW])
        wt = sb("wt", [P, DEPTH, weights.shape[2]])
        b2r = sb("b2r", [1, DEPTH, P])
        one_row = sb("one_row", [1, P])
        xT = sb("xT", [P, 2, SLOT])
        hid = sb("hid", [P, 2, chunks, SLOT])
        y = sb("y", [P, 2, 2, P])
        xb = sb("xb", [P, 2, 2, P])
        st = sb("st", [P, 2, 2, 6])
        mv = sb("mv", [P, 2, 2, 2])
        ve = sb("ve", [P, 2, 2])
        rstd = sb("rstd", [P, 2, 2])
        centred = sb("centred", [P, 2, 2, P])
        res = sb("res", [P, DEPTH, 2, P])
        token = sb("token", [P, DEPTH, 2], I32)
        told = sb("told", [P, CT])

        rows_in = [sem(f"rows_in{u}") for u in range(DEPTH)]
        weights_in = [sem(f"weights_in{u}") for u in range(DEPTH)]
        one_made = sem("one_made"); xT_psum = sem("xT_psum"); xT_ready = sem("xT_ready"); h_psum = sem("h_psum")
        hid_ready = sem("hid_ready"); out_psum = sem("out_psum"); y_ready = sem("y_ready"); stats = sem("stats")
        mv_ready = sem("mv_ready"); ve_done = sem("ve_done"); rstd_ready = sem("rstd_ready")
        xb_ready = sem("xb_ready"); centred_ready = sem("centred_ready")
        res_ready = sem("res_ready"); told_done = sem("told_done")

        block = ctx.enter_context(nc.Block())
        ident = c("ident")

        def over_slots(eng, step):
            turns = NSLOT // DEPTH
            for s in range(DEPTH):
                step(s, s, 0)
            with eng.Fori(1, turns - 1) as i:
                for u in range(DEPTH):
                    step(i * DEPTH + u, u, i)
            for u in range(DEPTH):
                step(NSLOT - DEPTH + u, u, turns - 1)

        def since(s, n):
            return not isinstance(s, int) or s >= n

        def last(s):
            return isinstance(s, int) and s == NSLOT - 1

        @block.sync
        def _(sp):
            def step(s, u, turn):
                r = sp.value_load(slot_row[0:1, bass.ds(s, 1)], min_val=0, max_val=ROWS - SLOT)
                e = sp.value_load(slot_expert[0:1, bass.ds(s, 1)], min_val=0, max_val=EXPERTS - 1)
                if since(s, DEPTH):
                    sp.wait_ge(res_ready, s - (DEPTH - 1))
                sp.dma_start(row[:, u, :, :], rows[bass.ds(r, SLOT), :].rearrange("(p a) r -> p a r", a=2)).then_inc(rows_in[u], 16)
                sp.dma_start(wt[:, u, :], weights[bass.ds(e, 1), :, :].rearrange("o p n -> (o p) n")).then_inc(weights_in[u], 16)
                if layer:
                    sp.dma_start(b2r[0:1, u, :], b2[bass.ds(e, 1), :]).then_inc(weights_in[u], 16)
            over_slots(sp, step)

        @block.gpsimd
        def _(pool):
            nc.gpsimd.memset(one_row[:, :], 1.0).then_inc(one_made, 1)

            def inverse_deviation(s, v):
                pool.wait_ge(mv_ready, s + 1)
                nc.gpsimd.tensor_tensor(ve[:, v, :], mv[:, v, :, 1], eps[:, 0:2], ALU.add).then_inc(ve_done, 1)
                pool.wait_ge(ve_done, s + 1)
                nc.gpsimd.tensor_tensor(rstd[:, v, :], ve[:, v, :], minus_half[:, 0:2], ALU.pow).then_inc(rstd_ready, 1)

            def store(s, u):
                pool.wait_ge(res_ready, s + 1)
                after_previous(pool, told_done, s)
                nc.gpsimd.tensor_tensor(told[:, :], minus_half[:, :], minus_half[:, :], ALU.mult).then_inc(told_done, 1)
                for a in range(2):
                    nc.gpsimd.indirect_dma_start(
                        out=dest, out_offset=bass.IndirectOffsetOnAxis(ap=token[:, u, a:a + 1], axis=0),
                        in_=res[:, u, a, :], in_offset=None, bounds_check=TOKENS - 1, oob_is_err=False).then_inc(stored[u], 16)

            def step(s, u, turn):
                if layer:
                    store(s, u)
                    return
                inverse_deviation(s, u % 2)
                if since(s, 1):
                    store(s - 1 if isinstance(s, int) else s + (-1), (u - 1) % DEPTH)
            over_slots(pool, step)
            if not layer:
                store(NSLOT - 1, DEPTH - 1)
            for u in range(DEPTH):
                pool.wait_ge(stored[u], 32 * NSLOT // DEPTH)

        @block.tensor
        def _(pe):
            pe.wait_ge(one_made, 1)

            def turn_rows(s, u, turn):
                pe.wait_ge(rows_in[u], 16 * (turn + 1))
                for a in range(2):
                    mm = nc.tensor.transpose(PS[:, u % 2, a * P:(a + 1) * P], row[:, u, a, 0:P], ident)
                mm.then_inc(xT_psum, 1)

            def up(s, u, turn):
                pe.wait_ge(weights_in[u], (16 + 16 * layer) * (turn + 1))
                pe.wait_ge(xT_ready, s + 1)
                for f in range(chunks):
                    bank, half = divmod(f, 2)
                    mm = nc.tensor.matmul(PS[:, 2 + 2 * (u % 2) + bank, half * SLOT:(half + 1) * SLOT],
                                          wt[:, u, f * P:(f + 1) * P], xT[:, u % 2, :], start=True, stop=True)
                mm.then_inc(h_psum, 1)

            def down(s, u):
                pe.wait_ge(hid_ready, s + 1)
                if since(s, 2):
                    pe.wait_ge(res_ready if layer else y_ready, s - 1)
                v = u % 2
                for a in range(2):
                    for f in range(chunks):
                        mm = nc.tensor.matmul(PS[:, 6 + v, a * P:(a + 1) * P], hid[:, v, f, a * P:(a + 1) * P],
                                              wt[:, u, (chunks + f) * P:(chunks + f + 1) * P],
                                              start=(f == 0), stop=(f == chunks - 1 and not layer))
                    if layer:
                        mm = nc.tensor.matmul(PS[:, 6 + v, a * P:(a + 1) * P], one_row[:, :], b2r[0:1, u, :],
                                              start=False, stop=True)
                mm.then_inc(out_psum, 1)

            turn_rows(0, 0, 0)

            def step(s, u, turn):
                if not last(s):
                    turn_rows(s + 1, (u + 1) % DEPTH, turn + (u + 1) // DEPTH)
                up(s, u, turn)
                if since(s, 1):
                    down(s + (-1), (u - 1) % DEPTH)
            over_slots(pe, step)
            down(NSLOT - 1, DEPTH - 1)

        @block.scalar
        def _(act):
            nc.scalar.preload_act_table(ACT.Gelu)

            def copy_xT(s, v):
                act.wait_ge(xT_psum, s + 1)
                nc.scalar.activation(xT[:, v, :], PS[:, v, 0:SLOT], ACT.Copy).then_inc(xT_ready, 1)

            def gelu(s, u):
                act.wait_ge(h_psum, s + 1)
                if since(s, 2):
                    act.wait_ge(out_psum, s - 1)
                v = u % 2
                if layer:
                    for f in range(chunks):
                        bank, half = divmod(f, 2)
                        ins = nc.scalar.activation(hid[:, v, f, :], PS[:, 2 + 2 * v + bank, half * SLOT:(half + 1) * SLOT],
                                                   ACT.Gelu, bias=wt[:, u, B1 + f:B1 + f + 1])
                else:
                    ins = nc.scalar.activation(hid[:, v, :, :].rearrange("p f t -> p (f t)"), PS[:, 2 + 2 * v, :], ACT.Gelu)
                ins.then_inc(hid_ready, 1)

            def gate(s, u, turn):
                act.wait_ge(out_psum, s + 1)
                if since(s, 2):
                    act.wait_ge(centred_ready, s - 1)
                v = u % 2
                for a in range(2):
                    ins = nc.scalar.activation(y[:, v, a, :], PS[:, 6 + v, a * P:(a + 1) * P], ACT.Copy,
                                               scale=row[:, u, a, COL_TV:COL_TV + 1])
                ins.then_inc(y_ready, 1)

            copy_xT(0, 0)

            def step(s, u, turn):
                if not last(s):
                    copy_xT(s + 1, (u + 1) % 2)
                gelu(s, u)
                if not layer and since(s, 1):
                    gate(s + (-1), (u - 1) % DEPTH, turn)
            over_slots(act, step)
            if not layer:
                gate(NSLOT - 1, DEPTH - 1, None)

        @block.vector
        def _(dve):
            def take_token(s, u, turn):
                dve.wait_ge(rows_in[u], 16 * (turn + 1))
                if since(s, DEPTH):
                    dve.wait_ge(stored[u], 32 * turn)
                nc.vector.tensor_copy(token[:, u, :].unsqueeze(2), row[:, u, :, COL_ID:COL_ID + 1])

            def add_x(s, u):
                dve.wait_ge(out_psum, s + 1)
                nc.vector.tensor_tensor(res[:, u, :, :], PS[:, 6 + u % 2, 0:SLOT].rearrange("p (a d) -> p a d", a=2),
                                        row[:, u, :, COL_X:COL_X + P], ALU.add).then_inc(res_ready, 1)

            def statistics(s, u):
                v = u % 2
                if since(s, 2):
                    dve.wait_ge(res_ready, s - 1)
                nc.vector.tensor_tensor(xb[:, v, :, :], row[:, u, :, COL_X:COL_X + P],
                                        w("beta").unsqueeze(1).to_broadcast([P, 2, P]), ALU.add).then_inc(xb_ready, 1)
                dve.wait_ge(y_ready, s + 1)
                for a in range(2):
                    nc.vector.bn_stats(st[:, v, a, :], y[:, v, a, :]).then_inc(stats, 1)
                wait_apart(dve, nc, stats, 2 * s + 2, scratch)
                for a in range(2):
                    ins = nc.vector.bn_aggr(mv[:, v, a, :], st[:, v, a, :])
                ins.then_inc(mv_ready, 1)

            def close(s, u):
                v = u % 2
                dve.wait_ge(mv_ready, s + 1)
                for a in range(2):
                    ins = nc.vector.scalar_tensor_tensor(centred[:, v, a, :], y[:, v, a, :], mv[:, v, a, 0:1], w("gamma"),
                                                         ALU.subtract, ALU.mult)
                ins.then_inc(centred_ready, 1)
                dve.wait_ge(centred_ready, s + 1)
                dve.wait_ge(xb_ready, s + 1)
                dve.wait_ge(rstd_ready, s + 1)
                for a in range(2):
                    ins = nc.vector.scalar_tensor_tensor(res[:, u, a, :], centred[:, v, a, :], rstd[:, v, a:a + 1],
                                                         xb[:, v, a, :], ALU.mult, ALU.add)
                ins.then_inc(res_ready, 1)

            def step(s, u, turn):
                take_token(s, u, turn)
                if layer:
                    add_x(s, u)
                    return
                statistics(s, u)
                if since(s, 1):
                    close(s + (-1), (u - 1) % DEPTH)
            over_slots(dve, step)
            if not layer:
                close(NSLOT - 1, DEPTH - 1)


def softmax_attention(nc, sems, X, w, c, PS, before, ones, minus_half, eps, scratch, mid, rows, slot_row, slot_expert, scattered):
    with ExitStack() as ctx:
        def sb(name, shape, dt=F32):
            return ctx.enter_context(nc.sbuf_tensor("s_" + name, shape, dt))

        def sem(name):
            return sems.enter_context(nc.semaphore("s_" + name))

        qk = sb("qk", [P, P])
        st = sb("st", [P, CT, 6])
        mv = sb("mv", [P, CT, 2])
        ve = sb("ve", [P, CT])
        rstd = sb("rstd", [P, CT])
        xn = sb("xn", [P, CT, P])
        xT = sb("xT", [P, 2, SEQ])
        yT = sb("yT", [P, 2, SEQ])
        v = sb("v", [P, 2, CT, P])
        nmax = sb("nmax", [P, CT])
        total = sb("total", [P, CT])
        inverse = sb("inverse", [P, 2, CT])
        prob = sb("prob", [P, 2, SEQ])
        probT = sb("probT", [P, 2, SEQ])

        x_in = sem("x_in"); qk_psum = sem("qk_psum"); qk_ready = sem("qk_ready")
        ln = sem("ln"); ln_stats = sem("ln_stats"); ve_done = sem("ve_done"); rstd_ready = sem("rstd_ready")
        xn_ready = sem("xn_ready"); xT_psum = sem("xT_psum"); xT_ready = sem("xT_ready")
        y_psum = sem("y_psum"); y_ready = sem("y_ready"); v_psum = sem("v_psum"); v_ready = sem("v_ready")
        score_psum = sem("score_psum"); max_ready = sem("max_ready"); prob_ready = sem("prob_ready")
        pT_psum = sem("pT_psum"); pT_ready = sem("pT_ready"); out_psum = sem("out_psum")
        inv_step = sem("inv_step"); x_ready = sem("x_ready")

        block = ctx.enter_context(nc.Block())
        ident = c("ident")

        routing = Routing(1, ctx, nc, sems, X, w, c, PS, before, ones, minus_half, eps, scratch, rows, slot_row, slot_expert,
                          bank=7, scattered=scattered, x_ready=x_ready)

        def stages(eng, f, a, route):
            for step in f(0, 0):
                step()
            a(0, 0, f(1, 1), [])
            a(1, 1, f(2, 0), route(0, 0, 0))
            a(2, 0, f(3, 1), route(1, 1, 0))
            with eng.Fori(1, (BATCHES - 2) // 2) as i:
                for u in range(2):
                    b = i * 2 + (1 + u)
                    a(b, 1 - u, f(b + 1, u), route(i * 2 + u, u, i))
            a(BATCHES - 1, 1, [], route(BATCHES - 2, 0, BATCHES // 2 - 1))
            for step in route(BATCHES - 1, 1, BATCHES // 2 - 1):
                step()

        def steps(eng, *which):
            return lambda b, u, turn: [lambda step=step: step(eng, b, u, turn) for step in which]

        @block.sync
        def _(sp):
            for b in range(BATCHES):
                if b:
                    sp.wait_ge(x_in, 16 * b)
                sp.dma_start(X[:, b * CT:(b + 1) * CT, :],
                             mid[b * SEQ:(b + 1) * SEQ, :].rearrange("(c p) d -> p c d", p=P)).then_inc(x_in, 16)
            sp.wait_ge(x_in, 16 * BATCHES)
            routing.sp_padding(sp)

        @block.gpsimd
        def _(pool):
            def f(b, u):
                def rstd_step():
                    pool.wait_ge(ln_stats, b + 1)
                    nc.gpsimd.tensor_tensor(ve[:, :], mv[:, :, 1], eps[:, 0:CT], ALU.add).then_inc(ve_done, 1)
                    pool.wait_ge(ve_done, b + 1)
                    nc.gpsimd.tensor_tensor(rstd[:, :], ve[:, :], minus_half[:, :], ALU.pow).then_inc(rstd_ready, 1)
                return [rstd_step]

            def a(b, u, nxt, sent):
                for step in sent[:1] + nxt + sent[1:]:
                    step()
            routing.pool_begin(pool)
            stages(pool, f, a, steps(pool, routing.pool_inverse_deviation, routing.pool_scatter))
            routing.pool_end(pool)

        @block.tensor
        def _(pe):
            nc.tensor.matmul(PS[:, 1, 0:P], w("q1"), w("k1"), start=True, stop=True).then_inc(qk_psum, 1)

            def f(b, u):
                def transpose_xn():
                    pe.wait_ge(xn_ready, b + 1)
                    after_previous(pe, v_ready, b)
                    for t in range(CT):
                        mm = nc.tensor.transpose(PS[:, 0, t * P:(t + 1) * P], xn[:, t, :], ident)
                    mm.then_inc(xT_psum, 1)

                def project():
                    pe.wait_ge(xT_ready, b + 1)
                    pe.wait_ge(qk_ready, 1)
                    after_previous(pe, y_ready, b)
                    nc.tensor.matmul(PS[:, 1, :], qk[:, :], xT[:, u, :], start=True, stop=True).then_inc(y_psum, 1)
                    for t in range(CT):
                        mm = nc.tensor.matmul(PS[:, 0, t * P:(t + 1) * P], xT[:, u, t * P:(t + 1) * P], w("v1"),
                                              start=True, stop=True)
                    mm.then_inc(v_psum, 1)
                return [transpose_xn, project]

            def a(b, u, nxt, sent):
                def score(t):
                    pe.wait_ge(y_ready, b + 1)
                    if t >= 2:
                        pe.wait_ge(prob_ready, CT * b + t - 1)
                    else:
                        after_previous(pe, prob_ready, b, CT)
                    nc.tensor.matmul(PS[:, 2 + t % 2, :], yT[:, u, t * P:(t + 1) * P], xT[:, u, :],
                                     start=True, stop=True).then_inc(score_psum, 1)

                def attend(t):
                    pe.wait_ge(prob_ready, CT * b + t + 1)
                    if t >= 2:
                        pe.wait_ge(pT_ready, CT * b + t - 1)
                    else:
                        after_previous(pe, pT_ready, b, CT)
                    for m in range(CT):
                        mm = nc.tensor.transpose(PS[:, 4 + t % 2, m * P:(m + 1) * P], prob[:, t % 2, m * P:(m + 1) * P], ident)
                    mm.then_inc(pT_psum, 1)

                def weigh(t):
                    pe.wait_ge(pT_ready, CT * b + t + 1)
                    if t == 0:
                        pe.wait_ge(v_ready, b + 1)
                        after_previous(pe, x_ready, b)
                    for m in range(CT):
                        mm = nc.tensor.matmul(PS[:, 6, t * P:(t + 1) * P], probT[:, t % 2, m * P:(m + 1) * P], v[:, u, m, :],
                                              start=(m == 0), stop=(m == CT - 1))
                    mm.then_inc(out_psum, 1)

                def turn(n):
                    if nxt:
                        nxt[n]()

                def route(n):
                    if sent:
                        sent[n]()
                score(0)
                score(1)
                attend(0)
                score(2)
                attend(1)
                weigh(0)
                route(0)
                score(3)
                turn(0)
                attend(2)
                route(1)
                weigh(1)
                turn(1)
                attend(3)
                weigh(2)
                route(2)
                weigh(3)
            stages(pe, f, a, steps(pe, routing.pe_turn, routing.pe_scores, routing.pe_count))

        @block.scalar
        def _(act):
            nc.scalar.preload_act_table(ACT.Exp)

            def f(b, u):
                def copy_x():
                    act.wait_ge(xT_psum, b + 1)
                    nc.scalar.activation(xT[:, u, :], PS[:, 0, :], ACT.Copy).then_inc(xT_ready, 1)

                def copy_v():
                    act.wait_ge(v_psum, b + 1)
                    nc.scalar.activation(v[:, u, :, :].rearrange("p c d -> p (c d)"), PS[:, 0, :], ACT.Copy).then_inc(v_ready, 1)

                def copy_y():
                    act.wait_ge(y_psum, b + 1)
                    nc.scalar.activation(yT[:, u, :], PS[:, 1, :], ACT.Copy).then_inc(y_ready, 1)
                return [copy_x, copy_y, copy_v]

            def a(b, u, nxt, sent):
                def exps(t):
                    act.wait_ge(max_ready, CT * b + t + 1)
                    if t >= 2:
                        act.wait_ge(pT_psum, CT * b + t - 1)
                    elif not (isinstance(b, int) and b == 0):
                        act.wait_ge(inv_step, 2 * b)
                    nc.scalar.activation(prob[:, t % 2, :], PS[:, 2 + t % 2, :], ACT.Exp, bias=nmax[:, t:t + 1],
                                         accum_out=total[:, t:t + 1]).then_inc(prob_ready, 1)

                def turn(n):
                    if nxt:
                        nxt[n]()

                def route(n):
                    if sent:
                        sent[n]()
                exps(0)
                exps(1)
                exps(2)
                route(0)
                turn(0)
                exps(3)
                route(1)
                turn(1)
                turn(2)
            stages(act, f, a, steps(act, routing.act_copy_xT, routing.act_copy_x))

        @block.vector
        def _(dve):
            dve.wait_ge(qk_psum, 1)
            nc.vector.tensor_copy(qk[:, :], PS[:, 1, 0:P]).then_inc(qk_ready, 1)

            def f(b, u):
                def stats():
                    dve.wait_ge(x_in, 16 * b + 16)
                    for t in range(CT):
                        nc.vector.bn_stats(st[:, t, :], X[:, bass.ds(b * CT + t, 1), :].rearrange("p o d -> p (o d)")).then_inc(ln, 1)
                    wait_apart(dve, nc, ln, CT * b + CT, scratch)
                    for t in range(CT):
                        ins = nc.vector.bn_aggr(mv[:, t, :], st[:, t, :])
                    ins.then_inc(ln_stats, 1)

                def normalise():
                    dve.wait_ge(rstd_ready, b + 1)
                    for t in range(CT):
                        xt = X[:, bass.ds(b * CT + t, 1), :].rearrange("p o d -> p (o d)")
                        ins = nc.vector.tensor_scalar(xn[:, t, :], xt, mv[:, t, 0:1], rstd[:, t:t + 1],
                                                      ALU.subtract, ALU.mult)
                    ins.then_inc(xn_ready, 1)
                return [stats, normalise]

            def a(b, u, nxt, sent):
                def turn(n):
                    if nxt:
                        nxt[n]()

                def route(n):
                    if sent:
                        sent[n]()

                def largest(t):
                    dve.wait_ge(score_psum, CT * b + t + 1)
                    nc.vector.tensor_reduce(nmax[:, t:t + 1], PS[:, 2 + t % 2, :], AX.X, ALU.max,
                                            negate=True).then_inc(max_ready, 1)

                def copy_p(t):
                    dve.wait_ge(pT_psum, CT * b + t + 1)
                    if t >= 2:
                        dve.wait_ge(out_psum, CT * b + t - 1)
                    nc.vector.tensor_copy(probT[:, t % 2, :], PS[:, 4 + t % 2, :]).then_inc(pT_ready, 1)

                def invert():
                    dve.wait_ge(prob_ready, CT * b + CT)
                    nc.vector.reciprocal(inverse[:, 0, :], total[:, :]).then_inc(inv_step, 1)
                    dve.wait_ge(inv_step, 2 * b + 1)
                    nc.vector.tensor_scalar(inverse[:, 1, :], inverse[:, 0, :], float(P) ** -0.5, None,
                                            ALU.mult).then_inc(inv_step, 1)

                def add_residual():
                    dve.wait_ge(inv_step, 2 * b + 2)
                    dve.wait_ge(out_psum, CT * b + CT)
                    for t in range(CT):
                        xt = X[:, bass.ds(b * CT + t, 1), :].rearrange("p o d -> p (o d)")
                        ins = nc.vector.scalar_tensor_tensor(xt, PS[:, 6, t * P:(t + 1) * P], inverse[:, 1, t:t + 1], xt,
                                                             ALU.mult, ALU.add)
                    ins.then_inc(x_ready, 1)
                largest(0)
                route(0)
                largest(1)
                turn(0)
                copy_p(0)
                route(1)
                largest(2)
                turn(1)
                copy_p(1)
                largest(3)
                copy_p(2)
                route(2)
                copy_p(3)
                route(3)
                invert()
                add_residual()
            routing.dve_begin(dve)
            stages(dve, f, a, steps(dve, routing.dve_statistics, routing.dve_normalise, routing.dve_pick, routing.dve_place))
            routing.dve_end(dve)



def _constants():
    t = {}
    p = np.arange(P)
    t["ident"] = np.eye(P)
    inv_freq = (np.float32(1.0) / np.power(np.float32(10000.0), np.arange(0, HD, 2, dtype=np.float32) / np.float32(HD))).astype(np.float32)
    theta = np.arange(SEQ, dtype=np.float32)[None, :] * inv_freq[(p % HD) // 2][:, None]
    t["cos"] = np.cos(theta)
    t["sin"] = np.sin(theta) * np.where(p % 2 == 0, -1.0, 1.0)[:, None]
    t["tri"] = p[:, None] <= p[None, :]
    t["before"] = p[:, None] < p[None, :]
    t["block"] = p[:, None] // HD == p[None, :] // HD
    t["group"] = (p[:, None] % 32) // HD == np.arange(4)[None, :]
    t["heads"] = p[:, None] // HD == np.arange(HEADS)[None, :]
    sel = np.zeros((P, MOE, P))
    for e in range(MOE):
        sel[[e, e + MOE], e, :] = 1.0
    t["sel"] = sel.reshape(P, -1)
    t["ids"] = p[:, None] + P * np.arange(TILES)[None, :]
    t["iota"] = np.broadcast_to(np.arange(EXPERTS), (P, EXPERTS))
    t["region"] = np.broadcast_to(REGION * np.arange(EXPERTS), (P, EXPERTS))
    t["slots"] = np.broadcast_to(np.arange(NSLOT), (P, NSLOT))
    return np.concatenate([np.asarray(t[n], np.float32) for n in CCOLS], axis=1)


def _layout(i):
    qkv = i["L0_attn_w_qkv"]
    swap = np.arange(P) ^ 1
    col = lambda a: a.reshape(-1, 1)
    rows = lambda a: np.broadcast_to(a, (P, a.shape[-1]))
    t = {
        "pw": i["L0_attn_w_pw"].T, "q": qkv[:P].T, "qs": qkv[:P][swap].T, "k": qkv[P:2 * P].T,
        "ks": qkv[P:2 * P][swap].T, "v": qkv[2 * P:].T, "o": i["L0_attn_w_o"].T, "gate": i["L0_attn_w_gate"].T,
        "moe_gate": i["L0_attn_w_moe_gate"].T, "dw": i["L0_attn_w_dw"], "b_gate": col(i["L0_attn_b_gate"]),
        "ln_g": col(i["L0_attn_ln_g"]), "ln_b": col(i["L0_attn_ln_b"]),
        "b1": i["L0_attn_b1"].reshape(MOE * MOE_CHUNKS, P).T, "b2": i["L0_attn_b2"].T,
        "router0": i["L0_ffn_gate_w"].T, "q1": i["L1_attn_Wq"], "k1": i["L1_attn_Wk"], "v1": i["L1_attn_Wv"].T,
        "router1": i["L1_ffn_wr"], "br1": rows(i["L1_ffn_br"]),
        "gamma": rows(i["L0_ffn_ln_gamma"]), "beta": rows(i["L0_ffn_ln_beta"]),
    }
    wsmall = np.concatenate([t[n] for n in WCOLS], axis=1)
    w1t = i["L0_attn_w1"].transpose(2, 0, 1).reshape(P, MOE * 512)
    w2t = i["L0_attn_w2"].reshape(MOE, P, MOE_CHUNKS, P).transpose(3, 0, 2, 1).reshape(P, MOE * 512)

    def experts(w1, w2, *more):
        f = w2.shape[1] // P
        return np.concatenate([w1, w2.reshape(EXPERTS, f, P, P).transpose(0, 2, 1, 3).reshape(EXPERTS, P, f * P), *more], axis=2)

    b1 = i["L1_ffn_b1"].reshape(EXPERTS, 4, P).transpose(0, 2, 1)
    return {
        "x": i["L0_attn_x"], "wsmall": wsmall, "consts": _constants(), "w1t": w1t, "w2t": w2t,
        "wr0": experts(i["L0_ffn_expert_w1"], i["L0_ffn_expert_w2"]),
        "wr1": experts(i["L1_ffn_w1"], i["L1_ffn_w2"], b1), "br2": i["L1_ffn_b2"],
    }


def kernel(**inputs):
    import concourse.bacc as bacc
    from concourse.bass_utils import run_bass_kernel_spmd

    nc = bacc.Bacc("TRN2", target_bir_lowering=False, num_devices=1)
    arrays = {n: np.ascontiguousarray(a) for n, a in _layout({n: np.asarray(a) for n, a in inputs.items()}).items()}
    args = {n: nc.dram_tensor(n, a.shape, mybir.dt.from_np(a.dtype), kind="ExternalInput").ap() for n, a in arrays.items()}
    args["out"] = nc.dram_tensor("out", (TOKENS, P), F32, kind="ExternalOutput").ap()
    program(nc, **args)
    r = run_bass_kernel_spmd(nc, [arrays], core_ids=[0])
    return r.results[0]["out"].reshape(BATCHES, SEQ, P)
```
